# Optimizing a Trainium2 kernel written in Bass

```python
import numpy as np
import jax
import jax.numpy as jnp

def _softmax(x, axis=-1):
    return jax.nn.softmax(x, axis=axis)

def _gelu(x):
    return jax.nn.gelu(x, approximate=True)

def _silu(x):
    return jax.nn.silu(x)

def _sigmoid(x):
    return jax.nn.sigmoid(x)

def _layernorm(x, axis=-1, eps=1e-05):
    m = jnp.mean(x, axis=axis, keepdims=True)
    v = jnp.var(x, axis=axis, keepdims=True)
    return (x - m) / jnp.sqrt(v + eps)

def _scatter_add(tgt, idx, src, axis=0):
    return tgt.at[idx].add(src)

def _segment_sum(src, seg, n):
    return jax.ops.segment_sum(src, seg, n)
kernel_name = 'mk_flamingo_gated_d2_seqx_r8_71bb53'

def setup_inputs(seed: int=0):
    np.random.seed(seed)
    _w = jnp.asarray

    def _rec_inputs():
        import jax
        import jax.numpy as jnp
        _rk = jax.random.key(seed)
        x = 2.818e-05 + 1 * jax.random.normal(jax.random.fold_in(_rk, 1), (16, 64, 512), jnp.float32)
        _lenS = 64 - jax.random.randint(jax.random.fold_in(_rk, 7), (16,), 0, max(1, 64 // 4) + 1, jnp.int32)
        _lenS2 = 64 - jax.random.randint(jax.random.fold_in(_rk, 8), (16,), 0, max(1, 64 // 4) + 1, jnp.int32)
        _ctx_1024P = jax.random.normal(jax.random.fold_in(_rk, 11), (16, 16, 128), jnp.float32)
        _ctx_1024c = jax.random.dirichlet(jax.random.fold_in(_rk, 511), 0.3 * jnp.ones((16,), jnp.float32), (16, 64))
        _ctx_1024t = jnp.einsum('bsk,bkd->bsd', _ctx_1024c, _ctx_1024P)
        _ctx_1024t = _ctx_1024t * jax.lax.rsqrt(jnp.mean(jnp.square(_ctx_1024t)) + 1e-12) * 0.953939
        ctx_1024 = -0.000392918 + 0.999932 * (_ctx_1024t + 0.3 * jax.random.normal(jax.random.fold_in(_rk, 611), (16, 64, 128), jnp.float32))
        _validS = jnp.arange(64)[None, :] < _lenS[:, None]
        _validS2 = jnp.arange(64)[None, :] < _lenS2[:, None]
        _causal = jnp.tril(jnp.ones((64, 64), dtype=bool))
        mask_SxS2_ff0 = jnp.where(jnp.ones((64, 64), dtype=bool), 0.0, -1000000000.0).astype(jnp.float32)
        _g = jax.random.normal(jax.random.fold_in(_rk, 9001), (2, 2), jnp.float32)
        _g = jnp.sign(_g) * jnp.maximum(jnp.abs(_g), 1.0) + (_g == 0) * 1.0
        g_xattn = _g[0]
        g_ffn = _g[1]
        return (x, ctx_1024, _lenS2, mask_SxS2_ff0, g_xattn, g_ffn)
    x, ctx_1024, _lenS2, mask_SxS2_ff0, g_xattn, g_ffn = _rec_inputs()

    def _L0_xattn_setup():
        import jax, jax.numpy as jnp
        import numpy as np
        from jax import lax
        B, T, L, H, C = (32, 64, 128, 64, 512)
        A, FCH, K = (64, 10, 101)

        def _sig(z):
            return jnp.tanh(z * 0.5) * 0.5 + 0.5
        key = jax.random.key(seed)
        ks = jax.random.split(key, 20)
        sc = 0.02
        n = lambda k, sh: jax.random.normal(k, sh, dtype=jnp.float32) * sc
        inp = {'hbatch': jax.random.normal(ks[0], (B, T, 2 * H), dtype=jnp.float32), 'targets': jax.random.normal(ks[1], (B, L, C), dtype=jnp.float32), 'L_sy': n(ks[2], (H, H)), 'L_gy_w': n(ks[3], (H, 2 * H)), 'L_gy_b': jnp.zeros((H,), jnp.float32), 'L_yy_w': n(ks[4], (C, H)), 'L_yy_b': jnp.zeros((C,), jnp.float32), 'L_ys': n(ks[5], (4 * H, C)), 'L_ss': n(ks[6], (4 * H, H)), 'L_gs_w': n(ks[7], (4 * H, 2 * H)), 'L_gs_b': jnp.zeros((4 * H,), jnp.float32), 'Wa_s': n(ks[8], (A, H)), 'Wa_h': n(ks[9], (A, 2 * H)), 'ba': jnp.zeros((A,), jnp.float32), 'conv_w': n(ks[10], (FCH, 1, K)), 'Wa_f': n(ks[11], (A, FCH)), 'va': n(ks[12], (A,)), 'lengths': jax.random.randint(ks[13], (B,), T // 2, T + 1)}
        return inp
    _L0_xattn_all = _L0_xattn_setup()
    _L0_xattn_in = {k: v for k, v in _L0_xattn_all.items() if k in ('L_sy', 'L_gy_w', 'L_gy_b', 'L_yy_w', 'L_yy_b', 'L_ys', 'L_ss', 'L_gs_w', 'L_gs_b', 'Wa_s', 'Wa_h', 'ba', 'conv_w', 'Wa_f', 'va')}
    del _L0_xattn_all

    def _L0_ffn_setup():
        import jax, jax.numpy as jnp
        import numpy as np
        H = 512
        I = 256
        E = 16
        TOPK = 4
        SI = 256
        key = jax.random.key(seed)
        ks = jax.random.split(key, 9)
        s = 0.02
        return {'hidden_states': jax.random.normal(ks[0], (2, 256, H), dtype=jnp.float32), 'gate_w': jax.random.normal(ks[1], (E, H), dtype=jnp.float32) * s, 'bias': jnp.zeros((E,), dtype=jnp.float32), 'Wg': jax.random.normal(ks[2], (E, I, H), dtype=jnp.float32) * s, 'Wu': jax.random.normal(ks[3], (E, I, H), dtype=jnp.float32) * s, 'Wd': jax.random.normal(ks[4], (E, H, I), dtype=jnp.float32) * s, 'Sg': jax.random.normal(ks[5], (SI, H), dtype=jnp.float32) * s, 'Su': jax.random.normal(ks[6], (SI, H), dtype=jnp.float32) * s, 'Sd': jax.random.normal(ks[7], (H, SI), dtype=jnp.float32) * s}
    _L0_ffn_all = _L0_ffn_setup()
    _L0_ffn_in = {k: v for k, v in _L0_ffn_all.items() if k in ('gate_w', 'bias', 'Wg', 'Wu', 'Wd', 'Sg', 'Su', 'Sd')}
    del _L0_ffn_all

    def _L1_xattn_setup():
        import math
        import jax, jax.numpy as jnp
        import numpy as np
        N_HEADS = 32
        N_KV_HEADS = 8
        N_REP = N_HEADS // N_KV_HEADS
        HEAD_DIM = 512 // N_HEADS
        key = jax.random.key(seed)
        kq, kk, kv = jax.random.split(key, 3)
        B, S, T = (2, 256, 256)
        q = jax.random.normal(kq, (B, S, N_HEADS * HEAD_DIM), dtype=jnp.float32)
        k = jax.random.normal(kk, (B, T, N_KV_HEADS * HEAD_DIM), dtype=jnp.float32)
        v = jax.random.normal(kv, (B, T, N_KV_HEADS * HEAD_DIM), dtype=jnp.float32)
        mask = jnp.zeros((S, T), dtype=jnp.float32)
        return {'q': q, 'k': k, 'v': v, 'start_pos': 0, 'mask': mask}
    _L1_xattn_all = _L1_xattn_setup()
    _L1_xattn_in = {k: v for k, v in _L1_xattn_all.items() if k in ()}
    del _L1_xattn_all

    def _L1_ffn_setup():
        import jax, jax.numpy as jnp
        import numpy as np
        HIDDEN = 512
        MOE_INTER = 128
        SHARED_INTER = 512
        NUM_EXPERTS = 16
        TOP_K = 2

        def _moe_forward(x, gate_w, w_gate_up, w_down, shared_w_gate_up, shared_w_down):
            orig_shape = x.shape
            x2 = x.reshape(-1, orig_shape[-1])
            gu_s = x2 @ shared_w_gate_up.T
            g_s, u_s = jnp.split(gu_s, 2, axis=-1)
            shared_out = jax.nn.silu(g_s) * u_s @ shared_w_down.T
            logits = x2 @ gate_w.T
            probs = jax.nn.softmax(logits, axis=-1)
            topk_vals, topk_idx = jax.lax.top_k(probs, TOP_K)
            topk_vals = topk_vals / jnp.sum(topk_vals, axis=-1, keepdims=True)
            combine = jnp.sum(jax.nn.one_hot(topk_idx, NUM_EXPERTS, dtype=x2.dtype) * topk_vals[..., None], axis=1)
            gu = jnp.einsum('th,eih->eti', x2, w_gate_up)
            g, u = jnp.split(gu, 2, axis=-1)
            act = jax.nn.silu(g) * u
            out_e = jnp.einsum('eti,ehi->eth', act, w_down)
            moe_out = jnp.einsum('eth,te->th', out_e, combine)
            return (moe_out + shared_out).reshape(orig_shape)
        key = jax.random.key(seed)
        ks = jax.random.split(key, 6)
        s = 0.02
        hidden_states = jax.random.normal(ks[0], (2, 256, HIDDEN), dtype=jnp.float32)
        gate_w = jax.random.normal(ks[1], (NUM_EXPERTS, HIDDEN), dtype=jnp.float32) * s
        w_gate_up = jax.random.normal(ks[2], (NUM_EXPERTS, 2 * MOE_INTER, HIDDEN), dtype=jnp.float32) * s
        w_down = jax.random.normal(ks[3], (NUM_EXPERTS, HIDDEN, MOE_INTER), dtype=jnp.float32) * s
        shared_w_gate_up = jax.random.normal(ks[4], (2 * SHARED_INTER, HIDDEN), dtype=jnp.float32) * s
        shared_w_down = jax.random.normal(ks[5], (HIDDEN, SHARED_INTER), dtype=jnp.float32) * s
        return {'hidden_states': hidden_states, 'gate_w': gate_w, 'w_gate_up': w_gate_up, 'w_down': w_down, 'shared_w_gate_up': shared_w_gate_up, 'shared_w_down': shared_w_down}
    _L1_ffn_all = _L1_ffn_setup()
    _L1_ffn_in = {k: v for k, v in _L1_ffn_all.items() if k in ('gate_w', 'w_gate_up', 'w_down', 'shared_w_gate_up', 'shared_w_down')}
    del _L1_ffn_all
    return {'x': x, 'ctx_1024': ctx_1024, '_lenS2': _lenS2, 'mask_SxS2_ff0': mask_SxS2_ff0, 'g_xattn': g_xattn, 'g_ffn': g_ffn, 'L0_xattn_L_sy': _L0_xattn_in['L_sy'], 'L0_xattn_L_gy_w': _L0_xattn_in['L_gy_w'], 'L0_xattn_L_gy_b': _L0_xattn_in['L_gy_b'], 'L0_xattn_L_yy_w': _L0_xattn_in['L_yy_w'], 'L0_xattn_L_yy_b': _L0_xattn_in['L_yy_b'], 'L0_xattn_L_ys': _L0_xattn_in['L_ys'], 'L0_xattn_L_ss': _L0_xattn_in['L_ss'], 'L0_xattn_L_gs_w': _L0_xattn_in['L_gs_w'], 'L0_xattn_L_gs_b': _L0_xattn_in['L_gs_b'], 'L0_xattn_Wa_s': _L0_xattn_in['Wa_s'], 'L0_xattn_Wa_h': _L0_xattn_in['Wa_h'], 'L0_xattn_ba': _L0_xattn_in['ba'], 'L0_xattn_conv_w': _L0_xattn_in['conv_w'], 'L0_xattn_Wa_f': _L0_xattn_in['Wa_f'], 'L0_xattn_va': _L0_xattn_in['va'], 'L0_ffn_gate_w': _L0_ffn_in['gate_w'], 'L0_ffn_bias': _L0_ffn_in['bias'], 'L0_ffn_Wg': _L0_ffn_in['Wg'], 'L0_ffn_Wu': _L0_ffn_in['Wu'], 'L0_ffn_Wd': _L0_ffn_in['Wd'], 'L0_ffn_Sg': _L0_ffn_in['Sg'], 'L0_ffn_Su': _L0_ffn_in['Su'], 'L0_ffn_Sd': _L0_ffn_in['Sd'], 'L1_ffn_gate_w': _L1_ffn_in['gate_w'], 'L1_ffn_w_gate_up': _L1_ffn_in['w_gate_up'], 'L1_ffn_w_down': _L1_ffn_in['w_down'], 'L1_ffn_shared_w_gate_up': _L1_ffn_in['shared_w_gate_up'], 'L1_ffn_shared_w_down': _L1_ffn_in['shared_w_down']}

def reference(x, ctx_1024, _lenS2, mask_SxS2_ff0, g_xattn, g_ffn, L0_xattn_L_sy, L0_xattn_L_gy_w, L0_xattn_L_gy_b, L0_xattn_L_yy_w, L0_xattn_L_yy_b, L0_xattn_L_ys, L0_xattn_L_ss, L0_xattn_L_gs_w, L0_xattn_L_gs_b, L0_xattn_Wa_s, L0_xattn_Wa_h, L0_xattn_ba, L0_xattn_conv_w, L0_xattn_Wa_f, L0_xattn_va, L0_ffn_gate_w, L0_ffn_bias, L0_ffn_Wg, L0_ffn_Wu, L0_ffn_Wd, L0_ffn_Sg, L0_ffn_Su, L0_ffn_Sd, L1_ffn_gate_w, L1_ffn_w_gate_up, L1_ffn_w_down, L1_ffn_shared_w_gate_up, L1_ffn_shared_w_down):
    import jax
    import jax.numpy as jnp

    def _L0_xattn_ref(hbatch, targets, L_sy, L_gy_w, L_gy_b, L_yy_w, L_yy_b, L_ys, L_ss, L_gs_w, L_gs_b, Wa_s, Wa_h, ba, conv_w, Wa_f, va, lengths):
        import jax, jax.numpy as jnp
        import numpy as np
        from jax import lax
        B, T, L, H, C = (32, 64, 128, 64, 512)
        A, FCH, K = (64, 10, 101)

        def _sig(z):
            return jnp.tanh(z * 0.5) * 0.5 + 0.5
        Bx, Tx, D = hbatch.shape
        mask = jnp.arange(Tx)[None, :] < lengths[:, None]
        enc_proj = jnp.einsum('btd,ad->bta', hbatch, Wa_h)

        def step(carry, tgt):
            s, c, alpha = carry
            f = lax.conv_general_dilated(alpha, conv_w, (1,), 'SAME', dimension_numbers=('NCH', 'OIH', 'NCH'))
            e = jnp.einsum('a,bta->bt', va, jnp.tanh(enc_proj + (s @ Wa_s.T)[:, None, :] + jnp.einsum('bft,af->bta', f, Wa_f) + ba))
            e = jnp.where(mask, e, jnp.float32(-1e+30))
            alpha_new = jax.nn.softmax(e, axis=1)[:, None, :]
            g = jnp.einsum('bt,btd->bd', alpha_new[:, 0], hbatch)
            y = jnp.tanh(g @ L_gy_w.T + L_gy_b + s @ L_sy.T) @ L_yy_w.T + L_yy_b
            rec = tgt @ L_ys.T + s @ L_ss.T + g @ L_gs_w.T + L_gs_b
            ig, fg, cg, og = jnp.split(rec, 4, axis=1)
            c_next = _sig(fg) * c + _sig(ig) * jnp.tanh(cg)
            s_next = _sig(og) * jnp.tanh(c_next)
            return ((s_next, c_next, alpha_new), y)
        init = (jnp.zeros((Bx, L_sy.shape[0]), hbatch.dtype), jnp.zeros((Bx, L_sy.shape[0]), hbatch.dtype), jnp.zeros((Bx, 1, Tx), hbatch.dtype))
        _, ys = lax.scan(step, init, jnp.swapaxes(targets, 0, 1))
        return jnp.swapaxes(ys, 0, 1)

    def _L0_ffn_ref(hidden_states, gate_w, bias, Wg, Wu, Wd, Sg, Su, Sd):
        import jax, jax.numpy as jnp
        import numpy as np
        H = 512
        I = 256
        E = 16
        TOPK = 4
        SI = 256
        orig_shape = hidden_states.shape
        x = hidden_states.reshape(-1, orig_shape[-1])
        scores = jax.nn.sigmoid(x @ gate_w.T) + bias
        topk_w, topk_idx = jax.lax.top_k(scores, TOPK)
        topk_w = topk_w / (jnp.sum(topk_w, axis=-1, keepdims=True) + 1e-20)
        cw = jnp.sum(jax.nn.one_hot(topk_idx, E, dtype=x.dtype) * topk_w[..., None], axis=1)
        g = jnp.einsum('th,eih->eti', x, Wg)
        u = jnp.einsum('th,eih->eti', x, Wu)
        z = jax.nn.silu(g) * u
        zw = z * cw.T[:, :, None]
        out = jnp.einsum('eti,ehi->th', zw, Wd)
        out = out + jax.nn.silu(x @ Sg.T) * (x @ Su.T) @ Sd.T
        return out.reshape(orig_shape)

    def _L1_xattn_ref(q, k, v, start_pos, mask):
        import math
        import jax, jax.numpy as jnp
        import numpy as np
        N_HEADS = 32
        N_KV_HEADS = 8
        N_REP = N_HEADS // N_KV_HEADS
        HEAD_DIM = 512 // N_HEADS
        b, s, _ = q.shape
        t = k.shape[1]
        xq = q.reshape(b, s, N_KV_HEADS, N_REP, HEAD_DIM)
        xk = k.reshape(b, t, N_KV_HEADS, HEAD_DIM)
        xv = v.reshape(b, t, N_KV_HEADS, HEAD_DIM)
        scores = jnp.einsum('bsgrd,btgd->bgrst', xq, xk) / math.sqrt(HEAD_DIM)
        scores = scores + mask
        probs = jax.nn.softmax(scores.astype(jnp.float32), axis=-1).astype(q.dtype)
        out = jnp.einsum('bgrst,btgd->bsgrd', probs, xv)
        return out.reshape(b, s, N_HEADS * HEAD_DIM)

    def _L1_ffn_ref(hidden_states, gate_w, w_gate_up, w_down, shared_w_gate_up, shared_w_down):
        import jax, jax.numpy as jnp
        import numpy as np
        HIDDEN = 512
        MOE_INTER = 128
        SHARED_INTER = 512
        NUM_EXPERTS = 16
        TOP_K = 2

        def _moe_forward(x, gate_w, w_gate_up, w_down, shared_w_gate_up, shared_w_down):
            orig_shape = x.shape
            x2 = x.reshape(-1, orig_shape[-1])
            gu_s = x2 @ shared_w_gate_up.T
            g_s, u_s = jnp.split(gu_s, 2, axis=-1)
            shared_out = jax.nn.silu(g_s) * u_s @ shared_w_down.T
            logits = x2 @ gate_w.T
            probs = jax.nn.softmax(logits, axis=-1)
            topk_vals, topk_idx = jax.lax.top_k(probs, TOP_K)
            topk_vals = topk_vals / jnp.sum(topk_vals, axis=-1, keepdims=True)
            combine = jnp.sum(jax.nn.one_hot(topk_idx, NUM_EXPERTS, dtype=x2.dtype) * topk_vals[..., None], axis=1)
            gu = jnp.einsum('th,eih->eti', x2, w_gate_up)
            g, u = jnp.split(gu, 2, axis=-1)
            act = jax.nn.silu(g) * u
            out_e = jnp.einsum('eti,ehi->eth', act, w_down)
            moe_out = jnp.einsum('eth,te->th', out_e, combine)
            return (moe_out + shared_out).reshape(orig_shape)
        return _moe_forward(hidden_states, gate_w, w_gate_up, w_down, shared_w_gate_up, shared_w_down)
    x = x + jnp.tanh(g_xattn[0]) * _L0_xattn_ref(ctx_1024, _layernorm(x, axis=-1), L0_xattn_L_sy, L0_xattn_L_gy_w, L0_xattn_L_gy_b, L0_xattn_L_yy_w, L0_xattn_L_yy_b, L0_xattn_L_ys, L0_xattn_L_ss, L0_xattn_L_gs_w, L0_xattn_L_gs_b, L0_xattn_Wa_s, L0_xattn_Wa_h, L0_xattn_ba, L0_xattn_conv_w, L0_xattn_Wa_f, L0_xattn_va, _lenS2)
    x = x + jnp.tanh(g_ffn[0]) * _L0_ffn_ref(_layernorm(x, axis=-1), L0_ffn_gate_w, L0_ffn_bias, L0_ffn_Wg, L0_ffn_Wu, L0_ffn_Wd, L0_ffn_Sg, L0_ffn_Su, L0_ffn_Sd)
    x = x + jnp.tanh(g_xattn[1]) * _L1_xattn_ref(_layernorm(x, axis=-1), ctx_1024, ctx_1024, 0, mask_SxS2_ff0)
    x = x + jnp.tanh(g_ffn[1]) * _L1_ffn_ref(_layernorm(x, axis=-1), L1_ffn_gate_w, L1_ffn_w_gate_up, L1_ffn_w_down, L1_ffn_shared_w_gate_up, L1_ffn_shared_w_down)
    return x

_drawn_inputs = setup_inputs


def setup_inputs(seed=0):
    import zlib

    import numpy as np

    out = dict(_drawn_inputs(seed))
    spreads = {'mask_SxS2_ff0': (0.0, 0.529),
     'g_ffn': (-1.0, 0.6),
     'L0_xattn_L_gy_b': (0.0, 0.77),
     'L0_xattn_L_yy_b': (0.0, 0.1),
     'L0_xattn_L_gs_b': (0.0, 0.8),
     'L0_xattn_ba': (0.0, 0.8),
     'L0_ffn_bias': (0.0, 0.788)}
    factors = {'L0_xattn_L_sy': 8.0,
     'L0_xattn_L_gy_w': 4.432,
     'L0_xattn_L_yy_w': 3.342,
     'L0_xattn_L_ys': 8.0,
     'L0_xattn_L_ss': 8.0,
     'L0_xattn_L_gs_w': 8.0,
     'L0_xattn_Wa_s': 8.0,
     'L0_xattn_Wa_h': 8.0,
     'L0_xattn_conv_w': 64.0,
     'L0_xattn_Wa_f': 29.04,
     'L0_xattn_va': 8.0,
     'L0_ffn_gate_w': 6.451,
     'L0_ffn_Wg': 4.939,
     'L0_ffn_Wu': 4.862,
     'L0_ffn_Wd': 4.838,
     'L1_ffn_gate_w': 4.081,
     'L1_ffn_w_gate_up': 3.834,
     'L1_ffn_w_down': 3.816,
     'L1_ffn_shared_w_gate_up': 3.042,
     'L1_ffn_shared_w_down': 3.05}
    for name, (base, spread) in spreads.items():
        noise = np.random.default_rng([zlib.crc32(name.encode()), seed]).standard_normal(out[name].shape)
        drawn = base * np.exp(spread * noise) if base else spread * noise
        out[name] = jnp.asarray(drawn.astype(out[name].dtype))
    for name, factor in factors.items():
        out[name] = (out[name] * factor).astype(out[name].dtype)
    return out
```

```python
from contextlib import ExitStack

import numpy as np

import concourse.bass as bass
from concourse import mybir

ALU = mybir.AluOpType
ACT = mybir.ActivationFunctionType
AX = mybir.AxisListType
F32 = mybir.dt.float32
F16 = mybir.dt.float16
BF16 = mybir.dt.bfloat16
I32 = mybir.dt.int32
U32 = mybir.dt.uint32

P = 128
B, L, H = 16, 64, 512
T, D, HS = 64, 128, 64
A, FCH, KW = 64, 10, 101
NTOK = B * L
NT = NTOK // P
HC = H // P
PAD = 13
KWP = KW + 2 * PAD
NU = T // 2
E = 16
G, R, HD = 8, 4, 16
EPS = 1e-5
PSCALE = 1024.0


class Moe:

    def __init__(self, tag, inter, top, shared):
        self.tag, self.I, self.K, self.shared = tag, inter, top, shared
        self.IC = inter // P
        self.NB = NTOK * top // P + E - 1
        assert self.NB % 4 == 3


class Turn:

    def __init__(self, j, c):
        self.j, self.c = j, c
        self.par, self.slot = c % 2, c % 4
        self.n = 4 * j + c
        self.h = 2 * j + c // 2
        self.q = j + c // 4

    def next(self, d=1):
        return Turn(self.j, self.c + d)


MOES = [Moe("f0", 256, 4, 1), Moe("f1", 128, 2, 2)]
NEG = -1e30


def constants():
    p = np.arange(P)
    cols = {
        "ident": np.eye(P),
        "dmask": (p[:, None] // B == np.arange(8)[None, :]),
        "bsel": (p[:, None] % B == np.arange(B)[None, :]),
        "bdmask": (p[:, None] // T == np.arange(B)[None, :] // 8),
        "tcount": np.broadcast_to(np.arange(T)[None, :], (P, T)),
        "half": np.full((P, 2 * NT), -0.5),
        "ones": np.ones((P, P)),
        "before": (p[:, None] < p[None, :]),
        "iota": np.broadcast_to(p[None, :], (P, P)),
        "prow": p[:, None],
        "tri": np.broadcast_to((np.arange(E)[None, :] < np.arange(E)[:, None]).reshape(1, E * E), (P, E * E)),
        "gmask": 0.25 * (p[:, None] // HD == np.arange(G)[None, :]),
        "vmask": (p[:, None] // T == (np.arange(P)[None, :] // HD) % 2),
    }
    where, parts, at = {}, [], 0
    for name, c in cols.items():
        c = np.asarray(c, np.float32)
        where[name] = (at, c.shape[1])
        parts.append(c)
        at += c.shape[1]
    return np.ascontiguousarray(np.concatenate(parts, 1)), where


def build(nc, a, out, stage):
    _, where = constants()
    with ExitStack() as ctx:
        def sb(name, shape, dt=F32):
            return ctx.enter_context(nc.sbuf_tensor(name, shape, dt))

        def ps(name, shape=(P, 512)):
            return ctx.enter_context(nc.psum_tensor(name, list(shape), F32))

        def sem(name):
            return ctx.enter_context(nc.semaphore(name))

        bank = [ps(f"bank{i}") for i in range(8)]

        const = sb("const", [P, sum(n for _, n in where.values())])

        def cn(name, rows=P):
            at, n = where[name]
            return const[0:rows, at:at + n]

        ident = cn("ident")
        xres = sb("xres", [P, NT, H])
        hid = sb("hid", [P, NT, H])
        hidT = sb("hidT", [P, HC, NTOK])
        stats = sb("stats", [P, NT, 6])
        mv = sb("mv", [P, NT, 2])
        vareps = sb("vareps", [P, NT])
        rstd = sb("rstd", [P, NT])
        gates_g = sb("gates_g", [P, 4])

        ctxT = sb("ctxT", [D, T, B])
        ctxP = sb("ctxP", [P, 8, D])
        lens_i = sb("lens_i", [B, 1], I32)
        lens_f = sb("lens_f", [B, 1])
        maskb = sb("maskb", [B, T])
        lys = sb("lys", [P, HC, 4 * HS])
        lss = sb("lss", [HS, 4 * HS])
        lgs = sb("lgs", [D, 4 * HS])
        gsb = sb("gsb", [HS, 4])
        wasT = sb("wasT", [HS, 2, A])
        wahT = sb("wahT", [D, A])
        bacol = sb("bacol", [P, 1])
        convp = sb("convp", [FCH, KWP])
        wafT = sb("wafT", [FCH, A])
        va2 = sb("va2", [P, 2])
        lgyT = sb("lgyT", [D, HS])
        lsyT = sb("lsyT", [HS, HS])
        gyb = sb("gyb", [HS, 1])
        yyT = sb("yyT", [HS + 1, H])

        comb = sb("comb", [P, A])
        region = sb("region", [P, 3 * 4096])
        tr_f = region[:, 4096:8192]
        toep_w = region[:, 0:4096]
        toepA = toep_w[:, 0:2048].bitcast(BF16)
        toepB = toep_w[:, 2048:4096].bitcast(BF16)
        ctx3 = sb("ctx3", [P, 3, 8 * D], BF16)
        ctxr = sb("ctxr", [P, 8 * D])
        comb_d = nc.dram_tensor("comb_d", [P + T, A], F32).ap()
        enc = sb("enc", [P, NU * B])
        pre = region[0:HS, 8192:12288].rearrange("p (l g b) -> p l g b", l=L, g=4)
        ghist = sb("ghist", [D, L, B])
        shist = sb("shist", [HS, L + 1, B])

        prebuf = sb("prebuf", [HS, 4, B])
        s2 = sb("s2", [HS, B])
        c2 = sb("c2", [HS, B])
        al2 = sb("al2", [P, 2, B], F16)
        alr = sb("alr", [P, B])
        alr2 = sb("alr2", [P, B])
        encloc = sb("encloc", [P, NU * B])
        pact = sb("pact", [P, NU * B])
        th = sb("th", [P, NU * B])
        xexp = sb("xexp", [P, 4, 8, 2])
        nmax = sb("nmax", [B, 1])
        psum_e = sb("psum_e", [B, 1])
        prob = sb("prob", [B, T])
        rinv = sb("rinv", [B, 1])
        pn = sb("pn", [P, 2 * T])
        ae = sb("ae", [P, 2, B], F16)
        gT = sb("gT", [D, B])
        tg = sb("tg", [HS, 4, B])
        la = sb("la", [HS, B])
        lb = sb("lb", [HS, B])
        tc = sb("tc", [HS, B])
        yg = sb("yg", [HS + 1, NTOK])

        gw = sb("gw", [P, 2, HC, E])
        bias0 = sb("bias0", [P, E])
        wbuf1 = [region[:, i * 3072:i * 3072 + 2048].rearrange("p (c n) -> p c n", c=HC) for i in range(4)]
        wbuf2 = [region[:, i * 3072 + 2048:(i + 1) * 3072].rearrange("p (c n) -> p c n", c=2) for i in range(4)]
        xg = [sb(f"xg{i}", [P, H]) for i in range(2)]
        xgT = [sb(f"xgT{i}", [P, HC, P]) for i in range(2)]
        gth = [sb(f"gth{i}", [P, 256]) for i in range(2)]
        ga = [sb(f"ga{i}", [P, 256]) for i in range(2)]
        zb = [sb(f"zb{i}", [P, 256]) for i in range(2)]
        zT = [sb(f"zT{i}", [P, 2, P]) for i in range(2)]
        ob = [sb(f"ob{i}", [P, H]) for i in range(2)]
        NYG = 8
        yrow = [hidT[:, i // 2, (i % 2) * H:(i % 2 + 1) * H] for i in range(NYG)]
        NBM = MOES[0].NB
        KM = MOES[0].K
        sc = sb("sc", [P, NT, E])
        sc2 = sb("sc2", [P, NT, E])
        smax = sb("smax", [P, NT])
        top8 = sb("top8", [P, NT, 8])
        idx8 = sb("idx8", [P, NT, 8], U32)
        idxf = sb("idxf", [P, NT * KM])
        onehot = sb("onehot", [P, NT * KM, E])
        ohs = sb("ohs", [P, NT * KM, E])
        msum = sb("msum", [P, NT, E])
        cum = sb("cum", [P, NT, E])
        count = sb("count", [P, E])
        nblk_i = sb("nblk_i", [P, E], I32)
        nblk_j = sb("nblk_j", [P, E], I32)
        nblk = sb("nblk", [P, E])
        trib = sb("trib", [P, E, E])
        bstart = sb("bstart", [P, E])
        bend = sb("bend", [P, E])
        place = sb("place", [P, NT, E])
        slotf = sb("slotf", [P, NT * KM])
        sloti = sb("sloti", [P, NT * KM], I32)
        slow_i = sb("slow_i", [P, NT * KM], I32)
        shigh_i = sb("shigh_i", [P, NT * KM], I32)
        slow = sb("slow", [P, NT * KM])
        shigh = sb("shigh", [P, NT * KM])
        wsum = sb("wsum", [P, NT])
        winv = sb("winv", [P, NT])
        wk = sb("wk", [P, NT, KM])
        ecmp = sb("ecmp", [P, NBM, E])
        ebf = sb("ebf", [P, NBM])
        ebi = sb("ebi", [P, NBM], I32)
        lowhot = [sb(f"lowhot{i}", [P, P], BF16) for i in range(4)]
        highhot = [sb(f"highhot{i}", [P, 2, NBM], BF16) for i in range(4)]
        tlf = sb("tlf", [P, NBM])
        tli = sb("tli", [P, NBM], I32)
        halfg = sb("halfg", [P, 4])
        hd = [nc.dram_tensor(f"hid_d{m}", [NTOK, H], F32).ap() for m in range(2)]
        yd = [nc.dram_tensor(f"y_d{m}", [mo.NB * P, H], F32).ap() for m, mo in enumerate(MOES)]

        amask = sb("amask", [P, T])
        ctxD = sb("ctxD", [P, B, D])
        qb = [sb(f"qb{i}", [P, R * L]) for i in range(2)]
        kb = [sb(f"kb{i}", [P, G, T]) for i in range(2)]
        vb = [sb(f"vb{i}", [P, P]) for i in range(2)]
        sm = [sb(f"sm{i}", [P, G, T]) for i in range(2)]
        amax = [sb(f"amax{i}", [P, G]) for i in range(2)]
        ap_ = [encloc, pact]
        aT = [x[:, :].rearrange("p (c t) -> p c t", c=4) for x in (enc, th)]
        arec = [sb(f"arec{i}", [P, P]) for i in range(2)]
        attT = region[:, 8192:12288].rearrange("p (r t) -> p r t", r=R)

        LOC2 = [bank[0], bank[7]]
        LOC, SW, E8, EB, AT, GT, RG = bank[0], bank[1], bank[2], bank[3], bank[4], bank[5], bank[6]

        names = """x_in w_in dchain achain  rstd_rdy hid_rdy tr_rdy tr_used pre_mm pre_used toep_mm comb_rdy comb_st toep_in toep_hi toep_rest ctx_hi ctx_rest 
        enc_mm enc_used w_ready init_rdy loc_rdy sw_rdy pact_rdy th_rdy e8_rdy x_rdy eb_rdy nmax_rdy p_rdy r_rdy at_rdy ae_rdy
        alT_rdy gt_rdy gT_rdy rg_rdy tg_rdy c2_rdy tc_rdy s_rdy prebuf_rdy ghist_rdy shist_rdy pb_free
        yg_mm yg_rdy y_mm x1_rdy out_done stat_rdy 
        qkv_rdy as_mm  smx_rdy am_rdy aexp_rdy at_mm aT_rdy ao_mm ao_used attb_mm att_x""".split()
        for mo in MOES:
            names += [f"{mo.tag}_{n}" for n in """hid_st logit_mm  act_done exp_in route_oh pos_mm  hot_rdy hot_mm 
            list_rdy eb_rdy w_in0 w_in1 w_in2 w_in3 xg_in0 xg_in1 xt_mm xt_rdy h_mm th_rdy  z_rdy zt_mm zt_rdy o_mm ob_rdy ob_st0 ob_st1
            sw_in sh_mm sh_th sh_z sh_zt sh_ztr sh_o sh_x yg_in0 yg_in1 yg_in2 yg_in3 yg_in4 yg_in5 yg_in6 yg_in7 yg_used""".split()]
        s = {n: sem(n) for n in names}

        block = ctx.enter_context(nc.Block())

        WLOADS = [(const[:, :], a["const"]), (ctxT[:, :, :], a["ctxT"]), (ctxP[:, :, :], a["ctxP"]), (lens_i[:, :], a["lens"]),
                  (lys[:, :, :], a["lysT"]), (lss[:, :], a["lssT"]), (lgs[:, :], a["lgsT"]), (gsb[:, :], a["gsb"]),
                  (wasT[:, 0, :], a["wasT"]), (wasT[:, 1, :], a["wasT"]), (wahT[:, :], a["wahT"]), (bacol[0:A, :], a["ba"]),
                  (bacol[A:P, :], a["ba"]), (wafT[:, :], a["wafT"]),
                  (lgyT[:, :], a["lgyT"]), (lsyT[:, :], a["lsyT"]), (gyb[:, :], a["gyb"]), (yyT[:, :], a["yyT"]),
                  (gates_g[:, :], a["gg"]), (gw[:, :, :, :], a["gw"]), (bias0[:, :], a["bias0"]),
                  (amask[0:T, :], a["amask"]), (amask[T:P, :], a["amask"]),
                  (ctxD[0:T, :, :], a["ctxD"]), (ctxD[T:P, :, :], a["ctxD"])]
        NW = len(WLOADS) + 3

        @block.sync
        def _(sp):
            for i in range(NT):
                sp.dma_start(xres[:, i, :], a["x"][i * P:(i + 1) * P, :]).then_inc(s["x_in"], 16)
            for dst, src in WLOADS:
                sp.dma_start(dst, src).then_inc(s["w_in"], 16)
            sp.wait_ge(s["init_rdy"], 1)
            sp.dma_start(convp[:, PAD:PAD + KW], a["convw"]).then_inc(s["w_in"], 16)
            sp.dma_start(va2[0:A, 1:2], a["va"]).then_inc(s["w_in"], 16)
            sp.dma_start(va2[A:P, 0:1], a["va"]).then_inc(s["w_in"], 16)
            sp.wait_ge(s["comb_rdy"], 1)
            sp.dma_start(comb_d[0:KWP, :], comb[0:KWP, :]).then_inc(s["comb_st"], 16)
            sp.wait_ge(s["comb_st"], 16)
            windows = bass.AP(comb_d.tensor, 0, [[A, T], [1, T * A]])
            for half in range(2):
                sp.dma_start(tr_f[half * T:(half + 1) * T, :], windows).then_inc(s["toep_in"], 16)

            def mixture(m):
                mo = MOES[m]
                q = lambda n: s[f"{mo.tag}_{n}"]
                for h in range(mo.shared):
                    if m == 0:
                        sp.wait_ge(s["loc_rdy"], 2 * L + 1)
                    else:
                        sp.wait_ge(s["f0_o_mm"], 4 + MOES[0].NB)
                    sp.dma_start(wbuf1[h][:, :, :], a[f"s1_{m}"][h]).then_inc(q("sw_in"), 16)
                    sp.dma_start(wbuf2[h][:, :, :], a[f"s2_{m}"][h]).then_inc(q("sw_in"), 16)
                for i in range(NT):
                    sp.wait_ge(s["hid_rdy"], (2 * m + 1) * NT + i + 1)
                    sp.dma_start(hd[m][i * P:(i + 1) * P, :], hid[:, i, :]).then_inc(q("hid_st"), 16)
                sp.wait_ge(q("eb_rdy"), 1)
                sp.wait_ge(q("sh_o"), NT * mo.shared)

                def weights(b):
                    sp.wait_ge(q("o_mm"), b.n + 1)
                    e = sp.value_load(ebi[0:1, bass.ds(b.n, 1)], min_val=0, max_val=E - 1)
                    sp.dma_start(wbuf1[b.slot][:, :, 0:2 * mo.I], a[f"w1_{m}"][bass.ds(e, 1)].rearrange("x p c n -> (x p) c n")).then_inc(q(f"w_in{b.slot}"), 16)
                    sp.dma_start(wbuf2[b.slot][:, 0:mo.IC, :], a[f"w2_{m}"][bass.ds(e, 1)].rearrange("x p c n -> (x p) c n")).then_inc(q(f"w_in{b.slot}"), 16)

                def store(b):
                    sp.wait_ge(q("ob_rdy"), b.n + 2)
                    sp.dma_start(yd[m][bass.ds(b.n * P, P), :], ob[b.par][:, :]).then_inc(q(f"ob_st{b.par}"), 16)

                def step(b, more=True):
                    if more:
                        weights(b.next(3))
                    store(b)

                for c_ in range(3):
                    weights(Turn(0, c_))
                step(Turn(0, 0))
                with sp.Fori(0, (mo.NB - 7) // 4) as j:
                    for c_ in range(1, 5):
                        step(Turn(j, c_))
                for n in range(mo.NB - 6, mo.NB):
                    step(Turn(0, n), more=n + 3 < mo.NB)

            mixture(0)
            mixture(1)
            for i in range(NT):
                sp.wait_ge(s["f1_yg_used"], MOES[1].K * (i + 1))
                sp.dma_start(out[i * P:(i + 1) * P, :], xres[:, i, :]).then_inc(s["out_done"], 16)
            sp.wait_ge(s["out_done"], 16 * NT)

        @block.vector
        def _(v):
            ch = [0]

            def link(ins):
                ch[0] += 1
                ins.then_inc(s["dchain"], 1)
                v.wait_ge(s["dchain"], ch[0])

            v.memset(convp[:, :], 0.0)
            link(v.memset(va2[:, :], 0.0))
            v.memset(s2[:, :], 0.0)
            v.memset(c2[:, :], 0.0)
            v.memset(al2[:, :, :], 0.0)
            v.memset(pn[:, :], 0.0)
            link(v.memset(yg[HS:HS + 1, :], 1.0))
            v.memset(prebuf[:, 0, 0:1], 0.0).then_inc(s["init_rdy"], 1)
            v.memset(alr[:, :], 0.0).then_inc(s["alT_rdy"], 1)
            v.memset(alr2[:, :], 0.0).then_inc(s["s_rdy"], 1)

            def layernorm_stats():
                for i in range(NT):
                    ins = v.bn_stats(stats[:, i, :], xres[:, i, :])
                link(ins)
                for i in range(NT):
                    ins = v.bn_aggr(mv[:, i, :], stats[:, i, :])
                link(ins)
                v.tensor_scalar(vareps[:, :], mv[:, :, 1], EPS, None, ALU.add).then_inc(s["stat_rdy"], 1)

            def layernorm_apply(n):
                v.wait_ge(s["rstd_rdy"], n)
                if n >= 3:
                    v.wait_ge(s["f0_hid_st"], 16 * NT)
                for i in range(NT):
                    src, dst = xres[:, i, :], hid[:, i, :]
                    if n == 3:
                        src = src.rearrange("p (g r d) -> p g r d", g=G, r=R)
                        dst = dst.rearrange("p (r g d) -> p g r d", g=G, r=R)
                    v.tensor_scalar(dst, src, mv[:, i, 0:1], rstd[:, i:i + 1], ALU.subtract,
                                    ALU.mult).then_inc(s["hid_rdy"], 1)

            def transposed(n):
                for i in range(NT):
                    v.wait_ge(s["tr_rdy"], (n - 1) * NT + i + 1)
                    src = bank[i % 2][:, :].rearrange("p (c t) -> p c t", c=HC)
                    if n == 3:
                        dst = hidT[:, :, :].rearrange("p c t -> p (c t)").rearrange(
                            "p (b c l) -> p c l b", b=B, c=HC)[:, :, i * 8:(i + 1) * 8, :]
                        for c in range(HC):
                            ins = v.tensor_copy(dst[:, c], src[:, c].rearrange("p (l b) -> p l b", b=B))
                        ins.then_inc(s["tr_used"], 1)
                    else:
                        v.tensor_copy(hidT[:, :, i * P:(i + 1) * P], src).then_inc(s["tr_used"], 1)

            v.wait_ge(s["x_in"], 16 * NT)
            layernorm_stats()
            layernorm_apply(1)
            transposed(1)
            v.wait_ge(s["w_in"], 16 * NW)
            v.tensor_scalar(wasT[:, :, :], wasT[:, :, :], 0.5, None, ALU.mult)
            v.tensor_scalar(lsyT[:, :], lsyT[:, :], 0.5, None, ALU.mult)
            v.tensor_scalar(lgs[:, 2 * HS:3 * HS], lgs[:, 2 * HS:3 * HS], 2.0, None, ALU.mult)
            v.tensor_copy(lens_f[:, :], lens_i[:, :])
            for g in (0, 1, 3):
                v.tensor_scalar(lss[:, g * HS:(g + 1) * HS], lss[:, g * HS:(g + 1) * HS], 0.5, None, ALU.mult)
            link(v.memset(nmax[:, :], 0.0))
            v.tensor_scalar(maskb[:, :], cn("tcount", B), lens_f[:, 0:1], NEG, ALU.is_ge, ALU.mult).then_inc(s["w_ready"], 1)
            for n in range(8):
                g, hf = n // 2, n % 2
                v.wait_ge(s["pre_mm"], n + 1)
                v.tensor_scalar(pre[:, hf * 32:(hf + 1) * 32, g, :],
                                bank[n % 2][0:HS, :].rearrange("p (l b) -> p l b", b=B), gsb[:, g:g + 1],
                                2.0 if g == 2 else 1.0, ALU.add, ALU.mult).then_inc(s["pre_used"], 1)
            v.wait_ge(s["enc_mm"], 1)
            v.tensor_scalar(enc[:, :], bank[2][:, :], bacol[:, 0:1], None, ALU.add).then_inc(s["enc_used"], 1)
            v.wait_ge(s["toep_mm"], 1)
            v.tensor_scalar(comb[0:KWP, :], bank[3][0:KWP, 0:A], 1.0 / PSCALE, None, ALU.mult).then_inc(s["comb_rdy"], 1)
            cflat = ctxP[:, :, :].rearrange("p j d -> p (j d)")
            v.tensor_scalar(cflat, cflat, 1.0 / PSCALE, None, ALU.mult).then_inc(s["ctx_rest"], 1)
            v.wait_ge(s["ctx_hi"], 1)
            v.tensor_tensor(ctxr[:, :], cflat, ctx3[:, 0, :], ALU.subtract).then_inc(s["ctx_rest"], 1)
            v.wait_ge(s["ctx_hi"], 2)
            v.tensor_tensor(ctx3[:, 2, :], ctxr[:, :], ctx3[:, 1, :], ALU.subtract).then_inc(s["ctx_rest"], 1)
            v.wait_ge(s["toep_hi"], 1)
            v.tensor_tensor(tr_f[T:P, :], tr_f[T:P, :], toepA[T:P, :], ALU.subtract).then_inc(s["toep_rest"], 1)
            v.wait_ge(s["toep_hi"], 2)
            v.tensor_tensor(toepB[T:P, :], tr_f[T:P, :], toepA[T:P, :], ALU.subtract).then_inc(s["toep_rest"], 1)
            base = ch[0]
            PER = 6
            with v.Fori(0, L) as l:
                k = [0]

                def clink(ins):
                    k[0] += 1
                    ins.then_inc(s["dchain"], 1)
                    v.wait_ge(s["dchain"], base + l * PER + k[0])

                for half in range(2):
                    v.wait_ge(s["loc_rdy"], 2 * l + half + 1)
                    sl = slice(half * 256, (half + 1) * 256)
                    clink(v.tensor_tensor(encloc[:, sl], enc[:, sl], LOC2[half][:, 0:256], ALU.add))
                    if half == 0:
                        v.wait_ge(s["sw_rdy"], l + 1)
                    for c in (2 * half, 2 * half + 1):
                        sl = slice(c * P, (c + 1) * P)
                        v.tensor_tensor(pact[:, sl].rearrange("p (u b) -> p u b", b=B),
                                        encloc[:, sl].rearrange("p (u b) -> p u b", b=B),
                                        SW[:, 0:B].unsqueeze(1).broadcast_to([P, 8, B]), ALU.add).then_inc(s["pact_rdy"], 1)
                v.wait_ge(s["e8_rdy"], l + 1)
                v.tensor_tensor(xexp[:, :, :, :],
                                E8[:, 0:8].rearrange("p (c t) -> p c t", c=4).unsqueeze(2).broadcast_to([P, 4, 8, 2]),
                                cn("dmask").unsqueeze(1).unsqueeze(3).broadcast_to([P, 4, 8, 2]),
                                ALU.mult).then_inc(s["x_rdy"], 1)
                v.wait_ge(s["eb_rdy"], l + 1)
                v.tensor_reduce(nmax[:, :], EB[0:B, 0:T], AX.X, ALU.max, negate=True).then_inc(s["nmax_rdy"], 1)
                v.wait_ge(s["p_rdy"], l + 1)
                clink(v.reciprocal(rinv[:, :], psum_e[:, :]))
                v.tensor_scalar(pn[0:B, :].rearrange("p (r t) -> p r t", r=2), prob[:, :].unsqueeze(1).broadcast_to([B, 2, T]),
                                rinv[:, 0:1], PSCALE, ALU.mult, ALU.mult).then_inc(s["r_rdy"], 1)
                v.wait_ge(s["at_rdy"], l + 1)
                clink(v.tensor_copy(al2[:, 0, :], AT[:, 0:B]))
                clink(v.tensor_tensor(al2[:, 1, :], AT[:, 0:B], al2[:, 0, :], ALU.subtract))
                v.tensor_tensor(ae[:, :, :], al2[:, :, :], cn("bdmask").unsqueeze(1).broadcast_to([P, 2, B]),
                                ALU.mult).then_inc(s["ae_rdy"], 1)
                v.wait_ge(s["gt_rdy"], l + 1)
                v.wait_ge(s["ghist_rdy"], l + 1)
                v.tensor_reduce(gT[:, :], GT[:, 0:2 * B].rearrange("p (s b) -> p b s", s=2), AX.X,
                                ALU.add).then_inc(s["gT_rdy"], 1)
                v.wait_ge(s["tg_rdy"], l + 1)
                v.scalar_tensor_tensor(la[:, :], tg[:, 0, :], 1.0, tg[:, 2, :], ALU.add, ALU.mult)
                clink(v.scalar_tensor_tensor(lb[:, :], tg[:, 1, :], 1.0, c2[:, :], ALU.add, ALU.mult))
                v.scalar_tensor_tensor(c2[:, :], lb[:, :], 0.5, la[:, :], ALU.mult, ALU.add).then_inc(s["c2_rdy"], 1)
                v.wait_ge(s["tc_rdy"], l + 1)
                v.wait_ge(s["shist_rdy"], l + 1)
                v.scalar_tensor_tensor(s2[:, :], tg[:, 3, :], 1.0, tc[:, :], ALU.add, ALU.mult).then_inc(s["s_rdy"], 1)
                assert k[0] == PER
            ch[0] += L * PER
            for i in range(NT):
                v.wait_ge(s["y_mm"], i + 1)
                ins = v.scalar_tensor_tensor(xres[:, i, :], bank[i % 2][:, :], gates_g[:, 0:1], xres[:, i, :], ALU.mult,
                                             ALU.add)
                ins.then_inc(s["x1_rdy"], 1)
            v.wait_ge(s["x1_rdy"], NT)
            link(v.tensor_scalar(halfg[:, :], gates_g[:, :], 0.5, None, ALU.mult))

            def route(m):
                mo = MOES[m]
                K, NB, NK = mo.K, mo.NB, NT * mo.K
                q = lambda n: s[f"{mo.tag}_{n}"]
                g_ffn = gates_g[:, 2 + m:3 + m]
                if m == 0:
                    v.wait_ge(q("act_done"), 1)
                    link(v.tensor_scalar(sc2[:, :, :], sc[:, :, :], 0.5, 0.5, ALU.mult, ALU.add))
                    link(v.tensor_tensor(sc[:, :, :], sc2[:, :, :], bias0[:, :].unsqueeze(1).broadcast_to([P, NT, E]),
                                         ALU.add))
                else:
                    v.wait_ge(q("logit_mm"), 1)
                    lg = bank[6][:, 0:NT * E].rearrange("p (i e) -> p i e", e=E)
                    link(v.tensor_reduce(smax[:, :], lg, AX.X, ALU.max))
                    v.tensor_tensor(sc2[:, :, :], lg, smax[:, :].unsqueeze(2).broadcast_to([P, NT, E]),
                                    ALU.subtract).then_inc(q("exp_in"), 1)
                    v.wait_ge(q("act_done"), 1)
                    link(v.tensor_reduce(wsum[:, :], sc[:, :, :], AX.X, ALU.add))
                    link(v.reciprocal(winv[:, :], wsum[:, :]))
                    link(v.tensor_tensor(sc[:, :, :], sc[:, :, :], winv[:, :].unsqueeze(2).broadcast_to([P, NT, E]), ALU.mult))
                for i in range(NT):
                    ins = v.max(top8[:, i, :], sc[:, i, :])
                link(ins)
                for i in range(NT):
                    ins = v.max_index(idx8[:, i, :], top8[:, i, :], sc[:, i, :])
                link(ins)
                link(v.tensor_copy(idxf[:, 0:NK].rearrange("p (i k) -> p i k", k=K), idx8[:, :, 0:K]))
                oh = onehot[:, 0:NK, :]
                link(v.tensor_tensor(oh, cn("iota")[:, 0:E].unsqueeze(1).broadcast_to([P, NK, E]),
                                     idxf[:, 0:NK].unsqueeze(2).broadcast_to([P, NK, E]), ALU.is_equal))
                v.tensor_reduce(msum[:, :, :], oh.rearrange("p (i k) e -> p i e k", k=K), AX.X,
                                ALU.add).then_inc(q("route_oh"), 1)
                link(v.tensor_reduce(wsum[:, :], top8[:, :, 0:K], AX.X, ALU.add))
                if m == 0:
                    link(v.tensor_scalar(wsum[:, :], wsum[:, :], 1e-20, None, ALU.add))
                link(v.reciprocal(winv[:, :], wsum[:, :]))
                link(v.tensor_scalar(winv[:, :], winv[:, :], g_ffn, None, ALU.mult))
                link(v.tensor_tensor(wk[:, :, 0:K], top8[:, :, 0:K], winv[:, :].unsqueeze(2).broadcast_to([P, NT, K]), ALU.mult))
                pos = bank[7][:, 0:NT * E].rearrange("p (i e) -> p i e", e=E)
                tot = bank[7][:, NT * E:2 * NT * E].rearrange("p (i e) -> p i e", e=E)
                v.wait_ge(q("pos_mm"), 1)
                link(v.memset(cum[:, 0, :], 0.0))
                for i in range(1, NT):
                    link(v.tensor_tensor(cum[:, i, :], cum[:, i - 1, :], tot[:, i - 1, :], ALU.add))
                link(v.tensor_tensor(count[:, :], cum[:, NT - 1, :], tot[:, NT - 1, :], ALU.add))
                link(v.tensor_scalar(nblk_i[:, :], count[:, :], float(P - 1), None, ALU.add))
                link(v.tensor_scalar(nblk_j[:, :], nblk_i[:, :], 7, None, ALU.arith_shift_right))
                link(v.tensor_copy(nblk[:, :], nblk_j[:, :]))
                link(v.tensor_tensor(trib[:, :, :], nblk[:, :].unsqueeze(1).broadcast_to([P, E, E]),
                                     cn("tri").rearrange("p (a b) -> p a b", a=E), ALU.mult))
                link(v.tensor_reduce(bstart[:, :], trib[:, :, :], AX.X, ALU.add))
                link(v.tensor_tensor(bend[:, :], bstart[:, :], nblk[:, :], ALU.add))
                link(v.tensor_tensor(ecmp[:, 0:NB, :], bend[:, :].unsqueeze(1).broadcast_to([P, NB, E]),
                                     cn("iota")[:, 0:NB].unsqueeze(2).broadcast_to([P, NB, E]), ALU.is_le))
                link(v.tensor_reduce(ebf[:, 0:NB], ecmp[:, 0:NB, :], AX.X, ALU.add))
                v.tensor_scalar(ebi[:, 0:NB], ebf[:, 0:NB], float(E - 1), None, ALU.min).then_inc(q("eb_rdy"), 1)
                link(v.scalar_tensor_tensor(place[:, :, :], bstart[:, :].unsqueeze(1).broadcast_to([P, NT, E]), float(P),
                                            cum[:, :, :], ALU.mult, ALU.add))
                link(v.tensor_tensor(place[:, :, :], place[:, :, :], pos, ALU.add))
                for k in range(K):
                    ins = v.tensor_tensor(ohs[:, 0:NK, :].rearrange("p (i k) e -> p i k e", k=K)[:, :, k, :],
                                          oh.rearrange("p (i k) e -> p i k e", k=K)[:, :, k, :], place[:, :, :], ALU.mult)
                link(ins)
                link(v.tensor_reduce(slotf[:, 0:NK], ohs[:, 0:NK, :], AX.X, ALU.add))
                link(v.tensor_copy(sloti[:, 0:NK], slotf[:, 0:NK]))
                v.tensor_scalar(slow_i[:, 0:NK], sloti[:, 0:NK], P - 1, None, ALU.bitwise_and)
                link(v.tensor_scalar(shigh_i[:, 0:NK], sloti[:, 0:NK], 7, None, ALU.arith_shift_right))
                v.tensor_copy(slow[:, 0:NK], slow_i[:, 0:NK])
                link(v.tensor_copy(shigh[:, 0:NK], shigh_i[:, 0:NK]))
                for n in range(NK):
                    if n >= 4:
                        v.wait_ge(q("hot_mm"), n - 3)
                    v.tensor_scalar(lowhot[n % 4][:, :], cn("iota"), slow[:, n:n + 1], None, ALU.is_equal)
                    v.tensor_scalar(highhot[n % 4][:, 0, 0:NB], cn("iota")[:, 0:NB], shigh[:, n:n + 1], cn("prow"),
                                    ALU.is_equal, ALU.mult)
                    v.tensor_scalar(highhot[n % 4][:, 1, 0:NB], cn("iota")[:, 0:NB], shigh[:, n:n + 1], float(n // K),
                                    ALU.is_equal, ALU.mult).then_inc(q("hot_rdy"), 1)
                v.wait_ge(q("hot_mm"), NK)
                link(v.tensor_copy(tlf[:, 0:NB], bank[6][:, 0:NB]))
                v.scalar_tensor_tensor(tli[:, 0:NB], bank[6][:, NB:2 * NB], float(P), tlf[:, 0:NB], ALU.mult,
                                       ALU.add).then_inc(q("list_rdy"), 1)

            def shared(m):
                mo = MOES[m]
                q = lambda n: s[f"{mo.tag}_{n}"]
                N = NT * mo.shared

                def inner(n):
                    p_ = n % 2
                    hb = bank[p_]
                    v.wait_ge(q("sh_th"), n + 1)
                    link(v.scalar_tensor_tensor(ga[p_][:, :], gth[p_][:, :], 1.0, hb[:, 0:256], ALU.add, ALU.mult))
                    v.tensor_tensor(zb[p_][:, :], ga[p_][:, :], hb[:, 256:512], ALU.mult).then_inc(q("sh_z"), 1)

                def outer(n):
                    p_ = n % 2
                    v.wait_ge(q("sh_zt"), n + 1)
                    v.tensor_copy(zT[p_][:, :, :], bank[2][:, 0:256].rearrange("p (c t) -> p c t", c=2)).then_inc(q("sh_ztr"), 1)
                    v.wait_ge(q("sh_o"), n + 1)
                    i = n % NT
                    if n >= NT:
                        v.wait_ge(q("sh_x"), n - NT + 1)
                    v.scalar_tensor_tensor(xres[:, i, :], bank[3 + p_][:, :], halfg[:, 2 + m:3 + m], xres[:, i, :],
                                           ALU.mult, ALU.add).then_inc(q("sh_x"), 1)

                for n in range(N + 1):
                    if n < N:
                        inner(n)
                    if n > 0:
                        outer(n - 1)

            def experts(m):
                mo = MOES[m]
                I, IC = mo.I, mo.IC
                q = lambda n: s[f"{mo.tag}_{n}"]
                base = ch[0]

                def inner(b):
                    v.wait_ge(q("th_rdy"), b.n + 1)
                    v.scalar_tensor_tensor(ga[b.par][:, 0:I], gth[b.par][:, 0:I], 1.0, bank[2 + b.par][:, 0:I], ALU.add,
                                           ALU.mult).then_inc(s["dchain"], 1)
                    v.wait_ge(s["dchain"], base + 1 + b.n)
                    v.tensor_tensor(zb[b.par][:, 0:I], ga[b.par][:, 0:I], bank[2 + b.par][:, I:2 * I], ALU.mult).then_inc(q("z_rdy"), 1)

                def outer(b):
                    v.wait_ge(q("zt_mm"), b.n + 1)
                    v.tensor_copy(zT[b.par][:, 0:IC, :], bank[4][:, 0:I].rearrange("p (c t) -> p c t", c=IC)).then_inc(q("zt_rdy"), 1)

                def step(b, first=False):
                    if not first:
                        outer(b.next(-1))
                    inner(b)

                step(Turn(0, 0), first=True)
                with v.Fori(0, (mo.NB - 3) // 4) as j:
                    for c_ in range(1, 5):
                        step(Turn(j, c_))
                step(Turn(0, mo.NB - 2))
                step(Turn(0, mo.NB - 1))
                outer(Turn(0, mo.NB - 1))
                ch[0] += mo.NB

            def combine(m):
                mo = MOES[m]
                q = lambda n: s[f"{mo.tag}_{n}"]
                v.wait_ge(q("sh_x"), NT * mo.shared)
                for n in range(NT * mo.K):
                    i, k = n // mo.K, n % mo.K
                    v.wait_ge(q(f"yg_in{n % NYG}"), 16 * (n // NYG + 1))
                    if k > 0:
                        v.wait_ge(q("yg_used"), n)
                    ins = v.scalar_tensor_tensor(xres[:, i, :], yrow[n % NYG][:, :], wk[:, i, k:k + 1], xres[:, i, :],
                                                 ALU.mult, ALU.add)
                    ins.then_inc(q("yg_used"), 1)
                v.wait_ge(q("yg_used"), NT * mo.K)

            def attention():
                base = ch[0]

                def scores(n, par):
                    v.wait_ge(s["as_mm"], n + 1)
                    v.wait_ge(s["aexp_rdy"], n + 1)
                    sb_ = bank[par][:, :].rearrange("p (g t) -> p g t", g=G)
                    v.tensor_tensor(sm[par][:, :, :], sb_, amask[:, :].unsqueeze(1).broadcast_to([P, G, T]),
                                    ALU.add).then_inc(s["smx_rdy"], 1)
                    v.wait_ge(s["smx_rdy"], n + 1)
                    v.tensor_reduce(amax[par][:, :], sm[par][:, :, :], AX.X, ALU.max).then_inc(s["dchain"], 1)
                    v.wait_ge(s["dchain"], base + 1 + n)
                    v.tensor_tensor(sm[par][:, :, :], sm[par][:, :, :], amax[par][:, :].unsqueeze(2).broadcast_to([P, G, T]),
                                    ALU.subtract).then_inc(s["am_rdy"], 1)

                def norm(n, par, b, rp):
                    v.wait_ge(s["ao_mm"], n + 5)
                    v.reciprocal(arec[par][:, :], bank[4 + par][:, P:2 * P]).then_inc(s["ao_used"], 1)
                    v.wait_ge(s["ao_used"], 2 * n + 5)
                    dst = attT[:, :, :].rearrange("p r (l b) -> p b r l", b=B)[:, bass.ds(b, 1), 2 * rp:2 * rp + 2, :]
                    v.tensor_tensor(dst, bank[4 + par][:, 0:P].rearrange("p (x r l) -> p x r l", x=1, r=2),
                                    arec[par][:, :].rearrange("p (x r l) -> p x r l", x=1, r=2), ALU.mult).then_inc(s["ao_used"], 1)

                def step(n, q_, b, first=False, last=False):
                    if not last:
                        scores(n, q_ % 2)
                    if not first:
                        norm(n - 2, q_ % 2, b - 1, q_ % 2)

                N = 2 * B
                v.sem_inc(s["ao_used"], 4)
                for n in range(2):
                    step(n, n, 0, first=True)
                with v.Fori(0, (N - 4) // 4) as j:
                    for q_ in range(4):
                        step(4 * j + 2 + q_, q_, 2 * j + 1 + q_ // 2)
                for n in range(N - 2, N + 2):
                    step(n, n, n // 2, last=n >= N)
                ch[0] += N
                for i in range(NT):
                    v.wait_ge(s["attb_mm"], i + 1)
                    for r_ in range(R):
                        x_r = xres[:, i, :].rearrange("p (g r d) -> p r g d", g=G, r=R)[:, r_]
                        ins = v.scalar_tensor_tensor(x_r, bank[i % 2][:, r_ * P:(r_ + 1) * P].rearrange("p (g d) -> p g d", g=G),
                                                     gates_g[:, 1:2], x_r, ALU.mult, ALU.add)
                    ins.then_inc(s["att_x"], 1)
                v.wait_ge(s["att_x"], NT)

            layernorm_stats()
            layernorm_apply(2)
            transposed(2)
            route(0)
            shared(0)
            experts(0)
            combine(0)
            layernorm_stats()
            layernorm_apply(3)
            transposed(3)
            attention()
            layernorm_stats()
            layernorm_apply(4)
            transposed(4)
            route(1)
            shared(1)
            experts(1)
            combine(1)

        @block.gpsimd
        def _(g):
            def rstds(n):
                g.wait_ge(s["stat_rdy"], n)
                g.tensor_tensor(rstd[:, :], vareps[:, :], cn("half")[:, 0:NT], ALU.pow).then_inc(s["rstd_rdy"], 1)
            g.wait_ge(s["w_in"], 16 * NW)
            rstds(1)
            g.wait_ge(s["pre_used"], 8)
            g.wait_ge(s["init_rdy"], 1)
            g.memset(shist[:, 0, :], 0.0).then_inc(s["shist_rdy"], 1)
            g.memset(ghist[:, 0, :], 0.0).then_inc(s["ghist_rdy"], 1)
            with g.Fori(0, L) as l:
                g.wait_ge(s["pb_free"], l + 1)
                g.tensor_copy(prebuf[:, :, :], pre[:, l, :, :]).then_inc(s["prebuf_rdy"], 1)
                g.wait_ge(s["gT_rdy"], l + 1)
                g.tensor_copy(ghist[:, l, :], gT[:, :]).then_inc(s["ghist_rdy"], 1)
                g.wait_ge(s["s_rdy"], l + 2)
                g.tensor_copy(shist[:, l + 1, :], s2[:, :]).then_inc(s["shist_rdy"], 1)


            def gathers(m):
                mo = MOES[m]
                q = lambda n: s[f"{mo.tag}_{n}"]
                g.wait_ge(q("list_rdy"), 1)
                g.wait_ge(q("hid_st"), 16 * NT)

                for b in range(mo.NB):
                    g.wait_ge(q("xt_mm"), b + 1)
                    g.indirect_dma_start(out=xg[b % 2][:, :], out_offset=None, in_=hd[m],
                                         in_offset=bass.IndirectOffsetOnAxis(ap=tli[:, b:b + 1], axis=0)).then_inc(q(f"xg_in{b % 2}"), 16)
                for par in range(2):
                    g.wait_ge(q(f"ob_st{par}"), 16 * (mo.NB // 2 + 2 - par))
                for n in range(NT * mo.K):
                    if n >= NYG:
                        g.wait_ge(q("yg_used"), n - NYG + 1)
                    g.indirect_dma_start(out=yrow[n % NYG][:, :], out_offset=None, in_=yd[m],
                                         in_offset=bass.IndirectOffsetOnAxis(ap=sloti[:, n:n + 1], axis=0)).then_inc(q(f"yg_in{n % NYG}"), 16)

            def attention_operands():
                g.wait_ge(s["tr_used"], 3 * NT)
                qT = hidT[:, :, :].rearrange("p c t -> p (c t)").rearrange("p (b x) -> p b x", b=B)

                def batch(b, par):
                    g.wait_ge(s["ao_mm"], 2 * b + 2)
                    g.tensor_copy(qb[par][:, :], qT[:, bass.ds(b, 1), :].rearrange("p x y -> p (x y)"))
                    g.tensor_tensor(kb[par][:, :, :], ctxT[:, :, bass.ds(b, 1)].rearrange("p t x -> p x t").broadcast_to([P, G, T]),
                                    cn("gmask").unsqueeze(2).broadcast_to([P, G, T]), ALU.mult)
                    g.tensor_tensor(vb[par][:, :], ctxD[:, bass.ds(b, 1), :].rearrange("p x y -> p (x y)"), cn("vmask"),
                                    ALU.mult).then_inc(s["qkv_rdy"], 1)

                with g.Fori(0, B // 2) as j:
                    batch(2 * j, 0)
                    batch(2 * j + 1, 1)

            rstds(2)
            gathers(0)
            rstds(3)
            attention_operands()
            rstds(4)
            gathers(1)

        @block.scalar
        def _(c):
            c.preload_act_table(ACT.Tanh)
            c.wait_ge(s["w_in"], 16 * NW)
            c.activation(gates_g[:, :], gates_g[:, :], ACT.Tanh).then_inc(s["achain"], 1)
            c.wait_ge(s["ctx_rest"], 1)
            c.copy(ctx3[:, 0, :], ctxP[:, :, :].rearrange("p j d -> p (j d)")).then_inc(s["ctx_hi"], 1)
            c.wait_ge(s["ctx_rest"], 2)
            c.copy(ctx3[:, 1, :], ctxr[:, :]).then_inc(s["ctx_hi"], 1)
            c.wait_ge(s["toep_in"], 32)
            c.copy(toepA[:, :], tr_f[:, :]).then_inc(s["toep_hi"], 1)
            c.wait_ge(s["toep_rest"], 1)
            c.copy(toepA[T:P, :], tr_f[T:P, :]).then_inc(s["toep_hi"], 1)
            with c.Fori(0, L) as l:
                for n in range(4):
                    c.wait_ge(s["pact_rdy"], 4 * l + n + 1)
                    c.activation(th[:, n * P:(n + 1) * P], pact[:, n * P:(n + 1) * P], ACT.Tanh).then_inc(s["th_rdy"], 1)
                c.wait_ge(s["nmax_rdy"], l + 1)
                c.activation(prob[:, :], EB[0:B, 0:T], ACT.Exp, bias=nmax[:, 0:1],
                             accum_out=psum_e[:, :]).then_inc(s["p_rdy"], 1)
                c.wait_ge(s["rg_rdy"], l + 1)
                c.activation(tg[:, :, :], RG[0:HS, 0:4 * B].rearrange("p (g b) -> p g b", g=4), ACT.Tanh,
                             scale=0.5).then_inc(s["tg_rdy"], 1)
                c.wait_ge(s["c2_rdy"], l + 1)
                c.activation(tc[:, :], c2[:, :], ACT.Tanh, scale=0.5).then_inc(s["tc_rdy"], 1)
            for n in range(2):
                c.wait_ge(s["yg_mm"], n + 1)
                c.activation(yg[0:HS, n * 512:(n + 1) * 512], bank[2 + n][0:HS, :], ACT.Tanh,
                             bias=gyb[:, 0:1]).then_inc(s["yg_rdy"], 1)


            def mixture(m):
                mo = MOES[m]
                I = mo.I
                q = lambda n: s[f"{mo.tag}_{n}"]
                lg = bank[6][:, 0:NT * E].rearrange("p (i e) -> p i e", e=E)
                if m == 0:
                    c.wait_ge(q("logit_mm"), 1)
                    c.activation(sc[:, :, :], lg, ACT.Tanh, scale=0.5).then_inc(q("act_done"), 1)
                else:
                    c.wait_ge(q("exp_in"), 1)
                    c.activation(sc[:, :, :], sc2[:, :, :], ACT.Exp).then_inc(q("act_done"), 1)
                for n in range(NT * mo.shared):
                    c.wait_ge(q("sh_mm"), n + 1)
                    if n >= 2:
                        c.wait_ge(q("sh_z"), n - 1)
                    c.activation(gth[n % 2][:, :], bank[n % 2][:, 0:256], ACT.Tanh, scale=0.5).then_inc(q("sh_th"), 1)

                def turned(b):
                    c.wait_ge(q("xt_mm"), b.n + 3)
                    c.copy(xgT[b.par][:, :, :], bank[b.par][:, :].rearrange("p (c t) -> p c t", c=HC)).then_inc(q("xt_rdy"), 1)

                def inner(b):
                    c.wait_ge(q("h_mm"), b.n + 1)
                    c.activation(gth[b.par][:, 0:I], bank[2 + b.par][:, 0:I], ACT.Tanh, scale=0.5).then_inc(q("th_rdy"), 1)

                def out_(b):
                    c.wait_ge(q("o_mm"), b.n + 5)
                    c.wait_ge(q(f"ob_st{b.par}"), 16 * (b.h + 1))
                    c.mul(ob[b.par][:, :], bank[5][:, :], 0.5).then_inc(q("ob_rdy"), 1)

                def step(b, first=False, last=False):
                    if not last:
                        turned(b.next())
                    if not first:
                        out_(b.next(-1))
                    inner(b)

                for par in range(2):
                    c.sem_inc(q(f"ob_st{par}"), 16)
                c.sem_inc(q("ob_rdy"), 1)
                turned(Turn(0, 0))
                step(Turn(0, 0), first=True)
                with c.Fori(0, (mo.NB - 3) // 4) as j:
                    for c_ in range(1, 5):
                        step(Turn(j, c_))
                step(Turn(0, mo.NB - 2))
                step(Turn(0, mo.NB - 1), last=True)
                out_(Turn(0, mo.NB - 1))

            def attention():
                def probs(n, par):
                    c.wait_ge(s["am_rdy"], n + 1)
                    c.activation(ap_[par][:, :], sm[par][:, :, :].rearrange("p g t -> p (g t)"), ACT.Exp).then_inc(s["aexp_rdy"], 1)

                def turned(n, par):
                    c.wait_ge(s["at_mm"], n + 1)
                    c.copy(aT[par][:, :, :], bank[2 + par][:, :].rearrange("p (c t) -> p c t", c=4)).then_inc(s["aT_rdy"], 1)

                def step(n, q_, first=False, last=False):
                    if not last:
                        probs(n, q_ % 2)
                    if not first:
                        turned(n - 1, (q_ + 1) % 2)

                N = 2 * B
                c.sem_inc(s["aexp_rdy"], 2)
                for n in range(2):
                    step(n, n, first=n == 0)
                with c.Fori(0, (N - 4) // 4) as j:
                    for q_ in range(4):
                        step(4 * j + 2 + q_, q_)
                for n in range(N - 2, N + 1):
                    step(n, n, last=n >= N)

            mixture(0)
            attention()
            mixture(1)

        @block.tensor
        def _(t):
            def turn_hidden(n):
                for i in range(NT):
                    t.wait_ge(s["hid_rdy"], (n - 1) * NT + i + 1)
                    if i >= 2:
                        t.wait_ge(s["tr_used"], (n - 1) * NT + i - 1)
                    for c in range(HC):
                        ins = t.transpose(bank[i % 2][:, c * P:(c + 1) * P], hid[:, i, c * P:(c + 1) * P], ident)
                    ins.then_inc(s["tr_rdy"], 1)

            t.wait_ge(s["w_in"], 16 * NW)
            turn_hidden(1)
            t.wait_ge(s["w_ready"], 1)
            t.wait_ge(s["tr_used"], NT)
            for n in range(8):
                gi, hf = n // 2, n % 2
                if n >= 2:
                    t.wait_ge(s["pre_used"], n - 1)
                for c in range(HC):
                    ins = t.matmul(bank[n % 2][0:HS, :], lys[:, c, gi * HS:(gi + 1) * HS],
                                   hidT[:, c, hf * 512:(hf + 1) * 512], start=(c == 0), stop=(c == HC - 1))
                ins.then_inc(s["pre_mm"], 1)
            for t2 in range(2):
                ins = t.matmul(bank[2][t2 * A:(t2 + 1) * A, :], wahT[:, :], ctxT[:, 1 - t2:T:2, :], start=True, stop=True)
            ins.then_inc(s["enc_mm"], 1)
            t.matmul(bank[3][0:KWP, 0:A], convp[:, :], wafT[:, :], start=True, stop=True).then_inc(s["toep_mm"], 1)
            t.wait_ge(s["pre_used"], 8)
            t.wait_ge(s["enc_used"], 1)
            t.wait_ge(s["comb_rdy"], 1)
            t.wait_ge(s["ctx_rest"], 3)
            t.wait_ge(s["toep_rest"], 2)
            t.transpose(bank[7][0:B, 0:B], ident[0:B, 0:B], ident[0:B, 0:B]).then_inc(s["pb_free"], 1)
            def locations(us):
                for u in us:
                    w = slice((NU - 1 - u) * P, (NU - u) * P)
                    dst = LOC2[u // 16][:, (u % 16) * B:(u % 16 + 1) * B]
                    t.matmul(dst, toepA[:, w], al2[:, 0, :], start=True, stop=False)
                    t.matmul(dst, toepA[:, w], al2[:, 1, :], start=False, stop=False)
                    ins = t.matmul(dst, toepB[T:P, w], al2[T:P, 0, :], start=False, stop=True)
                return ins

            t.wait_ge(s["alT_rdy"], 1)
            locations(range(0, 16)).then_inc(s["loc_rdy"], 1)
            with t.Fori(0, L) as l:
                locations(range(16, NU)).then_inc(s["loc_rdy"], 1)
                t.wait_ge(s["prebuf_rdy"], l + 1)
                t.wait_ge(s["s_rdy"], l + 1)
                t.matmul(SW[:, 0:B], wasT[:, :, :].rearrange("p r a -> p (r a)"), s2[:, :], start=True,
                         stop=True).then_inc(s["sw_rdy"], 1)
                t.matmul(EB[0:B, 0:T], ident[0:B, 0:B], maskb[:, :], start=True, stop=False)
                for n in range(4):
                    t.wait_ge(s["th_rdy"], 4 * l + n + 1)
                    ins = t.matmul(E8[:, 2 * n:2 * n + 2], th[:, n * P:(n + 1) * P], va2[:, :], start=True, stop=True)
                ins.then_inc(s["e8_rdy"], 1)
                t.wait_ge(s["x_rdy"], l + 1)
                t.matmul(EB[0:B, 0:T], cn("bsel"), xexp[:, :, :, :].rearrange("p c u t -> p (c u t)"), start=False,
                         stop=True).then_inc(s["eb_rdy"], 1)
                t.matmul(RG[0:HS, 0:4 * B], ident[0:HS, 0:HS], prebuf[:, :, :].rearrange("p g b -> p (g b)"), start=True, stop=False)
                for g in range(4):
                    ins = t.matmul(RG[0:HS, g * B:(g + 1) * B], lss[:, g * HS:(g + 1) * HS], s2[:, :], start=False, stop=False)
                ins.then_inc(s["pb_free"], 1)
                t.wait_ge(s["r_rdy"], l + 1)
                t.transpose(AT[:, 0:P], pn[:, :], ident).then_inc(s["at_rdy"], 1)
                t.wait_ge(s["ae_rdy"], l + 1)
                for j in range(8):
                    for k in range(3):
                        ins = t.matmul(GT[:, 0:2 * B].rearrange("p (s b) -> p s b", s=2)[:, :, j:B:8],
                                       ctx3[:, k, j * D:(j + 1) * D], ae[:, :, j:B:8], start=(k == 0), stop=(k == 2))
                ins.then_inc(s["gt_rdy"], 1)
                locations(range(0, 6))
                t.wait_ge(s["gT_rdy"], l + 1)
                for g in range(4):
                    ins = t.matmul(RG[0:HS, g * B:(g + 1) * B], lgs[:, g * HS:(g + 1) * HS], gT[:, :], start=False,
                                   stop=(g == 3))
                ins.then_inc(s["rg_rdy"], 1)
                locations(range(6, 16)).then_inc(s["loc_rdy"], 1)
            t.wait_ge(s["ghist_rdy"], L + 1)
            t.wait_ge(s["shist_rdy"], L)
            for n in range(2):
                t.matmul(bank[2 + n][0:HS, :], lgyT[:, :], ghist[:, n * 32:(n + 1) * 32, :], start=True, stop=False)
                t.matmul(bank[2 + n][0:HS, :], lsyT[:, :], shist[:, n * 32:(n + 1) * 32, :], start=False,
                         stop=True).then_inc(s["yg_mm"], 1)
            for i in range(NT):
                t.wait_ge(s["yg_rdy"], i // 4 + 1)
                if i >= 2:
                    t.wait_ge(s["x1_rdy"], i - 1)
                t.matmul(bank[i % 2][:, :], yg[:, i * P:(i + 1) * P], yyT[:, :], start=True, stop=True).then_inc(s["y_mm"], 1)

            def mixture(m):
                mo = MOES[m]
                I, IC, K, NB = mo.I, mo.IC, mo.K, mo.NB
                q = lambda n: s[f"{mo.tag}_{n}"]
                t.wait_ge(s["tr_used"], (2 * m + 2) * NT)
                for i in range(NT):
                    for c in range(HC):
                        ins = t.matmul(bank[6][:, i * E:(i + 1) * E], hidT[:, c, i * P:(i + 1) * P], gw[:, m, c, :],
                                       start=(c == 0), stop=(c == HC - 1))
                ins.then_inc(q("logit_mm"), 1)

                def sh_in(n):
                    h, i, p_ = n // NT, n % NT, n % 2
                    t.wait_ge(q("sw_in"), 32 * mo.shared)
                    if n >= 2:
                        t.wait_ge(q("sh_z"), n - 1)
                    for c in range(HC):
                        ins = t.matmul(bank[p_][:, :], hidT[:, c, i * P:(i + 1) * P], wbuf1[h][:, c, :], start=(c == 0),
                                       stop=(c == HC - 1))
                    ins.then_inc(q("sh_mm"), 1)

                def sh_turn(n):
                    t.wait_ge(q("sh_z"), n + 1)
                    if n >= 1:
                        t.wait_ge(q("sh_ztr"), n)
                    for c in range(2):
                        ins = t.transpose(bank[2][:, c * P:(c + 1) * P], zb[n % 2][:, c * P:(c + 1) * P], ident)
                    ins.then_inc(q("sh_zt"), 1)

                def sh_out(n):
                    t.wait_ge(q("sh_ztr"), n + 1)
                    if n >= 2:
                        t.wait_ge(q("sh_x"), n - 1)
                    for c in range(2):
                        ins = t.matmul(bank[3 + n % 2][:, :], zT[n % 2][:, c, :], wbuf2[n // NT][:, c, :], start=(c == 0),
                                       stop=(c == 1))
                    ins.then_inc(q("sh_o"), 1)

                t.wait_ge(q("route_oh"), 1)
                rhs = msum[:, :, :].rearrange("p i e -> p (i e)")
                t.matmul(bank[7][:, 0:NT * E], cn("before"), rhs, start=True, stop=True)
                t.matmul(bank[7][:, NT * E:2 * NT * E], cn("ones"), rhs, start=True, stop=True).then_inc(q("pos_mm"), 1)
                for n in range(NT * K):
                    t.wait_ge(q("hot_rdy"), n + 1)
                    t.matmul(bank[6][:, 0:2 * NB], lowhot[n % 4][:, :], highhot[n % 4][:, :, 0:NB], start=(n == 0),
                             stop=(n == NT * K - 1)).then_inc(q("hot_mm"), 1)
                N = NT * mo.shared
                for n in range(N + 1):
                    if n >= 1:
                        sh_turn(n - 1)
                    if n < N:
                        sh_in(n)
                    if n >= 1:
                        sh_out(n - 1)

                def turn(b):
                    t.wait_ge(q(f"xg_in{b.par}"), 16 * (b.h + 1))
                    for c in range(HC):
                        ins = t.transpose(bank[b.par][:, c * P:(c + 1) * P], xg[b.par][:, c * P:(c + 1) * P], ident)
                    ins.then_inc(q("xt_mm"), 1)

                def inner(b):
                    t.wait_ge(q(f"w_in{b.slot}"), 32 * (b.q + 1))
                    t.wait_ge(q("xt_rdy"), b.n + 1)
                    for c in range(HC):
                        ins = t.matmul(bank[2 + b.par][:, 0:2 * I], xgT[b.par][:, c, :], wbuf1[b.slot][:, c, 0:2 * I], start=(c == 0),
                                       stop=(c == HC - 1))
                    ins.then_inc(q("h_mm"), 1)

                def zturn(b):
                    t.wait_ge(q("z_rdy"), b.n + 1)
                    for c in range(IC):
                        ins = t.transpose(bank[4][:, c * P:(c + 1) * P], zb[b.par][:, c * P:(c + 1) * P], ident)
                    ins.then_inc(q("zt_mm"), 1)

                def outer(b):
                    t.wait_ge(q("zt_rdy"), b.n + 1)
                    t.wait_ge(q("ob_rdy"), b.n + 1)
                    for c in range(IC):
                        ins = t.matmul(bank[5][:, :], zT[b.par][:, c, :], wbuf2[b.slot][:, c, :], start=(c == 0), stop=(c == IC - 1))
                    ins.then_inc(q("o_mm"), 1)

                def step(b, first=False, last=False):
                    if not last:
                        turn(b.next())
                    if not first:
                        zturn(b.next(-1))
                    inner(b)
                    if not first:
                        outer(b.next(-1))

                t.sem_inc(q("xt_mm"), 2)
                t.sem_inc(q("o_mm"), 4)
                turn(Turn(0, 0))
                step(Turn(0, 0), first=True)
                with t.Fori(0, (NB - 3) // 4) as j:
                    for c_ in range(1, 5):
                        step(Turn(j, c_))
                step(Turn(0, NB - 2))
                step(Turn(0, NB - 1), last=True)
                zturn(Turn(0, NB - 1))
                outer(Turn(0, NB - 1))

            def attention():
                def scores(n, par, bpar, b, rp):
                    t.wait_ge(s["qkv_rdy"], b + 1)
                    t.matmul(bank[par][:, :], qb[bpar][:, rp * P:(rp + 1) * P], kb[bpar][:, :, :], start=True,
                             stop=True).then_inc(s["as_mm"], 1)

                def turn(n, par):
                    t.wait_ge(s["aexp_rdy"], n + 3)
                    for c in range(4):
                        ins = t.transpose(bank[2 + par][:, c * P:(c + 1) * P], ap_[par][:, c * P:(c + 1) * P], ident)
                    ins.then_inc(s["at_mm"], 1)

                def values(n, par, bpar):
                    t.wait_ge(s["aT_rdy"], n + 1)
                    t.wait_ge(s["ao_used"], 2 * n + 2)
                    for c in range(4):
                        t.matmul(bank[4 + par][32 * c:32 * c + 32, 0:P], vb[bpar][:, 32 * c:32 * c + 32], aT[par][:, c, :],
                                 start=True, stop=True)
                    for c in range(4):
                        ins = t.matmul(bank[4 + par][32 * c:32 * c + 32, P:2 * P], cn("vmask")[:, 0:32], aT[par][:, c, :],
                                       start=True, stop=True)
                    ins.then_inc(s["ao_mm"], 1)

                def step(n, q_, b, bq, scr=True, trn=True, val=True):
                    if scr:
                        scores(n, q_ % 2, bq % 2, b, q_ % 2)
                    if trn:
                        turn(n - 1, (q_ + 1) % 2)
                    if val:
                        values(n - 2, q_ % 2, (bq + 1) % 2)

                N = 2 * B
                t.sem_inc(s["ao_mm"], 4)
                t.wait_ge(s["tr_used"], 3 * NT)
                for n in range(2):
                    step(n, n, 0, 0, trn=n >= 1, val=False)
                with t.Fori(0, (N - 4) // 4) as j:
                    for q_ in range(4):
                        step(4 * j + 2 + q_, q_, 2 * j + 1 + q_ // 2, 1 + q_ // 2)
                for n in range(N - 2, N + 2):
                    step(n, n, n // 2, n // 2, scr=n < N, trn=n <= N)
                t.wait_ge(s["ao_used"], 2 * N + 4)
                for i in range(NT):
                    if i >= 2:
                        t.wait_ge(s["att_x"], i - 1)
                    for r in range(R):
                        ins = t.transpose(bank[i % 2][:, r * P:(r + 1) * P], attT[:, r, i * P:(i + 1) * P], ident)
                    ins.then_inc(s["attb_mm"], 1)

            turn_hidden(2)
            mixture(0)
            turn_hidden(3)
            attention()
            turn_hidden(4)
            mixture(1)


def up_layout(w):
    n, rows, _ = w.shape
    return w.reshape(n, rows, HC, P).transpose(0, 3, 2, 1)


def down_layout(w):
    n, _, inner = w.shape
    return w.reshape(n, H, inner // P, P).transpose(0, 3, 2, 1)


def kernel(**inp):
    import concourse.bacc as bacc
    from concourse.bass_utils import run_bass_kernel_spmd

    v = {k: np.asarray(x) for k, x in inp.items()}
    ctxa = v["ctx_1024"]
    arrays = {
        "const": constants()[0],
        "x": v["x"].transpose(1, 0, 2).reshape(NTOK, H),
        "ctxT": ctxa.transpose(2, 1, 0),
        "ctxP": ctxa.reshape(2, 8, T, D).transpose(0, 2, 1, 3).reshape(P, 8, D),
        "lens": v["_lenS2"].reshape(B, 1),
        "lysT": v["L0_xattn_L_ys"].T.reshape(HC, P, 4 * HS).transpose(1, 0, 2),
        "lssT": v["L0_xattn_L_ss"].T,
        "lgsT": v["L0_xattn_L_gs_w"].T,
        "gsb": v["L0_xattn_L_gs_b"].reshape(4, HS).T,
        "wasT": v["L0_xattn_Wa_s"].T,
        "wahT": v["L0_xattn_Wa_h"].T,
        "ba": v["L0_xattn_ba"].reshape(A, 1),
        "convw": v["L0_xattn_conv_w"].reshape(FCH, KW),
        "wafT": v["L0_xattn_Wa_f"].T,
        "va": v["L0_xattn_va"].reshape(A, 1),
        "lgyT": v["L0_xattn_L_gy_w"].T,
        "lsyT": v["L0_xattn_L_sy"].T,
        "gyb": v["L0_xattn_L_gy_b"].reshape(HS, 1),
        "yyT": np.concatenate([v["L0_xattn_L_yy_w"].T, v["L0_xattn_L_yy_b"].reshape(1, H)], 0),
        "gw": np.stack([v["L0_ffn_gate_w"], v["L1_ffn_gate_w"]]).reshape(2, E, HC, P).transpose(3, 0, 2, 1),
        "bias0": np.broadcast_to(v["L0_ffn_bias"].reshape(1, E), (P, E)),
        "amask": v["mask_SxS2_ff0"],
        "ctxD": ctxa.transpose(1, 0, 2),
        "w1_0": up_layout(np.concatenate([v["L0_ffn_Wg"], v["L0_ffn_Wu"]], 1)),
        "w2_0": down_layout(v["L0_ffn_Wd"]),
        "s1_0": up_layout(np.concatenate([v["L0_ffn_Sg"], v["L0_ffn_Su"]], 0)[None]),
        "s2_0": down_layout(v["L0_ffn_Sd"][None]),
        "w1_1": up_layout(v["L1_ffn_w_gate_up"]),
        "w2_1": down_layout(v["L1_ffn_w_down"]),
        "s1_1": up_layout(v["L1_ffn_shared_w_gate_up"].reshape(2, 2, 256, H).transpose(1, 0, 2, 3).reshape(2, 512, H)),
        "s2_1": down_layout(v["L1_ffn_shared_w_down"].reshape(H, 2, 256).transpose(1, 0, 2)),
        "gg": np.broadcast_to(np.concatenate([v["g_xattn"], v["g_ffn"]]), (P, 4)),
    }
    nc = bacc.Bacc("TRN2", target_bir_lowering=False, num_devices=1)
    arrays = {k: np.ascontiguousarray(x) for k, x in arrays.items()}
    aps = {k: nc.dram_tensor("in_" + k, list(x.shape), mybir.dt.from_np(x.dtype), kind="ExternalInput").ap()
           for k, x in arrays.items()}
    out = nc.dram_tensor("out_0", [NTOK, H], F32, kind="ExternalOutput").ap()
    build(nc, aps, out, 0)
    r = run_bass_kernel_spmd(nc, [{"in_" + k: x for k, x in arrays.items()}], core_ids=[0])
    return r.results[0]["out_0"].reshape(L, B, H).transpose(1, 0, 2)
```

```python
from contextlib import ExitStack

import numpy as np

import concourse.bass as bass
from concourse import mybir

ALU = mybir.AluOpType
ACT = mybir.ActivationFunctionType
AX = mybir.AxisListType
F32 = mybir.dt.float32
F16 = mybir.dt.float16
BF16 = mybir.dt.bfloat16
I32 = mybir.dt.int32
U32 = mybir.dt.uint32

P = 128
B, L, H = 16, 64, 512
T, D, HS = 64, 128, 64
A, FCH, KW = 64, 10, 101
NTOK = B * L
NT = NTOK // P
HC = H // P
PAD = 13
KWP = KW + 2 * PAD
NU = T // 2
GROUPS = [(0, 12), (12, 18), (18, 32)]
CHUNKS = [(0, 6), (6, 12), (12, 18), (18, 25), (25, 32)]
E = 16
G, R, HD = 8, 4, 16
EPS = 1e-5
PSCALE = 1024.0


class Moe:

    def __init__(self, tag, inter, top, shared):
        self.tag, self.I, self.K, self.shared = tag, inter, top, shared
        self.IC = inter // P
        self.NB = NTOK * top // P + E - 1
        assert self.NB % 4 == 3


class Turn:

    def __init__(self, j, c):
        self.j, self.c = j, c
        self.par, self.slot = c % 2, c % 4
        self.n = 4 * j + c
        self.h = 2 * j + c // 2
        self.q = j + c // 4

    def next(self, d=1):
        return Turn(self.j, self.c + d)


MOES = [Moe("f0", 256, 4, 1), Moe("f1", 128, 2, 2)]
NEG = -1e30


def constants():
    p = np.arange(P)
    cols = {
        "ident": np.eye(P),
        "dmask": (p[:, None] // B == np.arange(8)[None, :]),
        "bsel": (p[:, None] % B == np.arange(B)[None, :]),
        "tcount": np.broadcast_to(np.arange(T)[None, :], (P, T)),
        "half": np.full((P, 2 * NT), -0.5),
        "ones": np.ones((P, P)),
        "before": (p[:, None] < p[None, :]),
        "iota": np.broadcast_to(p[None, :], (P, P)),
        "prow": p[:, None],
        "tri": np.broadcast_to((np.arange(E)[None, :] < np.arange(E)[:, None]).reshape(1, E * E), (P, E * E)),
        "gmask": 0.25 * (p[:, None] // HD == np.arange(G)[None, :]),
        "vmask": (p[:, None] // T == (np.arange(P)[None, :] // HD) % 2),
    }
    where, parts, at = {}, [], 0
    for name, c in cols.items():
        c = np.asarray(c, np.float32)
        where[name] = (at, c.shape[1])
        parts.append(c)
        at += c.shape[1]
    return np.ascontiguousarray(np.concatenate(parts, 1)), where


def build(nc, a, out, stage):
    _, where = constants()
    with ExitStack() as ctx:
        def sb(name, shape, dt=F32):
            return ctx.enter_context(nc.sbuf_tensor(name, shape, dt))

        def ps(name, shape=(P, 512)):
            return ctx.enter_context(nc.psum_tensor(name, list(shape), F32))

        def sem(name):
            return ctx.enter_context(nc.semaphore(name))

        bank = [ps(f"bank{i}") for i in range(8)]

        const = sb("const", [P, sum(n for _, n in where.values())])

        def cn(name, rows=P):
            at, n = where[name]
            return const[0:rows, at:at + n]

        ident = cn("ident")
        xres = sb("xres", [P, NT, H])
        hid = sb("hid", [P, NT, H])
        hidT = sb("hidT", [P, HC, NTOK])
        stats = sb("stats", [P, NT, 6])
        mv = sb("mv", [P, NT, 2])
        vareps = sb("vareps", [P, NT])
        rstd = sb("rstd", [P, NT])
        gates_g = sb("gates_g", [P, 4])

        ctxT = sb("ctxT", [D, T, B])
        ctxP = sb("ctxP", [P, 8, D])
        lens_i = sb("lens_i", [B, 1], I32)
        lens_f = sb("lens_f", [B, 1])
        maskb = sb("maskb", [B, T])
        lys = sb("lys", [P, HC, 4 * HS])
        lss = sb("lss", [HS, 4 * HS])
        lgs = sb("lgs", [D, 4 * HS])
        gsb = sb("gsb", [P, 4])
        wasT = sb("wasT", [HS, 2, A])
        wahT = sb("wahT", [D, A])
        bacol = sb("bacol", [P, 1])
        convp = sb("convp", [FCH, KWP])
        wafT = sb("wafT", [FCH, A])
        va2 = sb("va2", [P, 2])
        lgyT = sb("lgyT", [D, HS])
        lsyT = sb("lsyT", [HS, HS])
        gyb = sb("gyb", [HS, 1])
        yyT = sb("yyT", [HS + 1, H])

        comb = sb("comb", [P, A])
        region = sb("region", [P, 3 * 4096])
        tr_f = region[:, 4096:8192]
        toep_w = region[:, 0:4096]
        toepA = toep_w[:, 0:2048].bitcast(BF16)
        toepB = toep_w[:, 2048:4096].bitcast(BF16)
        ctx3 = sb("ctx3", [P, 3, 8 * D], BF16)
        ctxr = sb("ctxr", [P, 8 * D])
        comb_d = nc.dram_tensor("comb_d", [P + T, A], F32).ap()
        enc = sb("enc", [P, NU * B])
        pre = region[0:HS, 8192:12288].rearrange("p (l g b) -> p l g b", l=L, g=4)
        ghist = sb("ghist", [D, L, B])
        shist = sb("shist", [HS, L + 1, B])

        prebuf = sb("prebuf", [HS, 4, B])
        s2 = sb("s2", [HS, B])
        c2 = sb("c2", [HS, B])
        al2 = sb("al2", [P, 2, B], F16)
        encloc = sb("encloc", [P, NU * B])
        pact = sb("pact", [P, NU * B])
        th = sb("th", [P, NU * B])
        nmax = sb("nmax", [B, 1])
        psum_e = sb("psum_e", [B, 1])
        prob = sb("prob", [B, T])
        rinv = sb("rinv", [B, 1])
        pn = sb("pn", [P, 2 * T])
        ae = sb("ae", [P, 2, B], F16)
        gT = sb("gT", [D, B])
        tg = sb("tg", [HS, 4, B])
        la = sb("la", [HS, B])
        lb = sb("lb", [HS, B])
        tc = sb("tc", [HS, B])
        yg = sb("yg", [HS + 1, NTOK])

        gw = sb("gw", [P, 2, HC, E])
        bias0 = sb("bias0", [P, E])
        wbuf1 = [region[:, i * 3072:i * 3072 + 2048].rearrange("p (c n) -> p c n", c=HC) for i in range(4)]
        wbuf2 = [region[:, i * 3072 + 2048:(i + 1) * 3072].rearrange("p (c n) -> p c n", c=2) for i in range(4)]
        xg = [sb(f"xg{i}", [P, H]) for i in range(2)]
        xgT = [sb(f"xgT{i}", [P, HC, P]) for i in range(2)]
        gth = [sb(f"gth{i}", [P, 256]) for i in range(2)]
        ga = [sb(f"ga{i}", [P, 256]) for i in range(2)]
        zb = [sb(f"zb{i}", [P, 256]) for i in range(2)]
        zT = [sb(f"zT{i}", [P, 2, P]) for i in range(2)]
        ob = [sb(f"ob{i}", [P, H]) for i in range(2)]
        NYG = 8
        yrow = [hidT[:, i // 2, (i % 2) * H:(i % 2 + 1) * H] for i in range(NYG)]
        NBM = MOES[0].NB
        KM = MOES[0].K
        sc = sb("sc", [P, NT, E])
        sc2 = sb("sc2", [P, NT, E])
        smax = sb("smax", [P, NT])
        top8 = sb("top8", [P, NT, 8])
        idx8 = sb("idx8", [P, NT, 8], U32)
        idxf = sb("idxf", [P, NT * KM])
        onehot = sb("onehot", [P, NT * KM, E])
        ohs = sb("ohs", [P, NT * KM, E])
        msum = sb("msum", [P, NT, E])
        cum = sb("cum", [P, NT, E])
        count = sb("count", [P, E])
        nblk_i = sb("nblk_i", [P, E], I32)
        nblk_j = sb("nblk_j", [P, E], I32)
        nblk = sb("nblk", [P, E])
        trib = sb("trib", [P, E, E])
        bstart = sb("bstart", [P, E])
        bend = sb("bend", [P, E])
        place = sb("place", [P, NT, E])
        slotf = sb("slotf", [P, NT * KM])
        sloti = sb("sloti", [P, NT * KM], I32)
        slow_i = sb("slow_i", [P, NT * KM], I32)
        shigh_i = sb("shigh_i", [P, NT * KM], I32)
        slow = sb("slow", [P, NT * KM])
        shigh = sb("shigh", [P, NT * KM])
        wsum = sb("wsum", [P, NT])
        winv = sb("winv", [P, NT])
        wk = sb("wk", [P, NT, KM])
        ecmp = sb("ecmp", [P, NBM, E])
        ebf = sb("ebf", [P, NBM])
        ebi = sb("ebi", [P, NBM], I32)
        lowhot = region[:, 6144:8192].bitcast(BF16).rearrange("p (n x) -> p n x", n=NT * KM)
        highhot = region[:, 8192:8192 + NT * KM * NBM].bitcast(BF16).rearrange("p (n r x) -> p n r x", n=NT * KM, r=2)
        tlf = sb("tlf", [P, NBM])
        tli = sb("tli", [P, NBM], I32)
        halfg = sb("halfg", [P, 4])
        hd = [nc.dram_tensor(f"hid_d{m}", [NTOK, H], F32).ap() for m in range(2)]
        yd = [nc.dram_tensor(f"y_d{m}", [mo.NB * P, H], F32).ap() for m, mo in enumerate(MOES)]

        amask = sb("amask", [P, T])
        ctxD = sb("ctxD", [P, B, D])
        qb = [sb(f"qb{i}", [P, R * L]) for i in range(2)]
        kb = [sb(f"kb{i}", [P, G, T]) for i in range(2)]
        vb = [sb(f"vb{i}", [P, P]) for i in range(2)]
        sm = [sb(f"sm{i}", [P, G, T]) for i in range(2)]
        amax = [sb(f"amax{i}", [P, G]) for i in range(2)]
        ap_ = [encloc, pact]
        aT = [x[:, :].rearrange("p (c t) -> p c t", c=4) for x in (enc, th)]
        arec = [sb(f"arec{i}", [P, P]) for i in range(2)]
        attT = region[:, 8192:12288].rearrange("p (r t) -> p r t", r=R)

        def loc(u0, u1):
            n = max(n for n in range(3) if u0 >= GROUPS[n][0])
            return bank[(0, 1, 7)[n]][:, (u0 - GROUPS[n][0]) * B:(u1 - GROUPS[n][0]) * B]

        SW, RO, EB, AT, GT, RG = bank[4][:, 256:256 + B], bank[2], bank[3], bank[4], bank[5], bank[6]

        def gate(g):
            return RO[0:HS, 0:B] if g == 3 else RG[0:HS, g * B:(g + 1) * B]

        names = """x_in e_in w_in l_in dchain achain  rstd_rdy hid_rdy tr_rdy tr_used pre_mm pre_used toep_mm comb_rdy comb_st toep_in toep_hi toep_rest ctx_hi ctx_rest 
        enc_mm enc_used w_ready init_rdy loc_rdy sw_rdy pact_rdy th_rdy al_rdy eb_rdy nmax_rdy p_rdy r_rdy at_rdy ae_rdy
        alT_rdy gt_rdy gT_rdy rg_rdy tg_rdy c2_rdy tc_rdy s_rdy prebuf_rdy ghist_rdy shist_rdy pb_free
        yg_mm yg_rdy y_mm x1_rdy out_done stat_rdy 
        qk_rdy v_rdy as_mm  smx_rdy am_rdy aexp_rdy at_mm aT_rdy ao_mm ao_used attb_mm att_x""".split()
        for mo in MOES:
            names += [f"{mo.tag}_{n}" for n in """hid_st logit_mm  act_done exp_in route_oh pos_mm  hot_rdy hot_mm 
            list_rdy eb_rdy w_in0 w_in1 w_in2 w_in3 xg_in0 xg_in1 xt_mm xt_rdy h_mm th_rdy  z_rdy zt_mm zt_rdy o_mm ob_rdy ob_st0 ob_st1
            sw_in sh_mm sh_th sh_z sh_zt sh_ztr sh_o sh_x yg_in0 yg_in1 yg_in2 yg_in3 yg_in4 yg_in5 yg_in6 yg_in7 yg_used""".split()]
        s = {n: sem(n) for n in names}

        block = ctx.enter_context(nc.Block())

        ELOADS = [(const[:, :], a["const"]), (ctxT[:, :, :], a["ctxT"]), (wahT[:, :], a["wahT"]), (bacol[0:A, :], a["ba"]),
                  (bacol[A:P, :], a["ba"]), (wafT[:, :], a["wafT"]), (convp[:, PAD:PAD + KW], a["convw"])]
        WLOADS = [(gsb[0:HS, :], a["gsb"]), (gsb[HS:P, :], a["gsb"]), (lys[:, :, :], a["lysT"]), (ctxP[:, :, :], a["ctxP"]),
                  (lens_i[:, :], a["lens"]), (lss[:, :], a["lssT"]), (lgs[:, :], a["lgsT"]),
                  (wasT[:, 0, :], a["wasT"]), (wasT[:, 1, :], a["wasT"]),
                  (lgyT[:, :], a["lgyT"]), (lsyT[:, :], a["lsyT"]), (gyb[:, :], a["gyb"]), (yyT[:, :], a["yyT"]),
                  (gates_g[:, :], a["gg"]), (gw[:, :, :, :], a["gw"]), (bias0[:, :], a["bias0"]),
                  (va2[0:A, 1:2], a["va"]), (va2[A:P, 0:1], a["va"])]
        LLOADS = [(amask[0:T, :], a["amask"]), (amask[T:P, :], a["amask"]),
                  (ctxD[0:T, :, :], a["ctxD"]), (ctxD[T:P, :, :], a["ctxD"])]
        NE, NW, NL = len(ELOADS), len(WLOADS), len(LLOADS)

        @block.sync
        def _(sp):
            for dst, src in ELOADS[:-1]:
                sp.dma_start(dst, src).then_inc(s["e_in"], 16)
            sp.wait_ge(s["init_rdy"], 1)
            dst, src = ELOADS[-1]
            sp.dma_start(dst, src).then_inc(s["e_in"], 16)
            for i in range(NT):
                sp.dma_start(xres[:, i, :], a["x"][i * P:(i + 1) * P, :]).then_inc(s["x_in"], 16)
            for dst, src in WLOADS:
                sp.dma_start(dst, src).then_inc(s["w_in"], 16)
            sp.wait_ge(s["comb_rdy"], 1)
            sp.dma_start(comb_d[0:KWP, :], comb[0:KWP, :]).then_inc(s["comb_st"], 16)
            sp.wait_ge(s["comb_st"], 16)
            windows = bass.AP(comb_d.tensor, 0, [[A, T], [1, T * A]])
            for half in range(2):
                sp.dma_start(tr_f[half * T:(half + 1) * T, :], windows).then_inc(s["toep_in"], 16)
            for dst, src in LLOADS:
                sp.dma_start(dst, src).then_inc(s["l_in"], 16)

            def mixture(m):
                mo = MOES[m]
                q = lambda n: s[f"{mo.tag}_{n}"]
                for h in range(mo.shared):
                    if m == 0:
                        sp.wait_ge(s["yg_mm"], 1)
                    else:
                        sp.wait_ge(s["f0_o_mm"], 4 + MOES[0].NB)
                    sp.dma_start(wbuf1[h][:, :, :], a[f"s1_{m}"][h]).then_inc(q("sw_in"), 16)
                    sp.dma_start(wbuf2[h][:, :, :], a[f"s2_{m}"][h]).then_inc(q("sw_in"), 16)
                for i in range(NT):
                    sp.wait_ge(s["hid_rdy"], (2 * m + 1) * NT + i + 1)
                    sp.dma_start(hd[m][i * P:(i + 1) * P, :], hid[:, i, :]).then_inc(q("hid_st"), 16)
                sp.wait_ge(q("eb_rdy"), 1)
                sp.wait_ge(q("sh_o"), NT * mo.shared)

                def weights(b):
                    sp.wait_ge(q("o_mm"), b.n + 1)
                    e = sp.value_load(ebi[0:1, bass.ds(b.n, 1)], min_val=0, max_val=E - 1)
                    sp.dma_start(wbuf1[b.slot][:, :, 0:2 * mo.I], a[f"w1_{m}"][bass.ds(e, 1)].rearrange("x p c n -> (x p) c n")).then_inc(q(f"w_in{b.slot}"), 16)
                    sp.dma_start(wbuf2[b.slot][:, 0:mo.IC, :], a[f"w2_{m}"][bass.ds(e, 1)].rearrange("x p c n -> (x p) c n")).then_inc(q(f"w_in{b.slot}"), 16)

                def store(b):
                    sp.wait_ge(q("ob_rdy"), b.n + 2)
                    sp.dma_start(yd[m][bass.ds(b.n * P, P), :], ob[b.par][:, :]).then_inc(q(f"ob_st{b.par}"), 16)

                def step(b, more=True):
                    if more:
                        weights(b.next(3))
                    store(b)

                for c_ in range(3):
                    weights(Turn(0, c_))
                step(Turn(0, 0))
                with sp.Fori(0, (mo.NB - 7) // 4) as j:
                    for c_ in range(1, 5):
                        step(Turn(j, c_))
                for n in range(mo.NB - 6, mo.NB):
                    step(Turn(0, n), more=n + 3 < mo.NB)

            mixture(0)
            mixture(1)
            for i in range(NT):
                sp.wait_ge(s["f1_yg_used"], MOES[1].K * (i + 1))
                sp.dma_start(out[i * P:(i + 1) * P, :], xres[:, i, :]).then_inc(s["out_done"], 16)
            sp.wait_ge(s["out_done"], 16 * NT)

        @block.vector
        def _(v):
            ch = [0]

            def link(ins):
                ch[0] += 1
                ins.then_inc(s["dchain"], 1)
                v.wait_ge(s["dchain"], ch[0])

            v.memset(convp[:, :], 0.0)
            link(v.memset(va2[:, :], 0.0))
            v.memset(s2[:, :], 0.0)
            v.memset(c2[:, :], 0.0)
            v.memset(al2[:, :, :], 0.0)
            v.memset(pn[:, :], 0.0)
            link(v.memset(yg[HS:HS + 1, :], 1.0))
            v.memset(prebuf[:, 0, 0:1], 0.0).then_inc(s["init_rdy"], 1)
            v.memset(ae[:, :, :], 0.0).then_inc(s["alT_rdy"], 1)
            v.memset(prebuf[:, 1, 0:1], 0.0).then_inc(s["s_rdy"], 1)

            def layernorm_stats():
                for i in range(NT):
                    ins = v.bn_stats(stats[:, i, :], xres[:, i, :])
                link(ins)
                for i in range(NT):
                    ins = v.bn_aggr(mv[:, i, :], stats[:, i, :])
                link(ins)
                v.tensor_scalar(vareps[:, :], mv[:, :, 1], EPS, None, ALU.add).then_inc(s["stat_rdy"], 1)

            def layernorm_apply(n):
                v.wait_ge(s["rstd_rdy"], n)
                if n >= 3:
                    v.wait_ge(s["f0_hid_st"], 16 * NT)
                for i in range(NT):
                    src, dst = xres[:, i, :], hid[:, i, :]
                    if n == 3:
                        src = src.rearrange("p (g r d) -> p g r d", g=G, r=R)
                        dst = dst.rearrange("p (r g d) -> p g r d", g=G, r=R)
                    v.tensor_scalar(dst, src, mv[:, i, 0:1], rstd[:, i:i + 1], ALU.subtract,
                                    ALU.mult).then_inc(s["hid_rdy"], 1)

            def transposed(n):
                for i in range(NT):
                    v.wait_ge(s["tr_rdy"], (n - 1) * NT + i + 1)
                    src = bank[i % 2][:, :].rearrange("p (c t) -> p c t", c=HC)
                    if n == 3:
                        dst = hidT[:, :, :].rearrange("p c t -> p (c t)").rearrange(
                            "p (b c l) -> p c l b", b=B, c=HC)[:, :, i * 8:(i + 1) * 8, :]
                        for c in range(HC):
                            ins = v.tensor_copy(dst[:, c], src[:, c].rearrange("p (l b) -> p l b", b=B))
                        ins.then_inc(s["tr_used"], 1)
                    else:
                        v.tensor_copy(hidT[:, :, i * P:(i + 1) * P], src).then_inc(s["tr_used"], 1)

            v.wait_ge(s["e_in"], 16 * NE)
            v.wait_ge(s["toep_mm"], 1)
            v.tensor_scalar(comb[0:KWP, :], bank[3][0:KWP, 0:A], 1.0 / PSCALE, None, ALU.mult).then_inc(s["comb_rdy"], 1)
            v.wait_ge(s["enc_mm"], 1)
            v.tensor_scalar(enc[:, :], bank[2][:, :], bacol[:, 0:1], None, ALU.add).then_inc(s["enc_used"], 1)
            v.wait_ge(s["x_in"], 16 * NT)
            layernorm_stats()
            layernorm_apply(1)
            transposed(1)
            v.wait_ge(s["w_in"], 16 * NW)
            v.tensor_scalar(wasT[:, :, :], wasT[:, :, :], 0.5, None, ALU.mult)
            v.tensor_scalar(lsyT[:, :], lsyT[:, :], 0.5, None, ALU.mult)
            v.tensor_scalar(lgs[:, 2 * HS:3 * HS], lgs[:, 2 * HS:3 * HS], 2.0, None, ALU.mult)
            v.tensor_copy(lens_f[:, :], lens_i[:, :])
            for g in (0, 1, 3):
                v.tensor_scalar(lss[:, g * HS:(g + 1) * HS], lss[:, g * HS:(g + 1) * HS], 0.5, None, ALU.mult)
            link(v.memset(nmax[:, :], 0.0))
            v.tensor_scalar(maskb[:, :], cn("tcount", B), lens_f[:, 0:1], NEG, ALU.is_ge, ALU.mult).then_inc(s["w_ready"], 1)
            cflat = ctxP[:, :, :].rearrange("p j d -> p (j d)")
            v.tensor_scalar(cflat, cflat, 1.0 / PSCALE, None, ALU.mult).then_inc(s["ctx_rest"], 1)
            v.wait_ge(s["toep_hi"], 1)
            v.tensor_tensor(tr_f[T:P, :], tr_f[T:P, :], toepA[T:P, :], ALU.subtract).then_inc(s["toep_rest"], 1)
            v.wait_ge(s["ctx_hi"], 1)
            v.tensor_tensor(ctxr[:, :], cflat, ctx3[:, 0, :], ALU.subtract).then_inc(s["ctx_rest"], 1)
            for n in range(4):
                gp, hf = n // 2, n % 2
                v.wait_ge(s["pre_mm"], n + 1)
                for h in range(2):
                    g, rows = 2 * gp + h, slice(h * HS, (h + 1) * HS)
                    ins = v.tensor_scalar(pre[:, hf * 32:(hf + 1) * 32, g, :],
                                          bank[4 + n][rows, :].rearrange("p (l b) -> p l b", b=B), gsb[rows, g:g + 1],
                                          2.0 if g == 2 else 1.0, ALU.add, ALU.mult)
                ins.then_inc(s["pre_used"], 1)
                if n == 0:
                    v.wait_ge(s["ctx_hi"], 2)
                    v.tensor_tensor(ctx3[:, 2, :], ctxr[:, :], ctx3[:, 1, :], ALU.subtract).then_inc(s["ctx_rest"], 1)
                if n == 1:
                    v.wait_ge(s["toep_hi"], 2)
                    v.tensor_tensor(toepB[T:P, :], tr_f[T:P, :], toepA[T:P, :], ALU.subtract).then_inc(s["toep_rest"], 1)
            def encoder_location(n):
                u0, u1 = GROUPS[n]
                return v.tensor_tensor(encloc[:, u0 * B:u1 * B], enc[:, u0 * B:u1 * B], loc(u0, u1), ALU.add)

            v.wait_ge(s["loc_rdy"], 2)
            link(encoder_location(0))
            link(encoder_location(1))
            base = ch[0]
            UB = GROUPS[2][0]
            PER = 5
            with v.Fori(0, L) as l:
                k = [0]

                def clink(ins):
                    k[0] += 1
                    ins.then_inc(s["dchain"], 1)
                    v.wait_ge(s["dchain"], base + l * PER + k[0])

                v.wait_ge(s["sw_rdy"], l + 1)
                for n, (u0, u1) in enumerate(CHUNKS):
                    if u0 == UB:
                        v.wait_ge(s["loc_rdy"], 3 * l + 3)
                        clink(encoder_location(2))
                    sl = slice(u0 * B, u1 * B)
                    v.tensor_tensor(pact[:, sl].rearrange("p (u b) -> p u b", b=B),
                                    encloc[:, sl].rearrange("p (u b) -> p u b", b=B),
                                    SW.unsqueeze(1).broadcast_to([P, u1 - u0, B]), ALU.add).then_inc(s["pact_rdy"], 1)
                v.wait_ge(s["eb_rdy"], l + 1)
                v.tensor_reduce(nmax[:, :], EB[0:B, 0:T], AX.X, ALU.max, negate=True).then_inc(s["nmax_rdy"], 1)
                v.wait_ge(s["p_rdy"], l + 1)
                clink(v.reciprocal(rinv[:, :], psum_e[:, :]))
                v.tensor_scalar(pn[0:B, :].rearrange("p (r t) -> p r t", r=2), prob[:, :].unsqueeze(1).broadcast_to([B, 2, T]),
                                rinv[:, 0:1], PSCALE, ALU.mult, ALU.mult).then_inc(s["r_rdy"], 1)
                v.wait_ge(s["at_rdy"], l + 1)
                v.tensor_copy(al2[:, 0, :], AT[:, 0:B]).then_inc(s["al_rdy"], 1)
                halves = [(slice(h * T, (h + 1) * T), slice(h * 8, (h + 1) * 8)) for h in range(2)]
                for r_, b_ in halves:
                    v.tensor_copy(ae[r_, 0, b_], AT[r_, b_])
                v.wait_ge(s["al_rdy"], 2 * l + 1)
                for r_, b_ in halves:
                    ins = v.tensor_tensor(ae[r_, 1, b_], AT[r_, b_], al2[r_, 0, b_], ALU.subtract)
                ins.then_inc(s["ae_rdy"], 1)
                v.tensor_tensor(al2[:, 1, :], AT[:, 0:B], al2[:, 0, :], ALU.subtract).then_inc(s["al_rdy"], 1)
                v.wait_ge(s["gt_rdy"], l + 1)
                v.wait_ge(s["ghist_rdy"], l + 1)
                v.tensor_reduce(gT[:, :], GT[:, 0:2 * B].rearrange("p (s b) -> p b s", s=2), AX.X,
                                ALU.add).then_inc(s["gT_rdy"], 1)
                v.wait_ge(s["loc_rdy"], 3 * l + 4)
                clink(encoder_location(0))
                v.wait_ge(s["tg_rdy"], 2 * l + 1)
                v.scalar_tensor_tensor(la[:, :], tg[:, 0, :], 1.0, tg[:, 2, :], ALU.add, ALU.mult)
                clink(v.scalar_tensor_tensor(lb[:, :], tg[:, 1, :], 1.0, c2[:, :], ALU.add, ALU.mult))
                v.scalar_tensor_tensor(c2[:, :], lb[:, :], 0.5, la[:, :], ALU.mult, ALU.add).then_inc(s["c2_rdy"], 1)
                v.wait_ge(s["loc_rdy"], 3 * l + 5)
                clink(encoder_location(1))
                v.wait_ge(s["tg_rdy"], 2 * l + 2)
                v.wait_ge(s["tc_rdy"], l + 1)
                v.wait_ge(s["shist_rdy"], l + 1)
                v.scalar_tensor_tensor(s2[:, :], tg[:, 3, :], 1.0, tc[:, :], ALU.add, ALU.mult).then_inc(s["s_rdy"], 1)
                assert k[0] == PER
            ch[0] += L * PER
            for i in range(NT):
                v.wait_ge(s["y_mm"], i + 1)
                ins = v.scalar_tensor_tensor(xres[:, i, :], bank[i % 2][:, :], gates_g[:, 0:1], xres[:, i, :], ALU.mult,
                                             ALU.add)
                ins.then_inc(s["x1_rdy"], 1)
            v.wait_ge(s["x1_rdy"], NT)
            link(v.tensor_scalar(halfg[:, :], gates_g[:, :], 0.5, None, ALU.mult))

            def shared_step(m, n):
                mo = MOES[m]
                q = lambda n: s[f"{mo.tag}_{n}"]
                p_, o_ = n % 2, (n - 1) % 2
                if n > 0:
                    v.wait_ge(q("sh_zt"), n)
                    v.tensor_copy(zT[o_][:, :, :], bank[2][:, 0:256].rearrange("p (c t) -> p c t", c=2)).then_inc(q("sh_ztr"), 1)
                if n < NT * mo.shared:
                    v.wait_ge(q("sh_th"), n + 1)
                    link(v.scalar_tensor_tensor(ga[p_][:, :], gth[p_][:, :], 1.0, bank[p_][:, 0:256], ALU.add, ALU.mult))
                    v.tensor_tensor(zb[p_][:, :], ga[p_][:, :], bank[p_][:, 256:512], ALU.mult).then_inc(q("sh_z"), 1)
                if n > 0:
                    i = (n - 1) % NT
                    v.wait_ge(q("sh_o"), n)
                    if n > NT:
                        v.wait_ge(q("sh_x"), n - NT)
                    v.scalar_tensor_tensor(xres[:, i, :], bank[3 + o_][:, :], halfg[:, 2 + m:3 + m], xres[:, i, :],
                                           ALU.mult, ALU.add).then_inc(q("sh_x"), 1)

            def route(m):
                mo = MOES[m]
                K, NB, NK = mo.K, mo.NB, NT * mo.K
                q = lambda n: s[f"{mo.tag}_{n}"]
                g_ffn = gates_g[:, 2 + m:3 + m]
                if m == 0:
                    v.wait_ge(q("act_done"), 1)
                    link(v.tensor_scalar(sc2[:, :, :], sc[:, :, :], 0.5, 0.5, ALU.mult, ALU.add))
                    link(v.tensor_tensor(sc[:, :, :], sc2[:, :, :], bias0[:, :].unsqueeze(1).broadcast_to([P, NT, E]),
                                         ALU.add))
                else:
                    v.wait_ge(q("logit_mm"), 1)
                    lg = bank[6][:, 0:NT * E].rearrange("p (i e) -> p i e", e=E)
                    link(v.tensor_reduce(smax[:, :], lg, AX.X, ALU.max))
                    v.tensor_tensor(sc2[:, :, :], lg, smax[:, :].unsqueeze(2).broadcast_to([P, NT, E]),
                                    ALU.subtract).then_inc(q("exp_in"), 1)
                    v.wait_ge(q("act_done"), 1)
                    link(v.tensor_reduce(wsum[:, :], sc[:, :, :], AX.X, ALU.add))
                    link(v.reciprocal(winv[:, :], wsum[:, :]))
                    link(v.tensor_tensor(sc[:, :, :], sc[:, :, :], winv[:, :].unsqueeze(2).broadcast_to([P, NT, E]), ALU.mult))
                for i in range(NT):
                    ins = v.max(top8[:, i, :], sc[:, i, :])
                link(ins)
                shared_step(m, 0)
                for i in range(NT):
                    ins = v.max_index(idx8[:, i, :], top8[:, i, :], sc[:, i, :])
                link(ins)
                link(v.tensor_copy(idxf[:, 0:NK].rearrange("p (i k) -> p i k", k=K), idx8[:, :, 0:K]))
                oh = onehot[:, 0:NK, :]
                link(v.tensor_tensor(oh, cn("iota")[:, 0:E].unsqueeze(1).broadcast_to([P, NK, E]),
                                     idxf[:, 0:NK].unsqueeze(2).broadcast_to([P, NK, E]), ALU.is_equal))
                v.tensor_reduce(msum[:, :, :], oh.rearrange("p (i k) e -> p i e k", k=K), AX.X,
                                ALU.add).then_inc(q("route_oh"), 1)
                link(v.tensor_reduce(wsum[:, :], top8[:, :, 0:K], AX.X, ALU.add))
                if m == 0:
                    link(v.tensor_scalar(wsum[:, :], wsum[:, :], 1e-20, None, ALU.add))
                link(v.reciprocal(winv[:, :], wsum[:, :]))
                link(v.tensor_scalar(winv[:, :], winv[:, :], g_ffn, None, ALU.mult))
                link(v.tensor_tensor(wk[:, :, 0:K], top8[:, :, 0:K], winv[:, :].unsqueeze(2).broadcast_to([P, NT, K]), ALU.mult))
                shared_step(m, 1)
                pos = bank[7][:, 0:NT * E].rearrange("p (i e) -> p i e", e=E)
                tot = bank[7][:, NT * E:2 * NT * E].rearrange("p (i e) -> p i e", e=E)
                v.wait_ge(q("pos_mm"), 1)
                link(v.memset(cum[:, 0, :], 0.0))
                for i in range(1, NT):
                    link(v.tensor_tensor(cum[:, i, :], cum[:, i - 1, :], tot[:, i - 1, :], ALU.add))
                link(v.tensor_tensor(count[:, :], cum[:, NT - 1, :], tot[:, NT - 1, :], ALU.add))
                link(v.tensor_scalar(nblk_i[:, :], count[:, :], float(P - 1), None, ALU.add))
                link(v.tensor_scalar(nblk_j[:, :], nblk_i[:, :], 7, None, ALU.arith_shift_right))
                link(v.tensor_copy(nblk[:, :], nblk_j[:, :]))
                link(v.tensor_tensor(trib[:, :, :], nblk[:, :].unsqueeze(1).broadcast_to([P, E, E]),
                                     cn("tri").rearrange("p (a b) -> p a b", a=E), ALU.mult))
                link(v.tensor_reduce(bstart[:, :], trib[:, :, :], AX.X, ALU.add))
                link(v.tensor_tensor(bend[:, :], bstart[:, :], nblk[:, :], ALU.add))
                link(v.tensor_tensor(ecmp[:, 0:NB, :], bend[:, :].unsqueeze(1).broadcast_to([P, NB, E]),
                                     cn("iota")[:, 0:NB].unsqueeze(2).broadcast_to([P, NB, E]), ALU.is_le))
                link(v.tensor_reduce(ebf[:, 0:NB], ecmp[:, 0:NB, :], AX.X, ALU.add))
                v.tensor_scalar(ebi[:, 0:NB], ebf[:, 0:NB], float(E - 1), None, ALU.min).then_inc(q("eb_rdy"), 1)
                shared_step(m, 2)
                link(v.scalar_tensor_tensor(place[:, :, :], bstart[:, :].unsqueeze(1).broadcast_to([P, NT, E]), float(P),
                                            cum[:, :, :], ALU.mult, ALU.add))
                link(v.tensor_tensor(place[:, :, :], place[:, :, :], pos, ALU.add))
                for k in range(K):
                    ins = v.tensor_tensor(ohs[:, 0:NK, :].rearrange("p (i k) e -> p i k e", k=K)[:, :, k, :],
                                          oh.rearrange("p (i k) e -> p i k e", k=K)[:, :, k, :], place[:, :, :], ALU.mult)
                link(ins)
                link(v.tensor_reduce(slotf[:, 0:NK], ohs[:, 0:NK, :], AX.X, ALU.add))
                link(v.tensor_copy(sloti[:, 0:NK], slotf[:, 0:NK]))
                v.tensor_scalar(slow_i[:, 0:NK], sloti[:, 0:NK], P - 1, None, ALU.bitwise_and)
                link(v.tensor_scalar(shigh_i[:, 0:NK], sloti[:, 0:NK], 7, None, ALU.arith_shift_right))
                v.tensor_copy(slow[:, 0:NK], slow_i[:, 0:NK])
                link(v.tensor_copy(shigh[:, 0:NK], shigh_i[:, 0:NK]))
                shared_step(m, 3)
                for n in range(NK):
                    if n in (NK // 4, NK // 2, 3 * NK // 4):
                        shared_step(m, 3 + 4 * n // NK)
                    v.tensor_scalar(lowhot[:, n, :], cn("iota"), slow[:, n:n + 1], None, ALU.is_equal)
                    v.tensor_scalar(highhot[:, n, 0, 0:NB], cn("iota")[:, 0:NB], shigh[:, n:n + 1], cn("prow"),
                                    ALU.is_equal, ALU.mult)
                    v.tensor_scalar(highhot[:, n, 1, 0:NB], cn("iota")[:, 0:NB], shigh[:, n:n + 1], float(n // K),
                                    ALU.is_equal, ALU.mult).then_inc(q("hot_rdy"), 1)
                shared_step(m, 7)
                v.wait_ge(q("hot_mm"), NK)
                link(v.tensor_copy(tlf[:, 0:NB], bank[6][:, 0:NB]))
                v.scalar_tensor_tensor(tli[:, 0:NB], bank[6][:, NB:2 * NB], float(P), tlf[:, 0:NB], ALU.mult,
                                       ALU.add).then_inc(q("list_rdy"), 1)
                for n in range(8, NT * mo.shared + 1):
                    shared_step(m, n)

            def experts(m):
                mo = MOES[m]
                I, IC = mo.I, mo.IC
                q = lambda n: s[f"{mo.tag}_{n}"]
                base = ch[0]

                def inner(b):
                    v.wait_ge(q("th_rdy"), b.n + 1)
                    v.scalar_tensor_tensor(ga[b.par][:, 0:I], gth[b.par][:, 0:I], 1.0, bank[2 + b.par][:, 0:I], ALU.add,
                                           ALU.mult).then_inc(s["dchain"], 1)
                    v.wait_ge(s["dchain"], base + 1 + b.n)
                    v.tensor_tensor(zb[b.par][:, 0:I], ga[b.par][:, 0:I], bank[2 + b.par][:, I:2 * I], ALU.mult).then_inc(q("z_rdy"), 1)

                def outer(b):
                    v.wait_ge(q("zt_mm"), b.n + 1)
                    v.tensor_copy(zT[b.par][:, 0:IC, :], bank[4][:, 0:I].rearrange("p (c t) -> p c t", c=IC)).then_inc(q("zt_rdy"), 1)

                def step(b, first=False):
                    if not first:
                        outer(b.next(-1))
                    inner(b)

                step(Turn(0, 0), first=True)
                with v.Fori(0, (mo.NB - 3) // 4) as j:
                    for c_ in range(1, 5):
                        step(Turn(j, c_))
                step(Turn(0, mo.NB - 2))
                step(Turn(0, mo.NB - 1))
                outer(Turn(0, mo.NB - 1))
                ch[0] += mo.NB

            def combine(m):
                mo = MOES[m]
                q = lambda n: s[f"{mo.tag}_{n}"]
                v.wait_ge(q("sh_x"), NT * mo.shared)
                for n in range(NT * mo.K):
                    i, k = n // mo.K, n % mo.K
                    v.wait_ge(q(f"yg_in{n % NYG}"), 16 * (n // NYG + 1))
                    if k > 0:
                        v.wait_ge(q("yg_used"), n)
                    ins = v.scalar_tensor_tensor(xres[:, i, :], yrow[n % NYG][:, :], wk[:, i, k:k + 1], xres[:, i, :],
                                                 ALU.mult, ALU.add)
                    ins.then_inc(q("yg_used"), 1)
                v.wait_ge(q("yg_used"), NT * mo.K)

            def attention():
                def scores(n, par):
                    v.wait_ge(s["as_mm"], n + 1)
                    v.wait_ge(s["aexp_rdy"], n + 1)
                    sb_ = bank[par][:, :].rearrange("p (g t) -> p g t", g=G)
                    v.tensor_tensor(sm[par][:, :, :], sb_, amask[:, :].unsqueeze(1).broadcast_to([P, G, T]),
                                    ALU.add).then_inc(s["smx_rdy"], 1)
                    v.wait_ge(s["smx_rdy"], n + 1)
                    v.tensor_reduce(amax[par][:, :], sm[par][:, :, :], AX.X, ALU.max, negate=True).then_inc(s["am_rdy"], 1)

                def norm(n, par, b, rp):
                    v.wait_ge(s["ao_mm"], n + 5)
                    v.reciprocal(arec[par][:, :], bank[4 + par][:, P:2 * P]).then_inc(s["ao_used"], 1)
                    v.wait_ge(s["ao_used"], 2 * n + 5)
                    dst = attT[:, :, :].rearrange("p r (l b) -> p b r l", b=B)[:, bass.ds(b, 1), 2 * rp:2 * rp + 2, :]
                    v.scalar_tensor_tensor(dst.rearrange("p x r l -> p (x r) l"), bank[4 + par][:, 0:P].rearrange("p (r l) -> p r l", r=2),
                                           gates_g[:, 1:2], arec[par][:, :].rearrange("p (r l) -> p r l", r=2), ALU.mult,
                                           ALU.mult).then_inc(s["ao_used"], 1)

                def step(n, q_, b, first=False, last=False):
                    if not last:
                        scores(n, q_ % 2)
                    if not first:
                        norm(n - 2, q_ % 2, b - 1, q_ % 2)

                N = 2 * B
                v.wait_ge(s["l_in"], 16 * NL)
                v.sem_inc(s["ao_used"], 4)
                for n in range(2):
                    step(n, n, 0, first=True)
                with v.Fori(0, (N - 4) // 4) as j:
                    for q_ in range(4):
                        step(4 * j + 2 + q_, q_, 2 * j + 1 + q_ // 2)
                for n in range(N - 2, N + 2):
                    step(n, n, n // 2, last=n >= N)
                for i in range(NT):
                    v.wait_ge(s["attb_mm"], i + 1)
                    x_i = xres[:, i, :].rearrange("p (g r d) -> p g r d", g=G, r=R)
                    v.tensor_tensor(x_i, bank[i % 2][:, :].rearrange("p (r g d) -> p g r d", g=G, r=R), x_i,
                                    ALU.add).then_inc(s["att_x"], 1)
                v.wait_ge(s["att_x"], NT)

            layernorm_stats()
            layernorm_apply(2)
            transposed(2)
            route(0)
            experts(0)
            combine(0)
            layernorm_stats()
            layernorm_apply(3)
            transposed(3)
            attention()
            layernorm_stats()
            layernorm_apply(4)
            transposed(4)
            route(1)
            experts(1)
            combine(1)

        @block.gpsimd
        def _(g):
            def rstds(n):
                g.wait_ge(s["stat_rdy"], n)
                g.tensor_tensor(rstd[:, :], vareps[:, :], cn("half")[:, 0:NT], ALU.pow).then_inc(s["rstd_rdy"], 1)
            g.wait_ge(s["e_in"], 16 * NE)
            rstds(1)
            g.wait_ge(s["pre_used"], 4)
            g.wait_ge(s["init_rdy"], 1)
            g.memset(shist[:, 0, :], 0.0).then_inc(s["shist_rdy"], 1)
            g.memset(ghist[:, 0, :], 0.0).then_inc(s["ghist_rdy"], 1)
            g.wait_ge(s["pb_free"], 1)
            g.tensor_copy(prebuf[:, :, :], pre[:, 0, :, :]).then_inc(s["prebuf_rdy"], 1)

            def keep(l):
                g.wait_ge(s["gT_rdy"], l + 1)
                g.tensor_copy(ghist[:, l, :], gT[:, :]).then_inc(s["ghist_rdy"], 1)
                g.wait_ge(s["s_rdy"], l + 2)
                g.tensor_copy(shist[:, l + 1, :], s2[:, :]).then_inc(s["shist_rdy"], 1)

            with g.Fori(0, L - 1) as l:
                g.wait_ge(s["pb_free"], l + 2)
                g.tensor_copy(prebuf[:, :, :], pre[:, l + 1, :, :]).then_inc(s["prebuf_rdy"], 1)
                keep(l)
            keep(L - 1)

            def gathers(m):
                mo = MOES[m]
                q = lambda n: s[f"{mo.tag}_{n}"]
                g.wait_ge(q("list_rdy"), 1)
                g.wait_ge(q("hid_st"), 16 * NT)

                for b in range(mo.NB):
                    g.wait_ge(q("xt_mm"), b + 1)
                    g.indirect_dma_start(out=xg[b % 2][:, :], out_offset=None, in_=hd[m],
                                         in_offset=bass.IndirectOffsetOnAxis(ap=tli[:, b:b + 1], axis=0)).then_inc(q(f"xg_in{b % 2}"), 16)
                for par in range(2):
                    g.wait_ge(q(f"ob_st{par}"), 16 * (mo.NB // 2 + 2 - par))
                for n in range(NT * mo.K):
                    if n >= NYG:
                        g.wait_ge(q("yg_used"), n - NYG + 1)
                    g.indirect_dma_start(out=yrow[n % NYG][:, :], out_offset=None, in_=yd[m],
                                         in_offset=bass.IndirectOffsetOnAxis(ap=sloti[:, n:n + 1], axis=0)).then_inc(q(f"yg_in{n % NYG}"), 16)

            def attention_operands():
                qT = hidT[:, :, :].rearrange("p c t -> p (c t)").rearrange("p (b x) -> p b x", b=B)

                def keys(b, par):
                    g.tensor_tensor(kb[par][:, :, :], ctxT[:, :, bass.ds(b, 1)].rearrange("p t x -> p x t").broadcast_to([P, G, T]),
                                    cn("gmask").unsqueeze(2).broadcast_to([P, G, T]), ALU.mult)

                def queries(b, par):
                    g.tensor_copy(qb[par][:, :], qT[:, bass.ds(b, 1), :].rearrange("p x y -> p (x y)")).then_inc(s["qk_rdy"], 1)

                def values(b, par):
                    g.tensor_tensor(vb[par][:, :], ctxD[:, bass.ds(b, 1), :].rearrange("p x y -> p (x y)"), cn("vmask"),
                                    ALU.mult).then_inc(s["v_rdy"], 1)

                for b in range(2):
                    keys(b, b)
                    values(b, b)
                g.wait_ge(s["tr_used"], 3 * NT)
                for b in range(2):
                    queries(b, b)
                with g.Fori(0, B // 2 - 1) as j:
                    for par in range(2):
                        b = 2 * j + 2 + par
                        g.wait_ge(s["as_mm"], 4 * j + 2 + 2 * par)
                        keys(b, par)
                        queries(b, par)
                        g.wait_ge(s["ao_mm"], 4 * j + 6 + 2 * par)
                        values(b, par)

            rstds(2)
            gathers(0)
            g.wait_ge(s["l_in"], 16 * NL)
            rstds(3)
            attention_operands()
            rstds(4)
            gathers(1)

        @block.scalar
        def _(c):
            c.preload_act_table(ACT.Tanh)
            c.wait_ge(s["w_in"], 16 * NW)
            c.activation(gates_g[:, :], gates_g[:, :], ACT.Tanh).then_inc(s["achain"], 1)
            c.wait_ge(s["ctx_rest"], 1)
            c.copy(ctx3[:, 0, :], ctxP[:, :, :].rearrange("p j d -> p (j d)")).then_inc(s["ctx_hi"], 1)
            c.wait_ge(s["toep_in"], 32)
            c.copy(toepA[:, :], tr_f[:, :]).then_inc(s["toep_hi"], 1)
            c.wait_ge(s["ctx_rest"], 2)
            c.copy(ctx3[:, 1, :], ctxr[:, :]).then_inc(s["ctx_hi"], 1)
            c.wait_ge(s["toep_rest"], 1)
            c.copy(toepA[T:P, :], tr_f[T:P, :]).then_inc(s["toep_hi"], 1)
            with c.Fori(0, L) as l:
                for n, (u0, u1) in enumerate(CHUNKS):
                    c.wait_ge(s["pact_rdy"], 5 * l + n + 1)
                    c.activation(th[:, u0 * B:u1 * B], pact[:, u0 * B:u1 * B], ACT.Tanh).then_inc(s["th_rdy"], 1)
                c.wait_ge(s["nmax_rdy"], l + 1)
                c.activation(prob[:, :], EB[0:B, 0:T], ACT.Exp, bias=nmax[:, 0:1],
                             accum_out=psum_e[:, :]).then_inc(s["p_rdy"], 1)
                c.wait_ge(s["rg_rdy"], 2 * l + 1)
                c.activation(tg[:, 0:3, :], RG[0:HS, 0:3 * B].rearrange("p (g b) -> p g b", g=3), ACT.Tanh,
                             scale=0.5).then_inc(s["tg_rdy"], 1)
                c.wait_ge(s["rg_rdy"], 2 * l + 2)
                c.activation(tg[:, 3, :], gate(3), ACT.Tanh, scale=0.5).then_inc(s["tg_rdy"], 1)
                c.wait_ge(s["c2_rdy"], l + 1)
                c.activation(tc[:, :], c2[:, :], ACT.Tanh, scale=0.5).then_inc(s["tc_rdy"], 1)
            for n in range(2):
                c.wait_ge(s["yg_mm"], n + 1)
                c.activation(yg[0:HS, n * 512:(n + 1) * 512], bank[2 + n][0:HS, :], ACT.Tanh,
                             bias=gyb[:, 0:1]).then_inc(s["yg_rdy"], 1)


            def mixture(m):
                mo = MOES[m]
                I = mo.I
                q = lambda n: s[f"{mo.tag}_{n}"]
                lg = bank[6][:, 0:NT * E].rearrange("p (i e) -> p i e", e=E)
                if m == 0:
                    c.wait_ge(q("logit_mm"), 1)
                    c.activation(sc[:, :, :], lg, ACT.Tanh, scale=0.5).then_inc(q("act_done"), 1)
                else:
                    c.wait_ge(q("exp_in"), 1)
                    c.activation(sc[:, :, :], sc2[:, :, :], ACT.Exp).then_inc(q("act_done"), 1)
                for n in range(NT * mo.shared):
                    c.wait_ge(q("sh_mm"), n + 1)
                    if n >= 2:
                        c.wait_ge(q("sh_z"), n - 1)
                    c.activation(gth[n % 2][:, :], bank[n % 2][:, 0:256], ACT.Tanh, scale=0.5).then_inc(q("sh_th"), 1)

                def turned(b):
                    c.wait_ge(q("xt_mm"), b.n + 3)
                    c.copy(xgT[b.par][:, :, :], bank[b.par][:, :].rearrange("p (c t) -> p c t", c=HC)).then_inc(q("xt_rdy"), 1)

                def inner(b):
                    c.wait_ge(q("h_mm"), b.n + 1)
                    c.activation(gth[b.par][:, 0:I], bank[2 + b.par][:, 0:I], ACT.Tanh, scale=0.5).then_inc(q("th_rdy"), 1)

                def out_(b):
                    c.wait_ge(q("o_mm"), b.n + 5)
                    c.wait_ge(q(f"ob_st{b.par}"), 16 * (b.h + 1))
                    c.mul(ob[b.par][:, :], bank[5][:, :], 0.5).then_inc(q("ob_rdy"), 1)

                def step(b, first=False, last=False):
                    if not last:
                        turned(b.next())
                    if not first:
                        out_(b.next(-1))
                    inner(b)

                for par in range(2):
                    c.sem_inc(q(f"ob_st{par}"), 16)
                c.sem_inc(q("ob_rdy"), 1)
                turned(Turn(0, 0))
                step(Turn(0, 0), first=True)
                with c.Fori(0, (mo.NB - 3) // 4) as j:
                    for c_ in range(1, 5):
                        step(Turn(j, c_))
                step(Turn(0, mo.NB - 2))
                step(Turn(0, mo.NB - 1), last=True)
                out_(Turn(0, mo.NB - 1))

            def attention():
                def probs(n, par):
                    c.wait_ge(s["am_rdy"], n + 1)
                    for g_ in range(G):
                        ins = c.activation(ap_[par][:, g_ * T:(g_ + 1) * T], sm[par][:, g_, :], ACT.Exp, bias=amax[par][:, g_:g_ + 1])
                    ins.then_inc(s["aexp_rdy"], 1)

                def turned(n, par):
                    c.wait_ge(s["at_mm"], n + 1)
                    c.copy(aT[par][:, :, :], bank[2 + par][:, :].rearrange("p (c t) -> p c t", c=4)).then_inc(s["aT_rdy"], 1)

                def step(n, q_, first=False, last=False):
                    if not last:
                        probs(n, q_ % 2)
                    if not first:
                        turned(n - 1, (q_ + 1) % 2)

                N = 2 * B
                c.sem_inc(s["aexp_rdy"], 2)
                for n in range(2):
                    step(n, n, first=n == 0)
                with c.Fori(0, (N - 4) // 4) as j:
                    for q_ in range(4):
                        step(4 * j + 2 + q_, q_)
                for n in range(N - 2, N + 1):
                    step(n, n, last=n >= N)

            mixture(0)
            attention()
            mixture(1)

        @block.tensor
        def _(t):
            def turn_hidden(n):
                for i in range(NT):
                    t.wait_ge(s["hid_rdy"], (n - 1) * NT + i + 1)
                    if i >= 2:
                        t.wait_ge(s["tr_used"], (n - 1) * NT + i - 1)
                    for c in range(HC):
                        ins = t.transpose(bank[i % 2][:, c * P:(c + 1) * P], hid[:, i, c * P:(c + 1) * P], ident)
                    ins.then_inc(s["tr_rdy"], 1)

            t.wait_ge(s["e_in"], 16 * NE)
            t.matmul(bank[3][0:KWP, 0:A], convp[:, :], wafT[:, :], start=True, stop=True).then_inc(s["toep_mm"], 1)
            for t2 in range(2):
                ins = t.matmul(bank[2][t2 * A:(t2 + 1) * A, :], wahT[:, :], ctxT[:, 1 - t2:T:2, :], start=True, stop=True)
            ins.then_inc(s["enc_mm"], 1)
            turn_hidden(1)
            t.wait_ge(s["w_ready"], 1)
            t.wait_ge(s["tr_used"], NT)
            for n in range(4):
                gp, hf = n // 2, n % 2
                for c in range(HC):
                    ins = t.matmul(bank[4 + n][:, :], lys[:, c, gp * 2 * HS:(gp + 1) * 2 * HS],
                                   hidT[:, c, hf * 512:(hf + 1) * 512], start=(c == 0), stop=(c == HC - 1))
                ins.then_inc(s["pre_mm"], 1)
            t.wait_ge(s["pre_used"], 4)
            t.wait_ge(s["enc_used"], 1)
            t.wait_ge(s["comb_rdy"], 1)
            t.wait_ge(s["ctx_rest"], 3)
            t.wait_ge(s["toep_rest"], 2)
            t.transpose(bank[7][0:B, 0:B], ident[0:B, 0:B], ident[0:B, 0:B]).then_inc(s["pb_free"], 1)
            FIRST = [u0 for u0, _ in GROUPS]

            def locations(us, parts=3, first=0):
                for u in us:
                    w = slice((NU - 1 - u) * P, (NU - u) * P)
                    dst = loc(u, u + 1)
                    if first == 0:
                        t.matmul(dst, toepA[:, w], al2[:, 0, :], start=(u in FIRST), stop=False)
                        ins = t.matmul(dst, toepB[T:P, w], al2[T:P, 0, :], start=False, stop=False)
                    if parts == 3:
                        ins = t.matmul(dst, toepA[:, w], al2[:, 1, :], start=False, stop=(u + 1 in FIRST or u == NU - 1))
                return ins

            U0, U2 = 9, 27
            (_, UA), (_, UB), _ = GROUPS
            t.wait_ge(s["alT_rdy"], 1)
            locations(range(0, UA)).then_inc(s["loc_rdy"], 1)
            locations(range(UA, UB)).then_inc(s["loc_rdy"], 1)
            locations(range(UB, U2))
            with t.Fori(0, L) as l:
                t.wait_ge(s["prebuf_rdy"], l + 1)
                t.wait_ge(s["s_rdy"], l + 1)
                t.matmul(SW, wasT[:, :, :].rearrange("p r a -> p (r a)"), s2[:, :], start=True,
                         stop=True).then_inc(s["sw_rdy"], 1)
                locations(range(U2, NU)).then_inc(s["loc_rdy"], 1)
                t.matmul(EB[0:B, 0:T], ident[0:B, 0:B], maskb[:, :], start=True, stop=False)
                for n, (u0, u1) in enumerate(CHUNKS):
                    t.wait_ge(s["th_rdy"], 5 * l + n + 1)
                    for u in range(u0, u1):
                        ins = t.matmul(EB[0:B, 2 * u:2 * u + 2], th[:, u * B:(u + 1) * B], va2[:, :], start=False, stop=(u == NU - 1))
                ins.then_inc(s["eb_rdy"], 1)
                t.matmul(RG[0:HS, 0:3 * B], ident[0:HS, 0:HS], prebuf[:, 0:3, :].rearrange("p g b -> p (g b)"), start=True, stop=False)
                t.matmul(gate(3), ident[0:HS, 0:HS], prebuf[:, 3, :], start=True, stop=False)
                for g in range(4):
                    ins = t.matmul(gate(g), lss[:, g * HS:(g + 1) * HS], s2[:, :], start=False, stop=False)
                ins.then_inc(s["pb_free"], 1)
                t.wait_ge(s["r_rdy"], l + 1)
                t.transpose(AT[:, 0:P], pn[:, :], ident).then_inc(s["at_rdy"], 1)
                t.wait_ge(s["al_rdy"], 2 * l + 1)
                locations(range(0, U0), parts=2)
                t.wait_ge(s["ae_rdy"], l + 1)
                for j in range(8):
                    for k in range(3):
                        ins = t.matmul(GT[:, 0:2 * B].rearrange("p (s b) -> p s b", s=2)[:, :, j:B:8],
                                       ctx3[:, k, j * D:(j + 1) * D], ae[:, :, j:B:8], start=(k == 0), stop=(k == 2))
                ins.then_inc(s["gt_rdy"], 1)
                t.wait_ge(s["al_rdy"], 2 * l + 2)
                locations(range(0, U0), first=2)
                locations(range(U0, UA)).then_inc(s["loc_rdy"], 1)
                t.wait_ge(s["gT_rdy"], l + 1)
                for g in range(4):
                    ins = t.matmul(gate(g), lgs[:, g * HS:(g + 1) * HS], gT[:, :], start=False, stop=(g >= 2))
                    if g >= 2:
                        ins.then_inc(s["rg_rdy"], 1)
                locations(range(UA, UB)).then_inc(s["loc_rdy"], 1)
                locations(range(UB, U2))
            locations(range(U2, NU))
            t.wait_ge(s["ghist_rdy"], L + 1)
            t.wait_ge(s["shist_rdy"], L + 1)
            for n in range(2):
                t.matmul(bank[2 + n][0:HS, :], lgyT[:, :], ghist[:, n * 32:(n + 1) * 32, :], start=True, stop=False)
                t.matmul(bank[2 + n][0:HS, :], lsyT[:, :], shist[:, n * 32:(n + 1) * 32, :], start=False,
                         stop=True).then_inc(s["yg_mm"], 1)
            for i in range(NT):
                t.wait_ge(s["yg_rdy"], i // 4 + 1)
                if i >= 2:
                    t.wait_ge(s["x1_rdy"], i - 1)
                t.matmul(bank[i % 2][:, :], yg[:, i * P:(i + 1) * P], yyT[:, :], start=True, stop=True).then_inc(s["y_mm"], 1)

            def mixture(m):
                mo = MOES[m]
                I, IC, K, NB = mo.I, mo.IC, mo.K, mo.NB
                q = lambda n: s[f"{mo.tag}_{n}"]
                t.wait_ge(s["tr_used"], (2 * m + 2) * NT)
                for i in range(NT):
                    for c in range(HC):
                        ins = t.matmul(bank[6][:, i * E:(i + 1) * E], hidT[:, c, i * P:(i + 1) * P], gw[:, m, c, :],
                                       start=(c == 0), stop=(c == HC - 1))
                ins.then_inc(q("logit_mm"), 1)

                def sh_in(n):
                    h, i, p_ = n // NT, n % NT, n % 2
                    t.wait_ge(q("sw_in"), 32 * mo.shared)
                    if n >= 2:
                        t.wait_ge(q("sh_z"), n - 1)
                    for c in range(HC):
                        ins = t.matmul(bank[p_][:, :], hidT[:, c, i * P:(i + 1) * P], wbuf1[h][:, c, :], start=(c == 0),
                                       stop=(c == HC - 1))
                    ins.then_inc(q("sh_mm"), 1)

                def sh_turn(n):
                    t.wait_ge(q("sh_z"), n + 1)
                    if n >= 1:
                        t.wait_ge(q("sh_ztr"), n)
                    for c in range(2):
                        ins = t.transpose(bank[2][:, c * P:(c + 1) * P], zb[n % 2][:, c * P:(c + 1) * P], ident)
                    ins.then_inc(q("sh_zt"), 1)

                def sh_out(n):
                    t.wait_ge(q("sh_ztr"), n + 1)
                    if n >= 2:
                        t.wait_ge(q("sh_x"), n - 1)
                    for c in range(2):
                        ins = t.matmul(bank[3 + n % 2][:, :], zT[n % 2][:, c, :], wbuf2[n // NT][:, c, :], start=(c == 0),
                                       stop=(c == 1))
                    ins.then_inc(q("sh_o"), 1)

                def sh_step(n):
                    if n >= 1:
                        sh_turn(n - 1)
                    if n < NT * mo.shared:
                        sh_in(n)
                    if n >= 1:
                        sh_out(n - 1)

                sh_step(0)
                sh_step(1)
                t.wait_ge(q("route_oh"), 1)
                rhs = msum[:, :, :].rearrange("p i e -> p (i e)")
                t.matmul(bank[7][:, 0:NT * E], cn("before"), rhs, start=True, stop=True)
                t.matmul(bank[7][:, NT * E:2 * NT * E], cn("ones"), rhs, start=True, stop=True).then_inc(q("pos_mm"), 1)
                sh_step(2)
                sh_step(3)
                NK = NT * K
                for n in range(NK):
                    if n % (NK // 4) == 0:
                        sh_step(4 + 4 * n // NK)
                    t.wait_ge(q("hot_rdy"), n + 1)
                    t.matmul(bank[6][:, 0:2 * NB], lowhot[:, n, :], highhot[:, n, :, 0:NB], start=(n == 0),
                             stop=(n == NK - 1)).then_inc(q("hot_mm"), 1)
                for n in range(8, NT * mo.shared + 1):
                    sh_step(n)

                def turn(b):
                    t.wait_ge(q(f"xg_in{b.par}"), 16 * (b.h + 1))
                    for c in range(HC):
                        ins = t.transpose(bank[b.par][:, c * P:(c + 1) * P], xg[b.par][:, c * P:(c + 1) * P], ident)
                    ins.then_inc(q("xt_mm"), 1)

                def inner(b):
                    t.wait_ge(q(f"w_in{b.slot}"), 32 * (b.q + 1))
                    t.wait_ge(q("xt_rdy"), b.n + 1)
                    for c in range(HC):
                        ins = t.matmul(bank[2 + b.par][:, 0:2 * I], xgT[b.par][:, c, :], wbuf1[b.slot][:, c, 0:2 * I], start=(c == 0),
                                       stop=(c == HC - 1))
                    ins.then_inc(q("h_mm"), 1)

                def zturn(b):
                    t.wait_ge(q("z_rdy"), b.n + 1)
                    for c in range(IC):
                        ins = t.transpose(bank[4][:, c * P:(c + 1) * P], zb[b.par][:, c * P:(c + 1) * P], ident)
                    ins.then_inc(q("zt_mm"), 1)

                def outer(b):
                    t.wait_ge(q("zt_rdy"), b.n + 1)
                    t.wait_ge(q("ob_rdy"), b.n + 1)
                    for c in range(IC):
                        ins = t.matmul(bank[5][:, :], zT[b.par][:, c, :], wbuf2[b.slot][:, c, :], start=(c == 0), stop=(c == IC - 1))
                    ins.then_inc(q("o_mm"), 1)

                def step(b, first=False, last=False):
                    if not last:
                        turn(b.next())
                    if not first:
                        zturn(b.next(-1))
                    inner(b)
                    if not first:
                        outer(b.next(-1))

                t.sem_inc(q("xt_mm"), 2)
                t.sem_inc(q("o_mm"), 4)
                turn(Turn(0, 0))
                step(Turn(0, 0), first=True)
                with t.Fori(0, (NB - 3) // 4) as j:
                    for c_ in range(1, 5):
                        step(Turn(j, c_))
                step(Turn(0, NB - 2))
                step(Turn(0, NB - 1), last=True)
                zturn(Turn(0, NB - 1))
                outer(Turn(0, NB - 1))

            def attention():
                def scores(n, par, bpar, b, rp):
                    t.wait_ge(s["qk_rdy"], b + 1)
                    t.matmul(bank[par][:, :], qb[bpar][:, rp * P:(rp + 1) * P], kb[bpar][:, :, :], start=True,
                             stop=True).then_inc(s["as_mm"], 1)

                def turn(n, par):
                    t.wait_ge(s["aexp_rdy"], n + 3)
                    for c in range(4):
                        ins = t.transpose(bank[2 + par][:, c * P:(c + 1) * P], ap_[par][:, c * P:(c + 1) * P], ident)
                    ins.then_inc(s["at_mm"], 1)

                def values(n, par, bpar, b):
                    t.wait_ge(s["aT_rdy"], n + 1)
                    t.wait_ge(s["v_rdy"], b + 1)
                    t.wait_ge(s["ao_used"], 2 * n + 2)
                    for c in range(4):
                        t.matmul(bank[4 + par][32 * c:32 * c + 32, 0:P], vb[bpar][:, 32 * c:32 * c + 32], aT[par][:, c, :],
                                 start=True, stop=True)
                    for c in range(4):
                        ins = t.matmul(bank[4 + par][32 * c:32 * c + 32, P:2 * P], cn("vmask")[:, 0:32], aT[par][:, c, :],
                                       start=True, stop=True)
                    ins.then_inc(s["ao_mm"], 1)

                def step(n, q_, b, bq, scr=True, trn=True, val=True):
                    if scr:
                        scores(n, q_ % 2, bq % 2, b, q_ % 2)
                    if trn:
                        turn(n - 1, (q_ + 1) % 2)
                    if val:
                        values(n - 2, q_ % 2, (bq + 1) % 2, b - 1)

                N = 2 * B
                t.sem_inc(s["ao_mm"], 4)
                t.wait_ge(s["tr_used"], 3 * NT)
                for n in range(2):
                    step(n, n, 0, 0, trn=n >= 1, val=False)
                with t.Fori(0, (N - 4) // 4) as j:
                    for q_ in range(4):
                        step(4 * j + 2 + q_, q_, 2 * j + 1 + q_ // 2, 1 + q_ // 2)
                for n in range(N - 2, N + 2):
                    step(n, n, n // 2, n // 2, scr=n < N, trn=n <= N)
                t.wait_ge(s["ao_used"], 2 * N + 4)
                for i in range(NT):
                    if i >= 2:
                        t.wait_ge(s["att_x"], i - 1)
                    for r in range(R):
                        ins = t.transpose(bank[i % 2][:, r * P:(r + 1) * P], attT[:, r, i * P:(i + 1) * P], ident)
                    ins.then_inc(s["attb_mm"], 1)

            turn_hidden(2)
            mixture(0)
            turn_hidden(3)
            attention()
            turn_hidden(4)
            mixture(1)


def up_layout(w):
    n, rows, _ = w.shape
    return w.reshape(n, rows, HC, P).transpose(0, 3, 2, 1)


def down_layout(w):
    n, _, inner = w.shape
    return w.reshape(n, H, inner // P, P).transpose(0, 3, 2, 1)


def kernel(**inp):
    import concourse.bacc as bacc
    from concourse.bass_utils import run_bass_kernel_spmd

    v = {k: np.asarray(x) for k, x in inp.items()}
    ctxa = v["ctx_1024"]
    arrays = {
        "const": constants()[0],
        "x": v["x"].transpose(1, 0, 2).reshape(NTOK, H),
        "ctxT": ctxa.transpose(2, 1, 0),
        "ctxP": ctxa.reshape(2, 8, T, D).transpose(0, 2, 1, 3).reshape(P, 8, D),
        "lens": v["_lenS2"].reshape(B, 1),
        "lysT": v["L0_xattn_L_ys"].T.reshape(HC, P, 4 * HS).transpose(1, 0, 2),
        "lssT": v["L0_xattn_L_ss"].T,
        "lgsT": v["L0_xattn_L_gs_w"].T,
        "gsb": v["L0_xattn_L_gs_b"].reshape(4, HS).T,
        "wasT": v["L0_xattn_Wa_s"].T,
        "wahT": v["L0_xattn_Wa_h"].T,
        "ba": v["L0_xattn_ba"].reshape(A, 1),
        "convw": v["L0_xattn_conv_w"].reshape(FCH, KW),
        "wafT": v["L0_xattn_Wa_f"].T,
        "va": v["L0_xattn_va"].reshape(A, 1),
        "lgyT": v["L0_xattn_L_gy_w"].T,
        "lsyT": v["L0_xattn_L_sy"].T,
        "gyb": v["L0_xattn_L_gy_b"].reshape(HS, 1),
        "yyT": np.concatenate([v["L0_xattn_L_yy_w"].T, v["L0_xattn_L_yy_b"].reshape(1, H)], 0),
        "gw": np.stack([v["L0_ffn_gate_w"], v["L1_ffn_gate_w"]]).reshape(2, E, HC, P).transpose(3, 0, 2, 1),
        "bias0": np.broadcast_to(v["L0_ffn_bias"].reshape(1, E), (P, E)),
        "amask": v["mask_SxS2_ff0"],
        "ctxD": ctxa.transpose(1, 0, 2),
        "w1_0": up_layout(np.concatenate([v["L0_ffn_Wg"], v["L0_ffn_Wu"]], 1)),
        "w2_0": down_layout(v["L0_ffn_Wd"]),
        "s1_0": up_layout(np.concatenate([v["L0_ffn_Sg"], v["L0_ffn_Su"]], 0)[None]),
        "s2_0": down_layout(v["L0_ffn_Sd"][None]),
        "w1_1": up_layout(v["L1_ffn_w_gate_up"]),
        "w2_1": down_layout(v["L1_ffn_w_down"]),
        "s1_1": up_layout(v["L1_ffn_shared_w_gate_up"].reshape(2, 2, 256, H).transpose(1, 0, 2, 3).reshape(2, 512, H)),
        "s2_1": down_layout(v["L1_ffn_shared_w_down"].reshape(H, 2, 256).transpose(1, 0, 2)),
        "gg": np.broadcast_to(np.concatenate([v["g_xattn"], v["g_ffn"]]), (P, 4)),
    }
    nc = bacc.Bacc("TRN2", target_bir_lowering=False, num_devices=1)
    arrays = {k: np.ascontiguousarray(x) for k, x in arrays.items()}
    aps = {k: nc.dram_tensor("in_" + k, list(x.shape), mybir.dt.from_np(x.dtype), kind="ExternalInput").ap()
           for k, x in arrays.items()}
    out = nc.dram_tensor("out_0", [NTOK, H], F32, kind="ExternalOutput").ap()
    build(nc, aps, out, 0)
    r = run_bass_kernel_spmd(nc, [{"in_" + k: x for k, x in arrays.items()}], core_ids=[0])
    return r.results[0]["out_0"].reshape(L, B, H).transpose(1, 0, 2)
```

```python
from contextlib import ExitStack

import numpy as np

import concourse.bass as bass
from concourse import mybir

ALU = mybir.AluOpType
ACT = mybir.ActivationFunctionType
AX = mybir.AxisListType
F32 = mybir.dt.float32
F16 = mybir.dt.float16
BF16 = mybir.dt.bfloat16
I32 = mybir.dt.int32
U32 = mybir.dt.uint32

P = 128
B, L, H = 16, 64, 512
T, D, HS = 64, 128, 64
A, FCH, KW = 64, 10, 101
NTOK = B * L
NT = NTOK // P
HC = H // P
PAD = 13
KWP = KW + 2 * PAD
NU = T // 2
GROUPS = [(0, 10), (10, 32)]
CHUNKS = [(0, 5), (5, 10), (10, 18), (18, 25), (25, 32)]
WTOP = 8192.0
E = 16
G, R, HD = 8, 4, 16
EPS = 1e-5
PSCALE = 1024.0


class Moe:

    def __init__(self, tag, inter, top, shared):
        self.tag, self.I, self.K, self.shared = tag, inter, top, shared
        self.IC = inter // P
        self.NB = NTOK * top // P + E - 1
        assert self.NB % 4 == 3


class Turn:

    def __init__(self, j, c):
        self.j, self.c = j, c
        self.par, self.slot = c % 2, c % 4
        self.n = 4 * j + c
        self.h = 2 * j + c // 2
        self.q = j + c // 4

    def next(self, d=1):
        return Turn(self.j, self.c + d)


MOES = [Moe("f0", 256, 4, 1), Moe("f1", 128, 2, 2)]
NEG = -1e30


def constants():
    p = np.arange(P)
    cols = {
        "ident": np.eye(P),
        "tcount": np.broadcast_to(np.arange(T)[None, :], (P, T)),
        "half": np.full((P, 2 * NT), -0.5),
        "ones": np.ones((P, P)),
        "before": (p[:, None] < p[None, :]),
        "iota": np.broadcast_to(p[None, :], (P, P)),
        "prow": p[:, None],
        "tri": np.broadcast_to((np.arange(E)[None, :] < np.arange(E)[:, None]).reshape(1, E * E), (P, E * E)),
        "gmask": 0.25 * (p[:, None] // HD == np.arange(G)[None, :]),
        "vmask": (p[:, None] // T == (np.arange(P)[None, :] // HD) % 2),
    }
    where, parts, at = {}, [], 0
    for name, c in cols.items():
        c = np.asarray(c, np.float32)
        where[name] = (at, c.shape[1])
        parts.append(c)
        at += c.shape[1]
    return np.ascontiguousarray(np.concatenate(parts, 1)), where


def build(nc, a, out):
    _, where = constants()
    with ExitStack() as ctx:
        def sb(name, shape, dt=F32):
            return ctx.enter_context(nc.sbuf_tensor(name, shape, dt))

        def ps(name, shape=(P, 512)):
            return ctx.enter_context(nc.psum_tensor(name, list(shape), F32))

        def sem(name):
            return ctx.enter_context(nc.semaphore(name))

        bank = [ps(f"bank{i}") for i in range(8)]

        const = sb("const", [P, sum(n for _, n in where.values())])

        def cn(name, rows=P):
            at, n = where[name]
            return const[0:rows, at:at + n]

        ident = cn("ident")
        xres = sb("xres", [P, NT, H])
        hid = sb("hid", [P, NT, H])
        hidT = sb("hidT", [P, HC, NTOK])
        stats = sb("stats", [P, NT, 6])
        mv = sb("mv", [P, NT, 2])
        vareps = sb("vareps", [P, NT])
        rstd = sb("rstd", [P, NT])
        gates_g = sb("gates_g", [P, 4])

        ctxT = sb("ctxT", [D, T, B])
        ctxP = sb("ctxP", [P, 8, D])
        lens_i = sb("lens_i", [B, 1], I32)
        lens_f = sb("lens_f", [B, 1])
        maskb = sb("maskb", [B, T])
        lys = sb("lys", [P, HC, 4 * HS])
        lss = sb("lss", [HS, 4 * HS])
        lgs = sb("lgs", [D, 4 * HS])
        gsb = sb("gsb", [P, 4])
        wasT = sb("wasT", [HS, 2, A])
        wahT = sb("wahT", [D, A])
        bacol = sb("bacol", [P, 1])
        convp = sb("convp", [FCH, KWP])
        wafT = sb("wafT", [FCH, A])
        va2 = sb("va2", [P, 2])
        lgyT = sb("lgyT", [D, HS])
        lsyT = sb("lsyT", [HS, HS])
        gyb = sb("gyb", [HS, 1])
        yyT = sb("yyT", [HS + 1, H])

        comb = sb("comb", [P, A])
        region = sb("region", [P, 3 * 4096])
        tr_f = region[:, 4096:8192]
        toep = region[:, 0:2048].bitcast(F16)
        wext = sb("wext", [P, 2])
        wabs = sb("wabs", [P, 1])
        wrow = sb("wrow", [1, 1])
        wmax = sb("wmax", [P, 1])
        wscale = sb("wscale", [P, 1])
        wback = sb("wback", [P, 1])
        ctx3 = sb("ctx3", [P, 3, 8 * D], BF16)
        ctxr = sb("ctxr", [P, 8 * D])
        comb_d = nc.dram_tensor("comb_d", [P + T, A], F32).ap()
        enc = sb("enc", [P, NU * B])
        pre = region[0:HS, 8192:12288].rearrange("p (l g b) -> p l g b", l=L, g=4)
        ghist = sb("ghist", [D, L, B])
        shist = sb("shist", [HS, L + 1, B])

        prebuf = sb("prebuf", [HS, 4, B])
        s2 = sb("s2", [HS, B])
        c2 = sb("c2", [HS, B])
        al2 = sb("al2", [P, 2, B], F16)
        encloc = sb("encloc", [P, NU * B])
        pact = sb("pact", [P, NU * B])
        th = sb("th", [P, NU * B])
        nmax = sb("nmax", [B, 1])
        psum_e = sb("psum_e", [B, 1])
        prob = sb("prob", [B, T])
        rinv = sb("rinv", [B, 1])
        pn = sb("pn", [P, 2 * T])
        ae = sb("ae", [P, 2, B], F16)
        gT = sb("gT", [D, B])
        tg = sb("tg", [HS, 4, B])
        la = sb("la", [HS, B])
        lb = sb("lb", [HS, B])
        tc = sb("tc", [HS, B])
        yg = sb("yg", [HS + 1, NTOK])

        gw = sb("gw", [P, 2, HC, E])
        bias0 = sb("bias0", [P, E])
        wbuf1 = [region[:, i * 3072:i * 3072 + 2048].rearrange("p (c n) -> p c n", c=HC) for i in range(4)]
        wbuf2 = [region[:, i * 3072 + 2048:(i + 1) * 3072].rearrange("p (c n) -> p c n", c=2) for i in range(4)]
        xg = [sb(f"xg{i}", [P, H]) for i in range(2)]
        xgT = [sb(f"xgT{i}", [P, HC, P]) for i in range(2)]
        gth = [sb(f"gth{i}", [P, 256]) for i in range(2)]
        ga = [sb(f"ga{i}", [P, 256]) for i in range(2)]
        zb = [sb(f"zb{i}", [P, 256]) for i in range(2)]
        zT = [sb(f"zT{i}", [P, 2, P]) for i in range(2)]
        ob = [sb(f"ob{i}", [P, H]) for i in range(2)]
        lgT = ob
        NYG = 6
        yrow = [hidT[:, i // 2, (i % 2) * H:(i % 2 + 1) * H] for i in range(NYG)]
        NBM = MOES[0].NB
        KM = MOES[0].K
        sc = sb("sc", [P, NT, E])
        sc2 = sb("sc2", [P, NT, E])
        smax = sb("smax", [P, NT])
        top8 = sb("top8", [P, NT, 8])
        idx8 = sb("idx8", [P, NT, 8], U32)
        idxf = sb("idxf", [P, NT * KM])
        onehot = sb("onehot", [P, NT * KM, E])
        ohs = sb("ohs", [P, NT * KM, E])
        msum = sb("msum", [P, NT, E])
        cum = sb("cum", [P, NT, E])
        count = sb("count", [P, E])
        nblk_i = sb("nblk_i", [P, E], I32)
        nblk_j = sb("nblk_j", [P, E], I32)
        nblk = sb("nblk", [P, E])
        trib = sb("trib", [P, E, E])
        bstart = sb("bstart", [P, E])
        bend = sb("bend", [P, E])
        place = sb("place", [P, NT, E])
        slotf = sb("slotf", [P, NT * KM])
        sloti = sb("sloti", [P, NT * KM], I32)
        slow_i = sb("slow_i", [P, NT * KM], I32)
        shigh_i = sb("shigh_i", [P, NT * KM], I32)
        slow = sb("slow", [P, NT * KM])
        shigh = sb("shigh", [P, NT * KM])
        wsum = sb("wsum", [P, NT])
        winv = sb("winv", [P, NT])
        wk = sb("wk", [P, NT, KM])
        ecmp = sb("ecmp", [P, NBM, E])
        ebf = sb("ebf", [P, NBM])
        ebi = sb("ebi", [P, NBM], I32)
        lowhot = region[:, 3072:5120].bitcast(BF16).rearrange("p (n x) -> p n x", n=NT * KM)
        highhot = region[:, 5120:5120 + NT * KM * NBM].bitcast(BF16).rearrange("p (n r x) -> p n r x", n=NT * KM, r=2)
        tlf = sb("tlf", [P, NBM])
        tli = sb("tli", [P, NBM], I32)
        halfg = sb("halfg", [P, 4])
        hd = [nc.dram_tensor(f"hid_d{m}", [NTOK, H], F32).ap() for m in range(2)]
        yd = [nc.dram_tensor(f"y_d{m}", [mo.NB * P, H], F32).ap() for m, mo in enumerate(MOES)]

        amask = sb("amask", [P, T])
        ctxD = sb("ctxD", [P, B, D])
        qb = [sb(f"qb{i}", [P, R * L]) for i in range(2)]
        kb = [sb(f"kb{i}", [P, G, T]) for i in range(2)]
        vb = [sb(f"vb{i}", [P, P]) for i in range(2)]
        sm = [sb(f"sm{i}", [P, G, T]) for i in range(2)]
        amax = [sb(f"amax{i}", [P, G]) for i in range(2)]
        ap_ = [encloc, pact]
        aT = [x[:, :].rearrange("p (c t) -> p c t", c=4) for x in (enc, th)]
        arec = [sb(f"arec{i}", [P, P]) for i in range(2)]
        attT = region[:, 8192:12288].rearrange("p (r t) -> p r t", r=R)

        def loc(u0, u1):
            n = max(n for n in range(2) if u0 >= GROUPS[n][0])
            return bank[(0, 7)[n]][:, (u0 - GROUPS[n][0]) * B:(u1 - GROUPS[n][0]) * B]

        SW, RO, EB, AT, GT, RG = bank[4][:, 256:256 + B], bank[2], bank[3], bank[4], bank[5], bank[6]

        def gate(g):
            return RO[0:HS, 0:B] if g == 3 else RG[0:HS, g * B:(g + 1) * B]

        names = """x_in e_in scale_in scale_mm w_in l_in dchain  rstd_rdy hid_rdy tr_rdy tr_used pre_mm pre_used toep_mm comb_rdy comb_st toep_in toep_hi toep_rest ctx_hi ctx_rest 
        enc_mm enc_used w_ready init_rdy loc_rdy sw_rdy pact_rdy th_rdy al_rdy eb_rdy nmax_rdy p_rdy r_rdy at_rdy ae_rdy
        alT_rdy gt_rdy gT_rdy rg_rdy tg_rdy c2_rdy tc_rdy s_rdy prebuf_rdy ghist_rdy shist_rdy pb_free
        yg_mm yg_rdy y_mm x1_rdy out_done st_rdy stat_rdy 
        qk_rdy v_rdy as_mm  smx_rdy am_rdy aexp_rdy at_mm aT_rdy ao_mm ao_used attb_mm att_x exp_in""".split()
        for mo in MOES:
            names += [f"{mo.tag}_{n}" for n in """hid_st logit_mm  act_done route_oh pos_mm  place_rdy low_rdy high_rdy hot_mm 
            list_rdy eb_rdy w_in0 w_in1 w_in2 w_in3 xg_in0 xg_in1 xt_mm xt_rdy h_mm th_rdy  z_rdy zt_mm zt_rdy o_mm ob_rdy ob_st0 ob_st1
            sw_in sh_mm sh_th sh_z sh_zt sh_ztr sh_o sh_x yg_in0 yg_in1 yg_in2 yg_in3 yg_in4 yg_in5 yg_used""".split()]
        s = {n: sem(n) for n in names}

        block = ctx.enter_context(nc.Block())

        ELOADS = [(const[:, :], a["const"]), (ctxT[:, :, :], a["ctxT"]), (wahT[:, :], a["wahT"]), (bacol[0:A, :], a["ba"]),
                  (bacol[A:P, :], a["ba"]), (wafT[:, :], a["wafT"]), (convp[:, PAD:PAD + KW], a["convw"])]
        WLOADS = [(gsb[0:HS, :], a["gsb"]), (gsb[HS:P, :], a["gsb"]), (lys[:, :, :], a["lysT"]), (ctxP[:, :, :], a["ctxP"]),
                  (lens_i[:, :], a["lens"]), (lss[:, :], a["lssT"]), (lgs[:, :], a["lgsT"]),
                  (wasT[:, 0, :], a["wasT"]), (wasT[:, 1, :], a["wasT"]),
                  (lgyT[:, :], a["lgyT"]), (lsyT[:, :], a["lsyT"]), (gyb[:, :], a["gyb"]), (yyT[:, :], a["yyT"]),
                  (gates_g[:, :], a["gg"]), (gw[:, :, :, :], a["gw"]), (bias0[:, :], a["bias0"]),
                  (va2[0:A, 1:2], a["va"]), (va2[A:P, 0:1], a["va"])]
        LLOADS = [(amask[0:T, :], a["amask"]), (amask[T:P, :], a["amask"]),
                  (ctxD[0:T, :, :], a["ctxD"]), (ctxD[T:P, :, :], a["ctxD"])]
        NE, NW, NL = len(ELOADS), len(WLOADS), len(LLOADS)

        @block.sync
        def _(sp):
            for dst, src in ELOADS[:-1]:
                sp.dma_start(dst, src).then_inc(s["e_in"], 16)
            sp.wait_ge(s["init_rdy"], 1)
            dst, src = ELOADS[-1]
            sp.dma_start(dst, src).then_inc(s["e_in"], 16)
            for i in range(NT):
                sp.dma_start(xres[:, i, :], a["x"][i * P:(i + 1) * P, :]).then_inc(s["x_in"], 16)
            sp.wait_ge(s["comb_rdy"], 1)
            sp.dma_start(comb_d[0:KWP, :], comb[0:KWP, :]).then_inc(s["comb_st"], 16)
            for dst, src in WLOADS[:3]:
                sp.dma_start(dst, src).then_inc(s["w_in"], 16)
            sp.wait_ge(s["comb_st"], 16)
            windows = bass.AP(comb_d.tensor, 0, [[A, T], [1, T * A]])
            for half in range(2):
                sp.dma_start(tr_f[half * T:(half + 1) * T, :], windows).then_inc(s["toep_in"], 16)
            for dst, src in WLOADS[3:]:
                sp.dma_start(dst, src).then_inc(s["w_in"], 16)
            for dst, src in LLOADS:
                sp.dma_start(dst, src).then_inc(s["l_in"], 16)

            def mixture(m):
                mo = MOES[m]
                q = lambda n: s[f"{mo.tag}_{n}"]
                for h in range(mo.shared):
                    if m == 0:
                        sp.wait_ge(s["yg_mm"], 1)
                    else:
                        sp.wait_ge(s["attb_mm"], NT)
                    w = 4 - mo.shared + h
                    sp.dma_start(wbuf1[w][:, :, :], a[f"s1_{m}"][h]).then_inc(q("sw_in"), 16)
                    sp.dma_start(wbuf2[w][:, :, :], a[f"s2_{m}"][h]).then_inc(q("sw_in"), 16)
                for i in range(NT):
                    sp.wait_ge(s["hid_rdy"], (2 * m + 1) * NT + i + 1)
                    sp.dma_start(hd[m][i * P:(i + 1) * P, :], hid[:, i, :]).then_inc(q("hid_st"), 16)
                sp.wait_ge(q("eb_rdy"), 1)

                def weights(b):
                    sp.wait_ge(q("o_mm"), b.n + 1)
                    e = sp.value_load(ebi[0:1, bass.ds(b.n, 1)], min_val=0, max_val=E - 1)
                    sp.dma_start(wbuf1[b.slot][:, :, 0:2 * mo.I], a[f"w1_{m}"][bass.ds(e, 1)].rearrange("x p c n -> (x p) c n")).then_inc(q(f"w_in{b.slot}"), 16)
                    sp.dma_start(wbuf2[b.slot][:, 0:mo.IC, :], a[f"w2_{m}"][bass.ds(e, 1)].rearrange("x p c n -> (x p) c n")).then_inc(q(f"w_in{b.slot}"), 16)

                def store(b):
                    sp.wait_ge(q("ob_rdy"), b.n + 2)
                    sp.dma_start(yd[m][bass.ds(b.n * P, P), :], ob[b.par][:, :]).then_inc(q(f"ob_st{b.par}"), 16)

                def step(b, more=True):
                    if more:
                        weights(b.next(3))
                    store(b)

                for c_ in range(3):
                    if c_ == 1:
                        sp.wait_ge(q("hot_mm"), NT * mo.K)
                    if c_ == 2 and mo.shared == 2:
                        sp.wait_ge(q("sh_o"), NT * mo.shared)
                    weights(Turn(0, c_))
                if mo.shared == 1:
                    sp.wait_ge(q("sh_o"), NT * mo.shared)
                step(Turn(0, 0))
                with sp.Fori(0, (mo.NB - 7) // 4) as j:
                    for c_ in range(1, 5):
                        step(Turn(j, c_))
                for n in range(mo.NB - 6, mo.NB):
                    step(Turn(0, n), more=n + 3 < mo.NB)

            mixture(0)
            mixture(1)
            for i in range(NT):
                sp.wait_ge(s["f1_yg_used"], MOES[1].K * (i + 1))
                sp.dma_start(out[i * P:(i + 1) * P, :], xres[:, i, :]).then_inc(s["out_done"], 16)
            sp.wait_ge(s["out_done"], 16 * NT)

        @block.vector
        def _(v):
            ch = [0]

            def link(ins):
                ch[0] += 1
                ins.then_inc(s["dchain"], 1)
                v.wait_ge(s["dchain"], ch[0])

            v.memset(convp[:, :], 0.0)
            v.memset(wabs[:, :], 0.0)
            link(v.memset(va2[:, :], 0.0))
            v.memset(s2[:, :], 0.0)
            v.memset(c2[:, :], 0.0)
            v.memset(al2[:, :, :], 0.0)
            v.memset(pn[:, :], 0.0)
            link(v.memset(yg[HS:HS + 1, :], 1.0))
            v.memset(prebuf[:, 0, 0:1], 0.0).then_inc(s["init_rdy"], 1)
            v.memset(ae[:, :, :], 0.0).then_inc(s["alT_rdy"], 1)
            v.memset(prebuf[:, 1, 0:1], 0.0).then_inc(s["s_rdy"], 1)

            def tile_stats(i):
                v.bn_stats(stats[:, i, :], xres[:, i, :]).then_inc(s["st_rdy"], 1)

            def layernorm_stats(n):
                v.wait_ge(s["st_rdy"], n * NT)
                for i in range(NT):
                    ins = v.bn_aggr(mv[:, i, :], stats[:, i, :])
                link(ins)
                v.tensor_scalar(vareps[:, :], mv[:, :, 1], EPS, None, ALU.add).then_inc(s["stat_rdy"], 1)

            def layernorm_apply(n):
                v.wait_ge(s["rstd_rdy"], n)
                if n >= 3:
                    v.wait_ge(s["f0_hid_st"], 16 * NT)
                for i in range(NT):
                    src, dst = xres[:, i, :], hid[:, i, :]
                    if n == 3:
                        src = src.rearrange("p (g r d) -> p g r d", g=G, r=R)
                        dst = dst.rearrange("p (r g d) -> p g r d", g=G, r=R)
                    v.tensor_scalar(dst, src, mv[:, i, 0:1], rstd[:, i:i + 1], ALU.subtract,
                                    ALU.mult).then_inc(s["hid_rdy"], 1)

            v.wait_ge(s["e_in"], 16 * NE)
            v.wait_ge(s["toep_mm"], 1)
            v.tensor_reduce(wext[0:KWP, 0:1], bank[3][0:KWP, 0:A], AX.X, ALU.max)
            link(v.tensor_reduce(wext[0:KWP, 1:2], bank[3][0:KWP, 0:A], AX.X, ALU.min, negate=True))
            v.tensor_reduce(wabs[0:KWP, :], wext[0:KWP, :], AX.X, ALU.max).then_inc(s["scale_in"], 1)
            v.wait_ge(s["scale_mm"], 1)
            link(v.tensor_reduce(wrow[:, :], bank[0][0:1, 0:P], AX.X, ALU.max))
            v.tensor_scalar(wrow[:, :], wrow[:, :], 1e-30, None, ALU.max).then_inc(s["scale_in"], 1)
            v.wait_ge(s["scale_mm"], 2)
            link(v.tensor_copy(wmax[:, :], bank[0][:, 0:1]))
            v.tensor_scalar(wback[:, :], wmax[:, :], 1.0 / (WTOP * PSCALE), None, ALU.mult)
            link(v.reciprocal(wscale[:, :], wmax[:, :]))
            v.tensor_scalar(comb[0:KWP, :], bank[3][0:KWP, 0:A], wscale[0:KWP, 0:1], WTOP, ALU.mult,
                            ALU.mult).then_inc(s["comb_rdy"], 1)
            v.wait_ge(s["enc_mm"], 1)
            v.tensor_scalar(enc[:, :], bank[2][:, :], bacol[:, 0:1], None, ALU.add).then_inc(s["enc_used"], 1)
            v.wait_ge(s["x_in"], 16 * NT)
            for i in range(NT):
                tile_stats(i)
            layernorm_stats(1)
            layernorm_apply(1)
            v.wait_ge(s["w_in"], 16 * NW)
            v.tensor_scalar(wasT[:, :, :], wasT[:, :, :], 0.5, None, ALU.mult)
            v.tensor_scalar(lsyT[:, :], lsyT[:, :], 0.5, None, ALU.mult)
            v.tensor_scalar(lgs[:, 2 * HS:3 * HS], lgs[:, 2 * HS:3 * HS], 2.0, None, ALU.mult)
            v.tensor_copy(lens_f[:, :], lens_i[:, :])
            for g in (0, 1, 3):
                v.tensor_scalar(lss[:, g * HS:(g + 1) * HS], lss[:, g * HS:(g + 1) * HS], 0.5, None, ALU.mult)
            link(v.memset(nmax[:, :], 0.0))
            v.tensor_scalar(maskb[:, :], cn("tcount", B), lens_f[:, 0:1], NEG, ALU.is_ge, ALU.mult).then_inc(s["w_ready"], 1)
            cflat = ctxP[:, :, :].rearrange("p j d -> p (j d)")
            v.tensor_scalar(cflat, cflat, 1.0 / PSCALE, None, ALU.mult).then_inc(s["ctx_rest"], 1)
            v.wait_ge(s["toep_hi"], 1)
            v.tensor_tensor(toep[T:P, :], tr_f[T:P, :], toep[T:P, :], ALU.subtract).then_inc(s["toep_rest"], 1)
            v.wait_ge(s["ctx_hi"], 1)
            v.tensor_tensor(ctxr[:, :], cflat, ctx3[:, 0, :], ALU.subtract).then_inc(s["ctx_rest"], 1)
            for n in range(4):
                gp, hf = n // 2, n % 2
                v.wait_ge(s["pre_mm"], n + 1)
                for h in range(2):
                    g, rows = 2 * gp + h, slice(h * HS, (h + 1) * HS)
                    ins = v.tensor_scalar(pre[:, hf * 32:(hf + 1) * 32, g, :],
                                          bank[4 + n][rows, :].rearrange("p (l b) -> p l b", b=B), gsb[rows, g:g + 1],
                                          2.0 if g == 2 else 1.0, ALU.add, ALU.mult)
                ins.then_inc(s["pre_used"], 1)
                if n == 0:
                    v.wait_ge(s["ctx_hi"], 2)
                    v.tensor_tensor(ctx3[:, 2, :], ctxr[:, :], ctx3[:, 1, :], ALU.subtract).then_inc(s["ctx_rest"], 1)

            def encoder_location(n):
                u0, u1 = GROUPS[n]
                return v.scalar_tensor_tensor(encloc[:, u0 * B:u1 * B], loc(u0, u1), wback[:, 0:1], enc[:, u0 * B:u1 * B],
                                              ALU.mult, ALU.add)

            v.wait_ge(s["loc_rdy"], 2)
            for n in range(2):
                link(encoder_location(n))
            base = ch[0]
            PER = 4
            UA = GROUPS[1][0]
            with v.Fori(0, L // 2) as l2:
                for l in (2 * l2, 2 * l2 + 1):
                    k = [0]

                    def note(ins):
                        k[0] += 1
                        ins.then_inc(s["dchain"], 1)

                    def clink(ins):
                        note(ins)
                        v.wait_ge(s["dchain"], base + l * PER + k[0])

                    v.wait_ge(s["sw_rdy"], l + 1)
                    for n, (u0, u1) in enumerate(CHUNKS):
                        if u0 == UA:
                            v.wait_ge(s["dchain"], base + l * PER)
                        sl = slice(u0 * B, u1 * B)
                        v.tensor_tensor(pact[:, sl].rearrange("p (u b) -> p u b", b=B),
                                        encloc[:, sl].rearrange("p (u b) -> p u b", b=B),
                                        SW.unsqueeze(1).broadcast_to([P, u1 - u0, B]), ALU.add).then_inc(s["pact_rdy"], 1)
                    v.wait_ge(s["eb_rdy"], l + 1)
                    v.tensor_reduce(nmax[:, :], EB[0:B, 0:T], AX.X, ALU.max, negate=True).then_inc(s["nmax_rdy"], 1)
                    v.wait_ge(s["p_rdy"], l + 1)
                    clink(v.reciprocal(rinv[:, :], psum_e[:, :]))
                    v.tensor_scalar(pn[0:B, :].rearrange("p (r t) -> p r t", r=2), prob[:, :].unsqueeze(1).broadcast_to([B, 2, T]),
                                    rinv[:, 0:1], PSCALE, ALU.mult, ALU.mult).then_inc(s["r_rdy"], 1)
                    v.wait_ge(s["at_rdy"], l + 1)
                    v.tensor_copy(al2[:, 0, :], AT[:, 0:B]).then_inc(s["al_rdy"], 1)
                    halves = [(slice(h * T, (h + 1) * T), slice(h * 8, (h + 1) * 8)) for h in range(2)]
                    for r_, b_ in halves:
                        v.tensor_copy(ae[r_, 0, b_], AT[r_, b_])
                    v.wait_ge(s["al_rdy"], 2 * l + 1)
                    for r_, b_ in halves:
                        ins = v.tensor_tensor(ae[r_, 1, b_], AT[r_, b_], al2[r_, 0, b_], ALU.subtract)
                    ins.then_inc(s["ae_rdy"], 1)
                    v.tensor_tensor(al2[:, 1, :], AT[:, 0:B], al2[:, 0, :], ALU.subtract).then_inc(s["al_rdy"], 1)
                    v.wait_ge(s["gt_rdy"], l + 1)
                    v.wait_ge(s["ghist_rdy"], l + 1)
                    v.tensor_reduce(gT[:, :], GT[:, 0:2 * B].rearrange("p (s b) -> p b s", s=2), AX.X,
                                    ALU.add).then_inc(s["gT_rdy"], 1)
                    v.wait_ge(s["loc_rdy"], 2 * l + 3)
                    note(encoder_location(0))
                    v.wait_ge(s["tg_rdy"], 2 * l + 1)
                    v.scalar_tensor_tensor(la[:, :], tg[:, 0, :], 1.0, tg[:, 2, :], ALU.add, ALU.mult)
                    clink(v.scalar_tensor_tensor(lb[:, :], tg[:, 1, :], 1.0, c2[:, :], ALU.add, ALU.mult))
                    v.scalar_tensor_tensor(c2[:, :], lb[:, :], 0.5, la[:, :], ALU.mult, ALU.add).then_inc(s["c2_rdy"], 1)
                    v.wait_ge(s["tg_rdy"], 2 * l + 2)
                    v.wait_ge(s["tc_rdy"], l + 1)
                    v.wait_ge(s["shist_rdy"], l + 1)
                    v.scalar_tensor_tensor(s2[:, :], tg[:, 3, :], 1.0, tc[:, :], ALU.add, ALU.mult).then_inc(s["s_rdy"], 1)
                    v.wait_ge(s["loc_rdy"], 2 * l + 4)
                    note(encoder_location(1))
                    assert k[0] == PER
            ch[0] += L * PER
            for i in range(NT):
                v.wait_ge(s["y_mm"], i + 1)
                ins = v.scalar_tensor_tensor(xres[:, i, :], bank[i % 2][:, :], gates_g[:, 0:1], xres[:, i, :], ALU.mult,
                                             ALU.add)
                ins.then_inc(s["x1_rdy"], 1)
                if i > 0:
                    v.wait_ge(s["x1_rdy"], i)
                    tile_stats(i - 1)
            v.wait_ge(s["x1_rdy"], NT)
            tile_stats(NT - 1)
            link(v.tensor_scalar(halfg[:, :], gates_g[:, :], 0.5, None, ALU.mult))

            def shared_step(m, n):
                mo = MOES[m]
                q = lambda n: s[f"{mo.tag}_{n}"]
                p_, o_ = n % 2, (n - 1) % 2
                if n > 0:
                    v.wait_ge(q("sh_zt"), n)
                    v.tensor_copy(zT[o_][:, :, :], bank[2][:, 0:256].rearrange("p (c t) -> p c t", c=2)).then_inc(q("sh_ztr"), 1)
                if n < NT * mo.shared:
                    v.wait_ge(q("sh_th"), n + 1)
                    link(v.scalar_tensor_tensor(ga[p_][:, :], gth[p_][:, :], 1.0, bank[p_][:, 0:256], ALU.add, ALU.mult))
                    v.tensor_tensor(zb[p_][:, :], ga[p_][:, :], bank[p_][:, 256:512], ALU.mult).then_inc(q("sh_z"), 1)
                if n > 0:
                    i = (n - 1) % NT
                    v.wait_ge(q("sh_o"), n)
                    if n > NT:
                        v.wait_ge(q("sh_x"), n - NT)
                    v.scalar_tensor_tensor(xres[:, i, :], bank[3 + o_][:, :], halfg[:, 2 + m:3 + m], xres[:, i, :],
                                           ALU.mult, ALU.add).then_inc(q("sh_x"), 1)

            def route(m):
                mo = MOES[m]
                K, NB, NK = mo.K, mo.NB, NT * mo.K
                q = lambda n: s[f"{mo.tag}_{n}"]
                g_ffn = gates_g[:, 2 + m:3 + m]
                if m == 0:
                    v.wait_ge(q("act_done"), 3)
                    link(v.tensor_scalar(sc2[:, :, :], sc[:, :, :], 0.5, 0.5, ALU.mult, ALU.add))
                    link(v.tensor_tensor(sc[:, :, :], sc2[:, :, :], bias0[:, :].unsqueeze(1).broadcast_to([P, NT, E]),
                                         ALU.add))
                else:
                    v.wait_ge(q("logit_mm"), 3)
                    lg = bank[6][:, 0:NT * E].rearrange("p (i e) -> p i e", e=E)
                    link(v.tensor_reduce(smax[:, :], lg, AX.X, ALU.max))
                    v.tensor_tensor(sc2[:, :, :], lg, smax[:, :].unsqueeze(2).broadcast_to([P, NT, E]),
                                    ALU.subtract).then_inc(s["exp_in"], 1)
                    v.wait_ge(q("act_done"), 3)
                    link(v.tensor_reduce(wsum[:, :], sc[:, :, :], AX.X, ALU.add))
                    link(v.reciprocal(winv[:, :], wsum[:, :]))
                    link(v.tensor_tensor(sc[:, :, :], sc[:, :, :], winv[:, :].unsqueeze(2).broadcast_to([P, NT, E]), ALU.mult))
                for i in range(NT):
                    ins = v.max(top8[:, i, :], sc[:, i, :])
                link(ins)
                shared_step(m, 0)
                for i in range(NT):
                    ins = v.max_index(idx8[:, i, :], top8[:, i, :], sc[:, i, :])
                link(ins)
                link(v.tensor_copy(idxf[:, 0:NK].rearrange("p (i k) -> p i k", k=K), idx8[:, :, 0:K]))
                oh = onehot[:, 0:NK, :]
                link(v.tensor_tensor(oh, cn("iota")[:, 0:E].unsqueeze(1).broadcast_to([P, NK, E]),
                                     idxf[:, 0:NK].unsqueeze(2).broadcast_to([P, NK, E]), ALU.is_equal))
                v.tensor_reduce(msum[:, :, :], oh.rearrange("p (i k) e -> p i e k", k=K), AX.X,
                                ALU.add).then_inc(q("route_oh"), 1)
                link(v.tensor_reduce(wsum[:, :], top8[:, :, 0:K], AX.X, ALU.add))
                if m == 0:
                    link(v.tensor_scalar(wsum[:, :], wsum[:, :], 1e-20, None, ALU.add))
                link(v.reciprocal(winv[:, :], wsum[:, :]))
                link(v.tensor_scalar(winv[:, :], winv[:, :], g_ffn, None, ALU.mult))
                link(v.tensor_tensor(wk[:, :, 0:K], top8[:, :, 0:K], winv[:, :].unsqueeze(2).broadcast_to([P, NT, K]), ALU.mult))
                shared_step(m, 1)
                pos = bank[7][:, 0:NT * E].rearrange("p (i e) -> p i e", e=E)
                tot = bank[7][:, NT * E:2 * NT * E].rearrange("p (i e) -> p i e", e=E)
                v.wait_ge(q("pos_mm"), 1)
                link(v.memset(cum[:, 0, :], 0.0))
                for i in range(1, NT):
                    link(v.tensor_tensor(cum[:, i, :], cum[:, i - 1, :], tot[:, i - 1, :], ALU.add))
                link(v.tensor_tensor(count[:, :], cum[:, NT - 1, :], tot[:, NT - 1, :], ALU.add))
                link(v.tensor_scalar(nblk_i[:, :], count[:, :], float(P - 1), None, ALU.add))
                link(v.tensor_scalar(nblk_j[:, :], nblk_i[:, :], 7, None, ALU.arith_shift_right))
                link(v.tensor_copy(nblk[:, :], nblk_j[:, :]))
                link(v.tensor_tensor(trib[:, :, :], nblk[:, :].unsqueeze(1).broadcast_to([P, E, E]),
                                     cn("tri").rearrange("p (a b) -> p a b", a=E), ALU.mult))
                link(v.tensor_reduce(bstart[:, :], trib[:, :, :], AX.X, ALU.add))
                link(v.tensor_tensor(bend[:, :], bstart[:, :], nblk[:, :], ALU.add))
                link(v.tensor_tensor(ecmp[:, 0:NB, :], bend[:, :].unsqueeze(1).broadcast_to([P, NB, E]),
                                     cn("iota")[:, 0:NB].unsqueeze(2).broadcast_to([P, NB, E]), ALU.is_le))
                link(v.tensor_reduce(ebf[:, 0:NB], ecmp[:, 0:NB, :], AX.X, ALU.add))
                v.tensor_scalar(ebi[:, 0:NB], ebf[:, 0:NB], float(E - 1), None, ALU.min).then_inc(q("eb_rdy"), 1)
                shared_step(m, 2)
                link(v.scalar_tensor_tensor(place[:, :, :], bstart[:, :].unsqueeze(1).broadcast_to([P, NT, E]), float(P),
                                            cum[:, :, :], ALU.mult, ALU.add))
                link(v.tensor_tensor(place[:, :, :], place[:, :, :], pos, ALU.add))
                for k in range(K):
                    ins = v.tensor_tensor(ohs[:, 0:NK, :].rearrange("p (i k) e -> p i k e", k=K)[:, :, k, :],
                                          oh.rearrange("p (i k) e -> p i k e", k=K)[:, :, k, :], place[:, :, :], ALU.mult)
                link(ins)
                link(v.tensor_reduce(slotf[:, 0:NK], ohs[:, 0:NK, :], AX.X, ALU.add))
                link(v.tensor_copy(sloti[:, 0:NK], slotf[:, 0:NK]))
                v.tensor_scalar(slow_i[:, 0:NK], sloti[:, 0:NK], P - 1, None, ALU.bitwise_and)
                link(v.tensor_scalar(shigh_i[:, 0:NK], sloti[:, 0:NK], 7, None, ALU.arith_shift_right))
                v.tensor_copy(slow[:, 0:NK], slow_i[:, 0:NK])
                v.tensor_copy(shigh[:, 0:NK], shigh_i[:, 0:NK]).then_inc(q("place_rdy"), 1)
                v.wait_ge(q("place_rdy"), 1)
                shared_step(m, 3)
                for n in range(NK):
                    if n in (NK // 4, NK // 2, 3 * NK // 4):
                        shared_step(m, 3 + 4 * n // NK)
                    v.tensor_scalar(highhot[:, n, 0, 0:NB], cn("iota")[:, 0:NB], shigh[:, n:n + 1], cn("prow"),
                                    ALU.is_equal, ALU.mult)
                    v.tensor_scalar(lowhot[:, n, :], cn("iota"), slow[:, n:n + 1], None, ALU.is_equal).then_inc(q("low_rdy"), 1)
                shared_step(m, 7)
                v.wait_ge(q("hot_mm"), NK)
                link(v.tensor_copy(tlf[:, 0:NB], bank[6][:, 0:NB]))
                v.scalar_tensor_tensor(tli[:, 0:NB], bank[6][:, NB:2 * NB], float(P), tlf[:, 0:NB], ALU.mult,
                                       ALU.add).then_inc(q("list_rdy"), 1)
                for n in range(8, NT * mo.shared + 1):
                    shared_step(m, n)

            def experts(m):
                mo = MOES[m]
                I, IC = mo.I, mo.IC
                q = lambda n: s[f"{mo.tag}_{n}"]
                base = ch[0]

                def inner(b):
                    v.wait_ge(q("th_rdy"), b.n + 1)
                    v.scalar_tensor_tensor(ga[b.par][:, 0:I], gth[b.par][:, 0:I], 1.0, bank[2 + b.par][:, 0:I], ALU.add,
                                           ALU.mult).then_inc(s["dchain"], 1)
                    v.wait_ge(s["dchain"], base + 1 + b.n)
                    v.tensor_tensor(zb[b.par][:, 0:I], ga[b.par][:, 0:I], bank[2 + b.par][:, I:2 * I], ALU.mult).then_inc(q("z_rdy"), 1)

                def outer(b):
                    v.wait_ge(q("zt_mm"), b.n + 1)
                    v.tensor_copy(zT[b.par][:, 0:IC, :], bank[4][:, 0:I].rearrange("p (c t) -> p c t", c=IC)).then_inc(q("zt_rdy"), 1)

                def step(b, first=False):
                    if not first:
                        outer(b.next(-1))
                    inner(b)

                step(Turn(0, 0), first=True)
                with v.Fori(0, (mo.NB - 3) // 4) as j:
                    for c_ in range(1, 5):
                        step(Turn(j, c_))
                step(Turn(0, mo.NB - 2))
                step(Turn(0, mo.NB - 1))
                outer(Turn(0, mo.NB - 1))
                ch[0] += mo.NB

            def combine(m):
                mo = MOES[m]
                q = lambda n: s[f"{mo.tag}_{n}"]
                v.wait_ge(q("sh_x"), NT * mo.shared)
                for n in range(NT * mo.K):
                    i, k = n // mo.K, n % mo.K
                    v.wait_ge(q(f"yg_in{n % NYG}"), 16 * (n // NYG + 1))
                    if k > 0:
                        v.wait_ge(q("yg_used"), n)
                    ins = v.scalar_tensor_tensor(xres[:, i, :], yrow[n % NYG][:, :], wk[:, i, k:k + 1], xres[:, i, :],
                                                 ALU.mult, ALU.add)
                    ins.then_inc(q("yg_used"), 1)
                    if m == 0 and k == mo.K - 1:
                        v.wait_ge(q("yg_used"), n + 1)
                        tile_stats(i)

            def attention():
                def scores(n, par):
                    v.wait_ge(s["as_mm"], n + 1)
                    v.wait_ge(s["aexp_rdy"], n + 1)
                    sb_ = bank[par][:, :].rearrange("p (g t) -> p g t", g=G)
                    v.tensor_tensor(sm[par][:, :, :], sb_, amask[:, :].unsqueeze(1).broadcast_to([P, G, T]),
                                    ALU.add).then_inc(s["smx_rdy"], 1)
                    v.wait_ge(s["smx_rdy"], n + 1)
                    v.tensor_reduce(amax[par][:, :], sm[par][:, :, :], AX.X, ALU.max, negate=True).then_inc(s["am_rdy"], 1)

                def norm(n, par, b, rp):
                    v.wait_ge(s["ao_mm"], n + 5)
                    v.reciprocal(arec[par][:, :], bank[4 + par][:, P:2 * P]).then_inc(s["ao_used"], 1)
                    v.wait_ge(s["ao_used"], 2 * n + 5)
                    dst = attT[:, :, :].rearrange("p r (l b) -> p b r l", b=B)[:, bass.ds(b, 1), 2 * rp:2 * rp + 2, :]
                    v.scalar_tensor_tensor(dst.rearrange("p x r l -> p (x r) l"), bank[4 + par][:, 0:P].rearrange("p (r l) -> p r l", r=2),
                                           gates_g[:, 1:2], arec[par][:, :].rearrange("p (r l) -> p r l", r=2), ALU.mult,
                                           ALU.mult).then_inc(s["ao_used"], 1)

                def step(n, q_, b, first=False, last=False):
                    if not last:
                        scores(n, q_ % 2)
                    if not first:
                        norm(n - 2, q_ % 2, b - 1, q_ % 2)

                N = 2 * B
                v.wait_ge(s["l_in"], 16 * NL)
                v.sem_inc(s["ao_used"], 4)
                for n in range(2):
                    step(n, n, 0, first=True)
                with v.Fori(0, (N - 4) // 4) as j:
                    for q_ in range(4):
                        step(4 * j + 2 + q_, q_, 2 * j + 1 + q_ // 2)
                for n in range(N - 2, N + 2):
                    step(n, n, n // 2, last=n >= N)
                for i in range(NT):
                    v.wait_ge(s["attb_mm"], i + 1)
                    x_i = xres[:, i, :].rearrange("p (g r d) -> p g r d", g=G, r=R)
                    v.tensor_tensor(x_i, bank[i % 2][:, :].rearrange("p (r g d) -> p g r d", g=G, r=R), x_i,
                                    ALU.add).then_inc(s["att_x"], 1)
                    if i > 0:
                        v.wait_ge(s["att_x"], i)
                        tile_stats(i - 1)
                v.wait_ge(s["att_x"], NT)
                tile_stats(NT - 1)

            layernorm_stats(2)
            layernorm_apply(2)
            route(0)
            experts(0)
            combine(0)
            layernorm_stats(3)
            layernorm_apply(3)
            attention()
            layernorm_stats(4)
            layernorm_apply(4)
            route(1)
            experts(1)
            combine(1)

        @block.gpsimd
        def _(g):
            def rstds(n):
                g.wait_ge(s["stat_rdy"], n)
                g.tensor_tensor(rstd[:, :], vareps[:, :], cn("half")[:, 0:NT], ALU.pow).then_inc(s["rstd_rdy"], 1)
            g.wait_ge(s["e_in"], 16 * NE)
            rstds(1)
            g.wait_ge(s["pre_used"], 4)
            g.wait_ge(s["init_rdy"], 1)
            g.memset(shist[:, 0, :], 0.0).then_inc(s["shist_rdy"], 1)
            g.memset(ghist[:, 0, :], 0.0).then_inc(s["ghist_rdy"], 1)
            g.wait_ge(s["pb_free"], 1)
            g.tensor_copy(prebuf[:, :, :], pre[:, 0, :, :]).then_inc(s["prebuf_rdy"], 1)

            def keep(l):
                g.wait_ge(s["gT_rdy"], l + 1)
                g.tensor_copy(ghist[:, l, :], gT[:, :]).then_inc(s["ghist_rdy"], 1)
                g.wait_ge(s["s_rdy"], l + 2)
                g.tensor_copy(shist[:, l + 1, :], s2[:, :]).then_inc(s["shist_rdy"], 1)

            with g.Fori(0, L - 1) as l:
                g.wait_ge(s["pb_free"], l + 2)
                g.tensor_copy(prebuf[:, :, :], pre[:, l + 1, :, :]).then_inc(s["prebuf_rdy"], 1)
                keep(l)
            keep(L - 1)

            def gathers(m):
                mo = MOES[m]
                NB = mo.NB
                q = lambda n: s[f"{mo.tag}_{n}"]
                g.wait_ge(q("place_rdy"), 1)
                for n in range(NT * mo.K):
                    g.tensor_scalar(highhot[:, n, 1, 0:NB], cn("iota")[:, 0:NB], shigh[:, n:n + 1], float(n // mo.K),
                                    ALU.is_equal, ALU.mult).then_inc(q("high_rdy"), 1)
                g.wait_ge(q("list_rdy"), 1)
                g.wait_ge(q("hid_st"), 16 * NT)

                for b in range(mo.NB):
                    g.wait_ge(q("xt_mm"), b + 1)
                    g.indirect_dma_start(out=xg[b % 2][:, :], out_offset=None, in_=hd[m],
                                         in_offset=bass.IndirectOffsetOnAxis(ap=tli[:, b:b + 1], axis=0)).then_inc(q(f"xg_in{b % 2}"), 16)
                for par in range(2):
                    g.wait_ge(q(f"ob_st{par}"), 16 * (mo.NB // 2 + 2 - par))
                for n in range(NT * mo.K):
                    if n >= NYG:
                        g.wait_ge(q("yg_used"), n - NYG + 1)
                    g.indirect_dma_start(out=yrow[n % NYG][:, :], out_offset=None, in_=yd[m],
                                         in_offset=bass.IndirectOffsetOnAxis(ap=sloti[:, n:n + 1], axis=0)).then_inc(q(f"yg_in{n % NYG}"), 16)

            def attention_operands():
                qT = hidT[:, :, :].rearrange("p c t -> p (c t)").rearrange("p (b x) -> p b x", b=B)

                def keys(b, par):
                    g.tensor_tensor(kb[par][:, :, :], ctxT[:, :, bass.ds(b, 1)].rearrange("p t x -> p x t").broadcast_to([P, G, T]),
                                    cn("gmask").unsqueeze(2).broadcast_to([P, G, T]), ALU.mult)

                def queries(b, par):
                    g.tensor_copy(qb[par][:, :], qT[:, bass.ds(b, 1), :].rearrange("p x y -> p (x y)")).then_inc(s["qk_rdy"], 1)

                def values(b, par):
                    g.tensor_tensor(vb[par][:, :], ctxD[:, bass.ds(b, 1), :].rearrange("p x y -> p (x y)"), cn("vmask"),
                                    ALU.mult).then_inc(s["v_rdy"], 1)

                for b in range(2):
                    keys(b, b)
                    values(b, b)
                g.wait_ge(s["tr_used"], 3 * NT)
                for b in range(2):
                    queries(b, b)
                with g.Fori(0, B // 2 - 1) as j:
                    for par in range(2):
                        b = 2 * j + 2 + par
                        g.wait_ge(s["as_mm"], 4 * j + 2 + 2 * par)
                        keys(b, par)
                        queries(b, par)
                        g.wait_ge(s["ao_mm"], 4 * j + 6 + 2 * par)
                        values(b, par)

            rstds(2)
            gathers(0)
            g.wait_ge(s["l_in"], 16 * NL)
            rstds(3)
            attention_operands()
            rstds(4)
            gathers(1)

        @block.scalar
        def _(c):
            def transposed(n):
                for i in range(NT):
                    c.wait_ge(s["tr_rdy"], (n - 1) * NT + i + 1)
                    src = bank[i % 2][:, :].rearrange("p (c t) -> p c t", c=HC)
                    if n == 3:
                        dst = hidT[:, :, :].rearrange("p c t -> p (c t)").rearrange(
                            "p (b c l) -> p c l b", b=B, c=HC)[:, :, i * 8:(i + 1) * 8, :]
                        for k in range(HC):
                            ins = c.copy(dst[:, k], src[:, k].rearrange("p (l b) -> p l b", b=B))
                        ins.then_inc(s["tr_used"], 1)
                    else:
                        c.copy(hidT[:, :, i * P:(i + 1) * P], src).then_inc(s["tr_used"], 1)

            c.preload_act_table(ACT.Tanh)
            transposed(1)
            c.wait_ge(s["toep_in"], 32)
            c.copy(toep[:, :], tr_f[:, :]).then_inc(s["toep_hi"], 1)
            c.wait_ge(s["w_in"], 16 * NW)
            c.activation(gates_g[:, :], gates_g[:, :], ACT.Tanh)
            c.wait_ge(s["ctx_rest"], 1)
            c.copy(ctx3[:, 0, :], ctxP[:, :, :].rearrange("p j d -> p (j d)")).then_inc(s["ctx_hi"], 1)
            c.wait_ge(s["ctx_rest"], 2)
            c.copy(ctx3[:, 1, :], ctxr[:, :]).then_inc(s["ctx_hi"], 1)
            with c.Fori(0, L // 2) as l2:
                for l in (2 * l2, 2 * l2 + 1):
                    for n, (u0, u1) in enumerate(CHUNKS):
                        c.wait_ge(s["pact_rdy"], len(CHUNKS) * l + n + 1)
                        c.activation(th[:, u0 * B:u1 * B], pact[:, u0 * B:u1 * B], ACT.Tanh).then_inc(s["th_rdy"], 1)
                    c.wait_ge(s["nmax_rdy"], l + 1)
                    c.activation(prob[:, :], EB[0:B, 0:T], ACT.Exp, bias=nmax[:, 0:1],
                                 accum_out=psum_e[:, :]).then_inc(s["p_rdy"], 1)
                    c.wait_ge(s["rg_rdy"], 2 * l + 1)
                    c.activation(tg[:, 0:3, :], RG[0:HS, 0:3 * B].rearrange("p (g b) -> p g b", g=3), ACT.Tanh,
                                 scale=0.5).then_inc(s["tg_rdy"], 1)
                    c.wait_ge(s["rg_rdy"], 2 * l + 2)
                    c.activation(tg[:, 3, :], gate(3), ACT.Tanh, scale=0.5).then_inc(s["tg_rdy"], 1)
                    c.wait_ge(s["c2_rdy"], l + 1)
                    c.activation(tc[:, :], c2[:, :], ACT.Tanh, scale=0.5).then_inc(s["tc_rdy"], 1)
            for n in range(2):
                c.wait_ge(s["yg_mm"], n + 1)
                c.activation(yg[0:HS, n * 512:(n + 1) * 512], bank[2 + n][0:HS, :], ACT.Tanh,
                             bias=gyb[:, 0:1]).then_inc(s["yg_rdy"], 1)


            def mixture(m):
                mo = MOES[m]
                I = mo.I
                q = lambda n: s[f"{mo.tag}_{n}"]
                lg = bank[6][:, 0:NT * E].rearrange("p (i e) -> p i e", e=E)
                for hf in range(2):
                    c.wait_ge(q("logit_mm"), hf + 1)
                    c.copy(lgT[hf][0:E, :], bank[4 + hf][0:E, :]).then_inc(q("act_done"), 1)
                if m == 0:
                    c.wait_ge(q("logit_mm"), 3)
                    c.activation(sc[:, :, :], lg, ACT.Tanh, scale=0.5).then_inc(q("act_done"), 1)
                else:
                    c.wait_ge(s["exp_in"], 1)
                    c.activation(sc[:, :, :], sc2[:, :, :], ACT.Exp).then_inc(q("act_done"), 1)
                for n in range(NT * mo.shared):
                    c.wait_ge(q("sh_mm"), n + 1)
                    if n >= 2:
                        c.wait_ge(q("sh_z"), n - 1)
                    c.activation(gth[n % 2][:, :], bank[n % 2][:, 0:256], ACT.Tanh, scale=0.5).then_inc(q("sh_th"), 1)

                def turned(b):
                    c.wait_ge(q("xt_mm"), b.n + 3)
                    c.copy(xgT[b.par][:, :, :], bank[b.par][:, :].rearrange("p (c t) -> p c t", c=HC)).then_inc(q("xt_rdy"), 1)

                def inner(b):
                    c.wait_ge(q("h_mm"), b.n + 1)
                    c.activation(gth[b.par][:, 0:I], bank[2 + b.par][:, 0:I], ACT.Tanh, scale=0.5).then_inc(q("th_rdy"), 1)

                def out_(b):
                    c.wait_ge(q("o_mm"), b.n + 5)
                    c.wait_ge(q(f"ob_st{b.par}"), 16 * (b.h + 1))
                    c.mul(ob[b.par][:, :], bank[5][:, :], 0.5).then_inc(q("ob_rdy"), 1)

                def step(b, first=False, last=False):
                    if not last:
                        turned(b.next())
                    inner(b)
                    if not first:
                        out_(b.next(-1))

                for par in range(2):
                    c.sem_inc(q(f"ob_st{par}"), 16)
                c.sem_inc(q("ob_rdy"), 1)
                turned(Turn(0, 0))
                step(Turn(0, 0), first=True)
                with c.Fori(0, (mo.NB - 3) // 4) as j:
                    for c_ in range(1, 5):
                        step(Turn(j, c_))
                step(Turn(0, mo.NB - 2))
                step(Turn(0, mo.NB - 1), last=True)
                out_(Turn(0, mo.NB - 1))

            def attention():
                def probs(n, par):
                    c.wait_ge(s["am_rdy"], n + 1)
                    for g_ in range(G):
                        ins = c.activation(ap_[par][:, g_ * T:(g_ + 1) * T], sm[par][:, g_, :], ACT.Exp, bias=amax[par][:, g_:g_ + 1])
                    ins.then_inc(s["aexp_rdy"], 1)

                def turned(n, par):
                    c.wait_ge(s["at_mm"], n + 1)
                    c.copy(aT[par][:, :, :], bank[2 + par][:, :].rearrange("p (c t) -> p c t", c=4)).then_inc(s["aT_rdy"], 1)

                def step(n, q_, first=False, last=False):
                    if not last:
                        probs(n, q_ % 2)
                    if not first:
                        turned(n - 1, (q_ + 1) % 2)

                N = 2 * B
                c.sem_inc(s["aexp_rdy"], 2)
                for n in range(2):
                    step(n, n, first=n == 0)
                with c.Fori(0, (N - 4) // 4) as j:
                    for q_ in range(4):
                        step(4 * j + 2 + q_, q_)
                for n in range(N - 2, N + 1):
                    step(n, n, last=n >= N)

            transposed(2)
            mixture(0)
            transposed(3)
            attention()
            transposed(4)
            mixture(1)

        @block.tensor
        def _(t):
            def turn_hidden(n):
                for i in range(NT):
                    t.wait_ge(s["hid_rdy"], (n - 1) * NT + i + 1)
                    if i >= 2:
                        t.wait_ge(s["tr_used"], (n - 1) * NT + i - 1)
                    for c in range(HC):
                        ins = t.transpose(bank[i % 2][:, c * P:(c + 1) * P], hid[:, i, c * P:(c + 1) * P], ident)
                    ins.then_inc(s["tr_rdy"], 1)

            t.wait_ge(s["e_in"], 16 * NE)
            t.matmul(bank[3][0:KWP, 0:A], convp[:, :], wafT[:, :], start=True, stop=True).then_inc(s["toep_mm"], 1)
            for t2 in range(2):
                ins = t.matmul(bank[2][t2 * A:(t2 + 1) * A, :], wahT[:, :], ctxT[:, 1 - t2:T:2, :], start=True, stop=True)
            ins.then_inc(s["enc_mm"], 1)
            t.wait_ge(s["scale_in"], 1)
            t.transpose(bank[0][0:1, 0:P], wabs[:, :], ident).then_inc(s["scale_mm"], 1)
            t.wait_ge(s["scale_in"], 2)
            t.matmul(bank[0][:, 0:1], cn("ones", 1), wrow[:, :], start=True, stop=True).then_inc(s["scale_mm"], 1)
            turn_hidden(1)
            t.wait_ge(s["w_ready"], 1)
            t.wait_ge(s["tr_used"], NT)
            for n in range(4):
                gp, hf = n // 2, n % 2
                for c in range(HC):
                    ins = t.matmul(bank[4 + n][:, :], lys[:, c, gp * 2 * HS:(gp + 1) * 2 * HS],
                                   hidT[:, c, hf * 512:(hf + 1) * 512], start=(c == 0), stop=(c == HC - 1))
                ins.then_inc(s["pre_mm"], 1)
            t.wait_ge(s["pre_used"], 4)
            t.wait_ge(s["enc_used"], 1)
            t.wait_ge(s["comb_rdy"], 1)
            t.wait_ge(s["ctx_rest"], 3)
            t.wait_ge(s["toep_rest"], 1)
            t.transpose(bank[7][0:B, 0:B], ident[0:B, 0:B], ident[0:B, 0:B]).then_inc(s["pb_free"], 1)
            FIRST = [u0 for u0, _ in GROUPS]

            def locations(us, hi=True, lo=True):
                for u in us:
                    w = slice((NU - 1 - u) * P, (NU - u) * P)
                    dst = loc(u, u + 1)
                    if hi:
                        ins = t.matmul(dst, toep[:, w], al2[:, 0, :], start=(u in FIRST), stop=False)
                    if lo:
                        ins = t.matmul(dst, toep[:, w], al2[:, 1, :], start=False, stop=(u + 1 in FIRST or u == NU - 1))
                return ins

            U0 = 8
            UA = GROUPS[1][0]
            t.wait_ge(s["alT_rdy"], 1)
            locations(range(0, UA)).then_inc(s["loc_rdy"], 1)
            locations(range(UA, NU)).then_inc(s["loc_rdy"], 1)
            with t.Fori(0, L // 2) as l2:
                for l in (2 * l2, 2 * l2 + 1):
                    t.wait_ge(s["prebuf_rdy"], l + 1)
                    t.wait_ge(s["s_rdy"], l + 1)
                    t.matmul(SW, wasT[:, :, :].rearrange("p r a -> p (r a)"), s2[:, :], start=True,
                             stop=True).then_inc(s["sw_rdy"], 1)
                    t.matmul(EB[0:B, 0:T], ident[0:B, 0:B], maskb[:, :], start=True, stop=False)
                    for n, (u0, u1) in enumerate(CHUNKS):
                        t.wait_ge(s["th_rdy"], len(CHUNKS) * l + n + 1)
                        for u in range(u0, u1):
                            ins = t.matmul(EB[0:B, 2 * u:2 * u + 2], th[:, u * B:(u + 1) * B], va2[:, :], start=False, stop=(u == NU - 1))
                    ins.then_inc(s["eb_rdy"], 1)
                    t.matmul(RG[0:HS, 0:3 * B], ident[0:HS, 0:HS], prebuf[:, 0:3, :].rearrange("p g b -> p (g b)"), start=True, stop=False)
                    t.matmul(gate(3), ident[0:HS, 0:HS], prebuf[:, 3, :], start=True, stop=False)
                    for g in range(4):
                        ins = t.matmul(gate(g), lss[:, g * HS:(g + 1) * HS], s2[:, :], start=False, stop=False)
                    ins.then_inc(s["pb_free"], 1)
                    t.wait_ge(s["r_rdy"], l + 1)
                    t.transpose(AT[:, 0:P], pn[:, :], ident).then_inc(s["at_rdy"], 1)
                    t.wait_ge(s["al_rdy"], 2 * l + 1)
                    locations(range(0, U0), lo=False)
                    t.wait_ge(s["ae_rdy"], l + 1)
                    for j in range(8):
                        for k in range(3):
                            ins = t.matmul(GT[:, 0:2 * B].rearrange("p (s b) -> p s b", s=2)[:, :, j:B:8],
                                           ctx3[:, k, j * D:(j + 1) * D], ae[:, :, j:B:8], start=(k == 0), stop=(k == 2))
                    ins.then_inc(s["gt_rdy"], 1)
                    t.wait_ge(s["al_rdy"], 2 * l + 2)
                    locations(range(0, U0), hi=False)
                    locations(range(U0, UA)).then_inc(s["loc_rdy"], 1)
                    t.wait_ge(s["gT_rdy"], l + 1)
                    for g in range(4):
                        ins = t.matmul(gate(g), lgs[:, g * HS:(g + 1) * HS], gT[:, :], start=False, stop=(g >= 2))
                        if g >= 2:
                            ins.then_inc(s["rg_rdy"], 1)
                    locations(range(UA, NU)).then_inc(s["loc_rdy"], 1)
            t.wait_ge(s["ghist_rdy"], L + 1)
            t.wait_ge(s["shist_rdy"], L + 1)
            for n in range(2):
                t.matmul(bank[2 + n][0:HS, :], lgyT[:, :], ghist[:, n * 32:(n + 1) * 32, :], start=True, stop=False)
                t.matmul(bank[2 + n][0:HS, :], lsyT[:, :], shist[:, n * 32:(n + 1) * 32, :], start=False,
                         stop=True).then_inc(s["yg_mm"], 1)
            for i in range(NT):
                t.wait_ge(s["yg_rdy"], i // 4 + 1)
                if i >= 2:
                    t.wait_ge(s["x1_rdy"], i - 1)
                t.matmul(bank[i % 2][:, :], yg[:, i * P:(i + 1) * P], yyT[:, :], start=True, stop=True).then_inc(s["y_mm"], 1)

            def mixture(m):
                mo = MOES[m]
                I, IC, K, NB = mo.I, mo.IC, mo.K, mo.NB
                q = lambda n: s[f"{mo.tag}_{n}"]
                t.sem_inc(q("xt_mm"), 2)
                t.sem_inc(q("o_mm"), 4)
                for hf in range(2):
                    t.wait_ge(s["tr_used"], (2 * m + 1) * NT + (hf + 1) * NT // 2)
                    for c in range(HC):
                        ins = t.matmul(bank[4 + hf][0:E, :], gw[:, m, c, :], hidT[:, c, hf * 512:(hf + 1) * 512],
                                       start=(c == 0), stop=(c == HC - 1))
                    ins.then_inc(q("logit_mm"), 1)
                t.wait_ge(q("act_done"), 2)
                for i in range(NT):
                    ins = t.transpose(bank[6][:, i * E:(i + 1) * E], lgT[i // 4][0:E, (i % 4) * P:(i % 4 + 1) * P], ident[0:E, 0:E])
                ins.then_inc(q("logit_mm"), 1)

                def sh_in(n):
                    h, i, p_ = n // NT, n % NT, n % 2
                    t.wait_ge(q("sw_in"), 32 * mo.shared)
                    if n >= 2:
                        t.wait_ge(q("sh_z"), n - 1)
                    for c in range(HC):
                        ins = t.matmul(bank[p_][:, :], hidT[:, c, i * P:(i + 1) * P], wbuf1[4 - mo.shared + h][:, c, :], start=(c == 0),
                                       stop=(c == HC - 1))
                    ins.then_inc(q("sh_mm"), 1)

                def sh_turn(n):
                    t.wait_ge(q("sh_z"), n + 1)
                    if n >= 1:
                        t.wait_ge(q("sh_ztr"), n)
                    for c in range(2):
                        ins = t.transpose(bank[2][:, c * P:(c + 1) * P], zb[n % 2][:, c * P:(c + 1) * P], ident)
                    ins.then_inc(q("sh_zt"), 1)

                def sh_out(n):
                    t.wait_ge(q("sh_ztr"), n + 1)
                    if n >= 2:
                        t.wait_ge(q("sh_x"), n - 1)
                    for c in range(2):
                        ins = t.matmul(bank[3 + n % 2][:, :], zT[n % 2][:, c, :], wbuf2[4 - mo.shared + n // NT][:, c, :], start=(c == 0),
                                       stop=(c == 1))
                    ins.then_inc(q("sh_o"), 1)

                def sh_step(n):
                    if n >= 1:
                        sh_turn(n - 1)
                    if n < NT * mo.shared:
                        sh_in(n)
                    if n >= 1:
                        sh_out(n - 1)

                sh_step(0)
                sh_step(1)
                t.wait_ge(q("route_oh"), 1)
                rhs = msum[:, :, :].rearrange("p i e -> p (i e)")
                t.matmul(bank[7][:, 0:NT * E], cn("before"), rhs, start=True, stop=True)
                t.matmul(bank[7][:, NT * E:2 * NT * E], cn("ones"), rhs, start=True, stop=True).then_inc(q("pos_mm"), 1)
                sh_step(2)
                sh_step(3)
                NK = NT * K
                for n in range(NK):
                    if n % (NK // 4) == 0:
                        sh_step(4 + 4 * n // NK)
                    t.wait_ge(q("low_rdy"), n + 1)
                    t.wait_ge(q("high_rdy"), n + 1)
                    t.matmul(bank[6][:, 0:2 * NB], lowhot[:, n, :], highhot[:, n, :, 0:NB], start=(n == 0),
                             stop=(n == NK - 1)).then_inc(q("hot_mm"), 1)
                for n in range(8, NT * mo.shared + 1):
                    sh_step(n)

                def turn(b):
                    t.wait_ge(q(f"xg_in{b.par}"), 16 * (b.h + 1))
                    for c in range(HC):
                        ins = t.transpose(bank[b.par][:, c * P:(c + 1) * P], xg[b.par][:, c * P:(c + 1) * P], ident)
                    ins.then_inc(q("xt_mm"), 1)

                def inner(b):
                    t.wait_ge(q(f"w_in{b.slot}"), 32 * (b.q + 1))
                    t.wait_ge(q("xt_rdy"), b.n + 1)
                    for c in range(HC):
                        ins = t.matmul(bank[2 + b.par][:, 0:2 * I], xgT[b.par][:, c, :], wbuf1[b.slot][:, c, 0:2 * I], start=(c == 0),
                                       stop=(c == HC - 1))
                    ins.then_inc(q("h_mm"), 1)

                def zturn(b):
                    t.wait_ge(q("z_rdy"), b.n + 1)
                    for c in range(IC):
                        ins = t.transpose(bank[4][:, c * P:(c + 1) * P], zb[b.par][:, c * P:(c + 1) * P], ident)
                    ins.then_inc(q("zt_mm"), 1)

                def outer(b):
                    t.wait_ge(q("zt_rdy"), b.n + 1)
                    t.wait_ge(q("ob_rdy"), b.n + 1)
                    for c in range(IC):
                        ins = t.matmul(bank[5][:, :], zT[b.par][:, c, :], wbuf2[b.slot][:, c, :], start=(c == 0), stop=(c == IC - 1))
                    ins.then_inc(q("o_mm"), 1)

                def step(b, first=False, last=False):
                    if not last:
                        turn(b.next())
                    if not first:
                        zturn(b.next(-1))
                    inner(b)
                    if not first:
                        outer(b.next(-1))

                turn(Turn(0, 0))
                step(Turn(0, 0), first=True)
                with t.Fori(0, (NB - 3) // 4) as j:
                    for c_ in range(1, 5):
                        step(Turn(j, c_))
                step(Turn(0, NB - 2))
                step(Turn(0, NB - 1), last=True)
                zturn(Turn(0, NB - 1))
                outer(Turn(0, NB - 1))

            def attention():
                def scores(n, par, bpar, b, rp):
                    t.wait_ge(s["qk_rdy"], b + 1)
                    t.matmul(bank[par][:, :], qb[bpar][:, rp * P:(rp + 1) * P], kb[bpar][:, :, :], start=True,
                             stop=True).then_inc(s["as_mm"], 1)

                def turn(n, par):
                    t.wait_ge(s["aexp_rdy"], n + 3)
                    for c in range(4):
                        ins = t.transpose(bank[2 + par][:, c * P:(c + 1) * P], ap_[par][:, c * P:(c + 1) * P], ident)
                    ins.then_inc(s["at_mm"], 1)

                def values(n, par, bpar, b):
                    t.wait_ge(s["aT_rdy"], n + 1)
                    t.wait_ge(s["v_rdy"], b + 1)
                    t.wait_ge(s["ao_used"], 2 * n + 2)
                    for c in range(4):
                        t.matmul(bank[4 + par][32 * c:32 * c + 32, 0:P], vb[bpar][:, 32 * c:32 * c + 32], aT[par][:, c, :],
                                 start=True, stop=True)
                    for c in range(4):
                        ins = t.matmul(bank[4 + par][32 * c:32 * c + 32, P:2 * P], cn("vmask")[:, 0:32], aT[par][:, c, :],
                                       start=True, stop=True)
                    ins.then_inc(s["ao_mm"], 1)

                def step(n, q_, b, bq, scr=True, trn=True, val=True):
                    if scr:
                        scores(n, q_ % 2, bq % 2, b, q_ % 2)
                    if trn:
                        turn(n - 1, (q_ + 1) % 2)
                    if val:
                        values(n - 2, q_ % 2, (bq + 1) % 2, b - 1)

                N = 2 * B
                t.sem_inc(s["ao_mm"], 4)
                t.wait_ge(s["tr_used"], 3 * NT)
                for n in range(2):
                    step(n, n, 0, 0, trn=n >= 1, val=False)
                with t.Fori(0, (N - 4) // 4) as j:
                    for q_ in range(4):
                        step(4 * j + 2 + q_, q_, 2 * j + 1 + q_ // 2, 1 + q_ // 2)
                for n in range(N - 2, N + 2):
                    step(n, n, n // 2, n // 2, scr=n < N, trn=n <= N)
                t.wait_ge(s["ao_used"], 2 * N + 4)
                for i in range(NT):
                    if i >= 2:
                        t.wait_ge(s["att_x"], i - 1)
                    for r in range(R):
                        ins = t.transpose(bank[i % 2][:, r * P:(r + 1) * P], attT[:, r, i * P:(i + 1) * P], ident)
                    ins.then_inc(s["attb_mm"], 1)

            turn_hidden(2)
            mixture(0)
            turn_hidden(3)
            attention()
            turn_hidden(4)
            mixture(1)


def up_layout(w):
    n, rows, _ = w.shape
    return w.reshape(n, rows, HC, P).transpose(0, 3, 2, 1)


def down_layout(w):
    n, _, inner = w.shape
    return w.reshape(n, H, inner // P, P).transpose(0, 3, 2, 1)


def kernel(**inp):
    import concourse.bacc as bacc
    from concourse.bass_utils import run_bass_kernel_spmd

    v = {k: np.asarray(x) for k, x in inp.items()}
    ctxa = v["ctx_1024"]
    arrays = {
        "const": constants()[0],
        "x": v["x"].transpose(1, 0, 2).reshape(NTOK, H),
        "ctxT": ctxa.transpose(2, 1, 0),
        "ctxP": ctxa.reshape(2, 8, T, D).transpose(0, 2, 1, 3).reshape(P, 8, D),
        "lens": v["_lenS2"].reshape(B, 1),
        "lysT": v["L0_xattn_L_ys"].T.reshape(HC, P, 4 * HS).transpose(1, 0, 2),
        "lssT": v["L0_xattn_L_ss"].T,
        "lgsT": v["L0_xattn_L_gs_w"].T,
        "gsb": v["L0_xattn_L_gs_b"].reshape(4, HS).T,
        "wasT": v["L0_xattn_Wa_s"].T,
        "wahT": v["L0_xattn_Wa_h"].T,
        "ba": v["L0_xattn_ba"].reshape(A, 1),
        "convw": v["L0_xattn_conv_w"].reshape(FCH, KW),
        "wafT": v["L0_xattn_Wa_f"].T,
        "va": v["L0_xattn_va"].reshape(A, 1),
        "lgyT": v["L0_xattn_L_gy_w"].T,
        "lsyT": v["L0_xattn_L_sy"].T,
        "gyb": v["L0_xattn_L_gy_b"].reshape(HS, 1),
        "yyT": np.concatenate([v["L0_xattn_L_yy_w"].T, v["L0_xattn_L_yy_b"].reshape(1, H)], 0),
        "gw": np.stack([v["L0_ffn_gate_w"], v["L1_ffn_gate_w"]]).reshape(2, E, HC, P).transpose(3, 0, 2, 1),
        "bias0": np.broadcast_to(v["L0_ffn_bias"].reshape(1, E), (P, E)),
        "amask": v["mask_SxS2_ff0"],
        "ctxD": ctxa.transpose(1, 0, 2),
        "w1_0": up_layout(np.concatenate([v["L0_ffn_Wg"], v["L0_ffn_Wu"]], 1)),
        "w2_0": down_layout(v["L0_ffn_Wd"]),
        "s1_0": up_layout(np.concatenate([v["L0_ffn_Sg"], v["L0_ffn_Su"]], 0)[None]),
        "s2_0": down_layout(v["L0_ffn_Sd"][None]),
        "w1_1": up_layout(v["L1_ffn_w_gate_up"]),
        "w2_1": down_layout(v["L1_ffn_w_down"]),
        "s1_1": up_layout(v["L1_ffn_shared_w_gate_up"].reshape(2, 2, 256, H).transpose(1, 0, 2, 3).reshape(2, 512, H)),
        "s2_1": down_layout(v["L1_ffn_shared_w_down"].reshape(H, 2, 256).transpose(1, 0, 2)),
        "gg": np.broadcast_to(np.concatenate([v["g_xattn"], v["g_ffn"]]), (P, 4)),
    }
    nc = bacc.Bacc("TRN2", target_bir_lowering=False, num_devices=1)
    arrays = {k: np.ascontiguousarray(x) for k, x in arrays.items()}
    aps = {k: nc.dram_tensor("in_" + k, list(x.shape), mybir.dt.from_np(x.dtype), kind="ExternalInput").ap()
           for k, x in arrays.items()}
    out = nc.dram_tensor("out_0", [NTOK, H], F32, kind="ExternalOutput").ap()
    build(nc, aps, out)
    r = run_bass_kernel_spmd(nc, [{"in_" + k: x for k, x in arrays.items()}], core_ids=[0])
    return r.results[0]["out_0"].reshape(L, B, H).transpose(1, 0, 2)
```
